# Optimizing a Trainium2 kernel written in Bass

```python
import numpy as np
import jax
import jax.numpy as jnp

def _softmax(x, axis=-1):
    return jax.nn.softmax(x, axis=axis)

def _gelu(x):
    return jax.nn.gelu(x, approximate=True)

def _silu(x):
    return jax.nn.silu(x)

def _sigmoid(x):
    return jax.nn.sigmoid(x)

def _layernorm(x, axis=-1, eps=1e-05):
    m = jnp.mean(x, axis=axis, keepdims=True)
    v = jnp.var(x, axis=axis, keepdims=True)
    return (x - m) / jnp.sqrt(v + eps)

def _scatter_add(tgt, idx, src, axis=0):
    return tgt.at[idx].add(src)

def _segment_sum(src, seg, n):
    return jax.ops.segment_sum(src, seg, n)
kernel_name = 'mk_decoder_postln_d1_seqx_r4_df3adf'

def setup_inputs(seed: int=0):
    np.random.seed(seed)
    _w = jnp.asarray

    def _rec_inputs():
        import jax
        import jax.numpy as jnp
        _rk = jax.random.key(seed)
        x = -1.394e-06 + 0.9999 * jax.random.normal(jax.random.fold_in(_rk, 1), (2, 1024, 256), jnp.float32)
        _lenS = 1024 - jax.random.randint(jax.random.fold_in(_rk, 7), (2,), 0, max(1, 1024 // 4) + 1, jnp.int32)
        _lenS2 = 77 - jax.random.randint(jax.random.fold_in(_rk, 8), (2,), 0, max(1, 77 // 4) + 1, jnp.int32)
        _ctx_1024P = jax.random.normal(jax.random.fold_in(_rk, 11), (2, 16, 256), jnp.float32)
        _ctx_1024c = jax.random.dirichlet(jax.random.fold_in(_rk, 511), 0.3 * jnp.ones((16,), jnp.float32), (2, 77))
        _ctx_1024t = jnp.einsum('bsk,bkd->bsd', _ctx_1024c, _ctx_1024P)
        _ctx_1024t = _ctx_1024t * jax.lax.rsqrt(jnp.mean(jnp.square(_ctx_1024t)) + 1e-12) * 0.953939
        ctx_1024 = -0.000292821 + 1.00034 * (_ctx_1024t + 0.3 * jax.random.normal(jax.random.fold_in(_rk, 611), (2, 77, 256), jnp.float32))
        return (x, ctx_1024)
    x, ctx_1024 = _rec_inputs()

    def _L0_attn_setup():
        import math
        import jax, jax.numpy as jnp
        import numpy as np
        B, T, D_MODEL = (4, 512, 256)
        H, HD = (16, 64)
        NF = 128
        EPS = 1e-06
        INV_SQRT_NF = 1.0 / math.sqrt(NF)

        def make_orf(key, head_dim, n_features, dtype=jnp.float32):
            n_blocks = math.ceil(n_features / head_dim)
            keys = jax.random.split(key, n_blocks)
            blocks = []
            for k in keys:
                g = jax.random.normal(k, (head_dim, head_dim), dtype)
                qm, _ = jnp.linalg.qr(g)
                blocks.append(qm)
            W = jnp.concatenate(blocks, axis=1)[:, :n_features]
            return W * jnp.asarray(math.sqrt(head_dim), dtype)

        def _favor_plus(x, W):
            sq = 0.5 * jnp.sum(x * x, axis=-1, keepdims=True)
            return jnp.exp(x @ W - sq) * INV_SQRT_NF

        def _causal_linear_attention(qp, kp, v):
            Bb, Hh = (qp.shape[0], qp.shape[1])

            def step(carry, qkv):
                S, z = carry
                q_t, k_t, v_t = qkv
                S = S + jnp.einsum('bhd,bhe->bhde', k_t, v_t)
                z = z + k_t
                num = jnp.einsum('bhd,bhde->bhe', q_t, S)
                den = jnp.einsum('bhd,bhd->bh', q_t, z) + EPS
                return ((S, z), num / den[..., None])
            S0 = jnp.zeros((Bb, Hh, NF, HD), qp.dtype)
            z0 = jnp.zeros((Bb, Hh, NF), qp.dtype)
            xs = (jnp.moveaxis(qp, 2, 0), jnp.moveaxis(kp, 2, 0), jnp.moveaxis(v, 2, 0))
            _, ys = jax.lax.scan(step, (S0, z0), xs)
            return jnp.moveaxis(ys, 0, 2)
        key = jax.random.key(seed)
        k0, k1, k2, k3, k4, k5 = jax.random.split(key, 6)
        s = 1.0 / math.sqrt(D_MODEL)
        x = jax.random.normal(k0, (B, T, D_MODEL), jnp.float32)
        Wq = jax.random.uniform(k1, (D_MODEL, H * HD), jnp.float32, -s, s)
        Wk = jax.random.uniform(k2, (D_MODEL, H * HD), jnp.float32, -s, s)
        Wv = jax.random.uniform(k3, (D_MODEL, H * HD), jnp.float32, -s, s)
        Wo = jax.random.uniform(k4, (H * HD, D_MODEL), jnp.float32, -s, s)
        W_feat = make_orf(k5, HD, NF)
        return {'x': x, 'Wq': Wq, 'Wk': Wk, 'Wv': Wv, 'Wo': Wo, 'W_feat': W_feat}
    _L0_attn_all = _L0_attn_setup()
    _L0_attn_in = {k: v for k, v in _L0_attn_all.items() if k in ('Wq', 'Wk', 'Wv', 'Wo', 'W_feat')}
    del _L0_attn_all

    def _L0_xattn_setup():
        import jax, jax.numpy as jnp
        import numpy as np
        B, N, T = (2, 512, 512)
        ENC, DEC, HID = (256, 256, 256)
        HEADS = 16
        DH = HID // HEADS
        HALF = DH // 2
        LAMBDA_INIT = 0.8
        key = jax.random.key(seed)
        ks = jax.random.split(key, 9)
        s = 0.02
        return {'encoder_feature': jax.random.normal(ks[0], (B, N, ENC), jnp.float32), 'decoder_feature': jax.random.normal(ks[1], (B, T, DEC), jnp.float32), 'Wq': jax.random.normal(ks[2], (HID, DEC), jnp.float32) * s, 'Wk': jax.random.normal(ks[3], (HID, ENC), jnp.float32) * s, 'Wv': jax.random.normal(ks[4], (HID, ENC), jnp.float32) * s, 'lambda_q1': jax.random.normal(ks[5], (HALF,), jnp.float32) * 0.1, 'lambda_q2': jax.random.normal(ks[6], (HALF,), jnp.float32) * 0.1, 'lambda_k1': jax.random.normal(ks[7], (HALF,), jnp.float32) * 0.1, 'lambda_k2': jax.random.normal(ks[8], (HALF,), jnp.float32) * 0.1}
    _L0_xattn_all = _L0_xattn_setup()
    _L0_xattn_in = {k: v for k, v in _L0_xattn_all.items() if k in ('Wq', 'Wk', 'Wv', 'lambda_q1', 'lambda_q2', 'lambda_k1', 'lambda_k2')}
    del _L0_xattn_all

    def _L0_ffn_setup():
        import jax, jax.numpy as jnp
        import numpy as np
        HIDDEN = 256
        INTER = 128
        N_EXPERTS = 16
        N_GROUP = 4
        TOPK_GROUP = 2
        TOP_K = 4
        SCALING = 2.5

        def _gate(x_flat, gate_w, e_bias):
            logits = x_flat @ gate_w.T
            scores = jax.nn.sigmoid(logits)
            scores_for_choice = scores + e_bias[None, :]
            T = x_flat.shape[0]
            per_group = N_EXPERTS // N_GROUP
            grouped = scores_for_choice.reshape(T, N_GROUP, per_group)
            top2, _ = jax.lax.top_k(grouped, 2)
            group_scores = top2.sum(-1)
            _, group_idx = jax.lax.top_k(group_scores, TOPK_GROUP)
            group_mask = jax.nn.one_hot(group_idx, N_GROUP, dtype=jnp.float32).sum(1) > 0
            score_mask = jnp.repeat(group_mask, per_group, axis=-1)
            tmp_scores = jnp.where(score_mask, scores_for_choice, 0.0)
            _, topk_idx = jax.lax.top_k(tmp_scores, TOP_K)
            topk_weight = jnp.take_along_axis(scores, topk_idx, axis=1)
            topk_weight = topk_weight / (topk_weight.sum(-1, keepdims=True) + 1e-20)
            topk_weight = topk_weight * SCALING
            return (topk_idx, topk_weight)
        key = jax.random.key(seed)
        ks = jax.random.split(key, 8)
        B, S = (2, 512)
        hidden_states = jax.random.normal(ks[0], (B, S, HIDDEN), dtype=jnp.float32)
        gate_w = jax.random.normal(ks[1], (N_EXPERTS, HIDDEN), dtype=jnp.float32) * 0.02
        e_bias = jnp.zeros((N_EXPERTS,), dtype=jnp.float32)
        gate_proj = jax.random.normal(ks[2], (N_EXPERTS, INTER, HIDDEN), dtype=jnp.float32) * 0.02
        up_proj = jax.random.normal(ks[3], (N_EXPERTS, INTER, HIDDEN), dtype=jnp.float32) * 0.02
        down_proj = jax.random.normal(ks[4], (N_EXPERTS, HIDDEN, INTER), dtype=jnp.float32) * 0.02
        shared_gate_w = jax.random.normal(ks[5], (INTER, HIDDEN), dtype=jnp.float32) * 0.02
        shared_up_w = jax.random.normal(ks[6], (INTER, HIDDEN), dtype=jnp.float32) * 0.02
        shared_down_w = jax.random.normal(ks[7], (HIDDEN, INTER), dtype=jnp.float32) * 0.02
        return {'hidden_states': hidden_states, 'gate_w': gate_w, 'e_bias': e_bias, 'gate_proj': gate_proj, 'up_proj': up_proj, 'down_proj': down_proj, 'shared_gate_w': shared_gate_w, 'shared_up_w': shared_up_w, 'shared_down_w': shared_down_w}
    _L0_ffn_all = _L0_ffn_setup()
    _L0_ffn_in = {k: v for k, v in _L0_ffn_all.items() if k in ('gate_w', 'e_bias', 'gate_proj', 'up_proj', 'down_proj', 'shared_gate_w', 'shared_up_w', 'shared_down_w')}
    del _L0_ffn_all
    return {'x': x, 'ctx_1024': ctx_1024, 'L0_attn_Wq': _L0_attn_in['Wq'], 'L0_attn_Wk': _L0_attn_in['Wk'], 'L0_attn_Wv': _L0_attn_in['Wv'], 'L0_attn_Wo': _L0_attn_in['Wo'], 'L0_attn_W_feat': _L0_attn_in['W_feat'], 'L0_xattn_Wq': _L0_xattn_in['Wq'], 'L0_xattn_Wk': _L0_xattn_in['Wk'], 'L0_xattn_Wv': _L0_xattn_in['Wv'], 'L0_xattn_lambda_q1': _L0_xattn_in['lambda_q1'], 'L0_xattn_lambda_q2': _L0_xattn_in['lambda_q2'], 'L0_xattn_lambda_k1': _L0_xattn_in['lambda_k1'], 'L0_xattn_lambda_k2': _L0_xattn_in['lambda_k2'], 'L0_ffn_gate_w': _L0_ffn_in['gate_w'], 'L0_ffn_e_bias': _L0_ffn_in['e_bias'], 'L0_ffn_gate_proj': _L0_ffn_in['gate_proj'], 'L0_ffn_up_proj': _L0_ffn_in['up_proj'], 'L0_ffn_down_proj': _L0_ffn_in['down_proj'], 'L0_ffn_shared_gate_w': _L0_ffn_in['shared_gate_w'], 'L0_ffn_shared_up_w': _L0_ffn_in['shared_up_w'], 'L0_ffn_shared_down_w': _L0_ffn_in['shared_down_w']}

def reference(x, ctx_1024, L0_attn_Wq, L0_attn_Wk, L0_attn_Wv, L0_attn_Wo, L0_attn_W_feat, L0_xattn_Wq, L0_xattn_Wk, L0_xattn_Wv, L0_xattn_lambda_q1, L0_xattn_lambda_q2, L0_xattn_lambda_k1, L0_xattn_lambda_k2, L0_ffn_gate_w, L0_ffn_e_bias, L0_ffn_gate_proj, L0_ffn_up_proj, L0_ffn_down_proj, L0_ffn_shared_gate_w, L0_ffn_shared_up_w, L0_ffn_shared_down_w):
    import jax
    import jax.numpy as jnp

    def _L0_attn_ref(x, Wq, Wk, Wv, Wo, W_feat):
        import math
        import jax, jax.numpy as jnp
        import numpy as np
        B, T, D_MODEL = (4, 512, 256)
        H, HD = (16, 64)
        NF = 128
        EPS = 1e-06
        INV_SQRT_NF = 1.0 / math.sqrt(NF)

        def make_orf(key, head_dim, n_features, dtype=jnp.float32):
            n_blocks = math.ceil(n_features / head_dim)
            keys = jax.random.split(key, n_blocks)
            blocks = []
            for k in keys:
                g = jax.random.normal(k, (head_dim, head_dim), dtype)
                qm, _ = jnp.linalg.qr(g)
                blocks.append(qm)
            W = jnp.concatenate(blocks, axis=1)[:, :n_features]
            return W * jnp.asarray(math.sqrt(head_dim), dtype)

        def _favor_plus(x, W):
            sq = 0.5 * jnp.sum(x * x, axis=-1, keepdims=True)
            return jnp.exp(x @ W - sq) * INV_SQRT_NF

        def _causal_linear_attention(qp, kp, v):
            Bb, Hh = (qp.shape[0], qp.shape[1])

            def step(carry, qkv):
                S, z = carry
                q_t, k_t, v_t = qkv
                S = S + jnp.einsum('bhd,bhe->bhde', k_t, v_t)
                z = z + k_t
                num = jnp.einsum('bhd,bhde->bhe', q_t, S)
                den = jnp.einsum('bhd,bhd->bh', q_t, z) + EPS
                return ((S, z), num / den[..., None])
            S0 = jnp.zeros((Bb, Hh, NF, HD), qp.dtype)
            z0 = jnp.zeros((Bb, Hh, NF), qp.dtype)
            xs = (jnp.moveaxis(qp, 2, 0), jnp.moveaxis(kp, 2, 0), jnp.moveaxis(v, 2, 0))
            _, ys = jax.lax.scan(step, (S0, z0), xs)
            return jnp.moveaxis(ys, 0, 2)
        Bb, Tt, _ = x.shape

        def heads(W):
            return (x @ W).reshape(Bb, Tt, H, HD).transpose(0, 2, 1, 3)
        q, k, v = (heads(Wq), heads(Wk), heads(Wv))
        qp = _favor_plus(q, W_feat)
        kp = _favor_plus(k, W_feat)
        y = _causal_linear_attention(qp, kp, v)
        y = y.transpose(0, 2, 1, 3).reshape(Bb, Tt, H * HD)
        return y @ Wo

    def _L0_xattn_ref(encoder_feature, decoder_feature, Wq, Wk, Wv, lambda_q1, lambda_q2, lambda_k1, lambda_k2):
        import jax, jax.numpy as jnp
        import numpy as np
        B, N, T = (2, 512, 512)
        ENC, DEC, HID = (256, 256, 256)
        HEADS = 16
        DH = HID // HEADS
        HALF = DH // 2
        LAMBDA_INIT = 0.8
        b, n, _ = encoder_feature.shape
        _, t, _ = decoder_feature.shape
        hid = Wq.shape[0]
        dh = hid // HEADS
        half = dh // 2
        q = decoder_feature @ Wq.T
        k = encoder_feature @ Wk.T
        v = encoder_feature @ Wv.T
        q = q.reshape(b, t, 2 * HEADS, half).transpose(0, 2, 1, 3)
        k = k.reshape(b, n, 2 * HEADS, half).transpose(0, 2, 1, 3)
        v = v.reshape(b, n, HEADS, dh).transpose(0, 2, 1, 3)
        lam = jnp.exp(jnp.sum(lambda_q1 * lambda_k1)) - jnp.exp(jnp.sum(lambda_q2 * lambda_k2)) + LAMBDA_INIT
        scale = 1.0 / jnp.sqrt(jnp.float32(half))
        att = jax.nn.softmax(jnp.einsum('bhtd,bhnd->bhtn', q, k) * scale, axis=-1)
        att = att.reshape(b, HEADS, 2, t, n)
        att = att[:, :, 0] - lam * att[:, :, 1]
        out = jnp.einsum('bhtn,bhnd->bhtd', att, v)
        return out.transpose(0, 2, 1, 3).reshape(b, t, hid)

    def _L0_ffn_ref(hidden_states, gate_w, e_bias, gate_proj, up_proj, down_proj, shared_gate_w, shared_up_w, shared_down_w):
        import jax, jax.numpy as jnp
        import numpy as np
        HIDDEN = 256
        INTER = 128
        N_EXPERTS = 16
        N_GROUP = 4
        TOPK_GROUP = 2
        TOP_K = 4
        SCALING = 2.5

        def _gate(x_flat, gate_w, e_bias):
            logits = x_flat @ gate_w.T
            scores = jax.nn.sigmoid(logits)
            scores_for_choice = scores + e_bias[None, :]
            T = x_flat.shape[0]
            per_group = N_EXPERTS // N_GROUP
            grouped = scores_for_choice.reshape(T, N_GROUP, per_group)
            top2, _ = jax.lax.top_k(grouped, 2)
            group_scores = top2.sum(-1)
            _, group_idx = jax.lax.top_k(group_scores, TOPK_GROUP)
            group_mask = jax.nn.one_hot(group_idx, N_GROUP, dtype=jnp.float32).sum(1) > 0
            score_mask = jnp.repeat(group_mask, per_group, axis=-1)
            tmp_scores = jnp.where(score_mask, scores_for_choice, 0.0)
            _, topk_idx = jax.lax.top_k(tmp_scores, TOP_K)
            topk_weight = jnp.take_along_axis(scores, topk_idx, axis=1)
            topk_weight = topk_weight / (topk_weight.sum(-1, keepdims=True) + 1e-20)
            topk_weight = topk_weight * SCALING
            return (topk_idx, topk_weight)
        B, S, H = hidden_states.shape
        x = hidden_states.reshape(-1, H)
        T = x.shape[0]
        topk_idx, topk_weight = _gate(x, gate_w, e_bias)
        g = jnp.einsum('th,eih->eti', x, gate_proj)
        u = jnp.einsum('th,eih->eti', x, up_proj)
        inter = jax.nn.silu(g) * u
        expert_out = jnp.einsum('eti,ehi->eth', inter, down_proj)
        sel = expert_out[topk_idx, jnp.arange(T)[:, None]]
        y = jnp.einsum('tkh,tk->th', sel, topk_weight)
        y = y.reshape(B, S, H)
        sg = hidden_states @ shared_gate_w.T
        su = hidden_states @ shared_up_w.T
        shared_out = jax.nn.silu(sg) * su @ shared_down_w.T
        return y + shared_out
    x = _layernorm(x + _L0_attn_ref(x, L0_attn_Wq, L0_attn_Wk, L0_attn_Wv, L0_attn_Wo, L0_attn_W_feat), axis=-1)
    x = _layernorm(x + _L0_xattn_ref(ctx_1024, x, L0_xattn_Wq, L0_xattn_Wk, L0_xattn_Wv, L0_xattn_lambda_q1, L0_xattn_lambda_q2, L0_xattn_lambda_k1, L0_xattn_lambda_k2), axis=-1)
    x = _layernorm(x + _L0_ffn_ref(x, L0_ffn_gate_w, L0_ffn_e_bias, L0_ffn_gate_proj, L0_ffn_up_proj, L0_ffn_down_proj, L0_ffn_shared_gate_w, L0_ffn_shared_up_w, L0_ffn_shared_down_w), axis=-1)
    return x

_drawn_inputs = setup_inputs


def setup_inputs(seed=0):
    import zlib

    import numpy as np

    out = dict(_drawn_inputs(seed))
    spreads = {'L0_ffn_e_bias': (0.0, 0.481)}
    factors = {'L0_xattn_Wq': 6.804,
     'L0_xattn_Wk': 6.897,
     'L0_xattn_lambda_q1': 8.0,
     'L0_xattn_lambda_q2': 8.0,
     'L0_xattn_lambda_k1': 8.0,
     'L0_xattn_lambda_k2': 6.372,
     'L0_ffn_gate_w': 7.749,
     'L0_ffn_gate_proj': 3.796,
     'L0_ffn_up_proj': 3.752,
     'L0_ffn_down_proj': 3.767,
     'L0_ffn_shared_gate_w': 4.849,
     'L0_ffn_shared_up_w': 4.761,
     'L0_ffn_shared_down_w': 4.754}
    for name, (base, spread) in spreads.items():
        noise = np.random.default_rng([zlib.crc32(name.encode()), seed]).standard_normal(out[name].shape)
        drawn = base * np.exp(spread * noise) if base else spread * noise
        out[name] = jnp.asarray(drawn.astype(out[name].dtype))
    for name, factor in factors.items():
        out[name] = (out[name] * factor).astype(out[name].dtype)
    return out
```

```python
from contextlib import ExitStack

import numpy as np

import concourse.bass as bass
from concourse import mybir

ALU = mybir.AluOpType
ACT = mybir.ActivationFunctionType
AX = mybir.AxisListType
F32 = mybir.dt.float32
F16 = mybir.dt.float16
I32 = mybir.dt.int32

P = 128
B, S, D = 2, 1024, 256
CTX = 77
H, HD, NF = 16, 64, 128
PAIRS = H // 2
XHALVES, XD = 32, 8
XV = 16
NE, INTER, NGROUP, PER_GROUP, TOPK_GROUP, TOPK = 16, 128, 4, 4, 2, 4
SCALING = 2.5
LN_EPS = 1e-5
EPS = 1e-6 * NF
LAMBDA_INIT = 0.8
W_SCALE = 64.0

TB = 512
NT = TB // P
NBLK = B * S // TB
BLK_PER_BATCH = S // TB
KD = D // P
V1 = HD + 1
GH = 4
NG = XHALVES // GH
GROUPS = NT * NG
GN = GH * CTX
GC = 3
GV = GH * (XV + 1)
EXPERTS = NE + 1
FW = 2 * D + D
ROUTE_STEPS = 28
ROOT_STEPS = 12
LAST = 20


def steps(s, attn, cross):
    jobs = []

    def add(on, kind, n, count):
        if on and 0 <= n < count:
            jobs.append((kind, n))

    if s == 0:
        add(attn, "project", 0, H)
        add(attn, "project", 1, H)
    add(attn, "project", s + 2, H)
    add(attn, "turn keys", s - 1, H)
    add(attn, "q features", s, H)
    add(cross, "scores", 2 * s, GROUPS)
    add(attn, "state", s - 2, H)
    add(attn, "attend", s - 1, H)
    add(cross, "turn probs", 2 * s - 2, GROUPS)
    add(attn, "k features", s, H)
    add(cross, "exp", 2 * s, GROUPS)
    add(cross, "scores", 2 * s + 1, GROUPS)
    add(attn, "output", s - 3, H)
    add(cross, "turn probs", 2 * s - 1, GROUPS)
    add(cross, "values", 2 * s - 4, GROUPS)
    add(cross, "values", 2 * s - 3, GROUPS)
    add(cross, "exp", 2 * s + 1, GROUPS)
    if s % 2 == 1:
        add(attn, "turn output", (s - 5) // 2, PAIRS)
    if s % 4 == 2:
        add(cross, "norm", (s - 6) // 4, NT)
    if s % 4 == 3:
        add(cross, "turn cross", (s - 7) // 4, NT)
    return jobs


class Signal:

    def __init__(self, sem, per, unit):
        self.sem, self.per, self.unit = sem, per, unit

    def __call__(self, block, n):
        return self.sem, (block * self.per + n) * self.unit


def decoder_layer(nc, x, xT, ctxT, wq, wk, wv, wo, wfeat, xwqT, xwkT, xwvT, lam_q1, lam_q2, lam_k1,
                  lam_k2, gate_wT, e_bias, ffn_w, out):
    with ExitStack() as stack:
        def sb(name, shape, dt=F32):
            return stack.enter_context(nc.sbuf_tensor(name, shape, dt))

        def signal(name, per=1, unit=1):
            return Signal(stack.enter_context(nc.semaphore(name)), per, unit)

        w_q = sb("w_q", [P, 2, KD, H * HD], F16)
        w_k = sb("w_k", [P, 2, KD, H * HD], F16)
        w_v = sb("w_v", [P, 2, KD, H * HD], F16)
        w_o = sb("w_o", [P, 2, PAIRS, D], F16)
        w_xq = sb("w_xq", [P, 2, KD, D], F16)
        w_gate = sb("w_gate", [P, 2, KD, NE], F16)
        w_feat = sb("w_feat", [P, 2, 2, NF], F16)
        neg_half = sb("neg_half", [P, 2, NF], F16)
        ident = sb("ident", [P, P])
        causal = sb("causal", [P, P])
        before_e = sb("before_e", [P, NE, NE], F16)
        before_g = sb("before_g", [P, NGROUP, NGROUP], F16)
        bias = sb("bias", [P, NE])
        lam_in = sb("lam_in", [P, 4, XD])
        lam_prod = sb("lam_prod", [P, 2, XD])
        lam_sum = sb("lam_sum", [P, 2])
        lam_exp = sb("lam_exp", [P, 2])
        coef = sb("coef", [P, 2 * XV // 2, 1])
        x_stage = sb("x_stage", [P, KD, TB])
        x_split = sb("x_split", [P, 2, KD, TB], F16)
        resid = sb("resid", [P, NT, D])
        out_buf = sb("out_buf", [P, NT, D])
        turned = sb("turned", [P, 2, KD, TB], F16)
        qk = sb("qk", [P, 2, 2, 4, TB], F16)
        square = sb("square", [P, 2, TB])
        v1 = sb("v1", [P, NT, H, V1])
        qf = sb("qf", [P, 4, TB])
        kf = sb("kf", [P, 2, TB])
        kt = sb("kt", [P, 2, NT, NF])
        att = sb("att", [P, 3, NT, P])
        state = sb("state", [P, H, V1])
        keep = sb("keep", [P, 1])
        run = sb("run", [P, 2, NT, V1])
        den = sb("den", [P, 2, NT, 1])
        rec = sb("rec", [P, 2, NT, 1])
        y = sb("y", [P, 2, NT, P])
        yT = sb("yT", [P, 2, PAIRS, TB], F16)
        xq_hl = sb("xq_hl", [P, 2, KD, TB], F16)
        xq = sb("xq", [P, NG, TB], F16)
        xk = sb("xk", [P, NG, GN], F16)
        xv = sb("xv", [P, NG, GC, GV])
        xmax = sb("xmax", [P, 4, GH, 1])
        prob = sb("prob", [P, 4, GC * P])
        probT = sb("probT", [P, 4, GC, P])
        xrec = sb("xrec", [P, 2, XHALVES // 2, 1])
        xrec2 = sb("xrec2", [P, 2, XHALVES // 2, 1])
        xterm = sb("xterm", [P, 2, XHALVES // 4, 2, XV])
        xsum = sb("xsum", [P, 2, XHALVES // 4, XV])
        st = sb("st", [P, NT, 6])
        mv = sb("mv", [P, NT, 2])
        rstd = sb("rstd", [P, NT, 1])
        root_v = sb("root_v", [P, NT, 1])
        root_a = sb("root_a", [P, NT, 1])
        ffn_mem = sb("ffn_mem", [P, 3072])
        hT = sb("hT", [P, 3, 2, TB], F16)
        ge = sb("ge", [P, NT * NE])
        gd = sb("gd", [P, NT * NE])
        score = sb("score", [P, NT, NE])
        choice = sb("choice", [P, NT, NE])
        g_max = sb("g_max", [P, NT * NGROUP, 2])
        g_min = sb("g_min", [P, NT * NGROUP, 2])
        g_a = sb("g_a", [P, NT * NGROUP])
        g_b = sb("g_b", [P, NT * NGROUP])
        g_c = sb("g_c", [P, NT * NGROUP])
        g_d = sb("g_d", [P, NT * NGROUP])
        g_sum = sb("g_sum", [P, NT, NGROUP])
        g_gt = sb("g_gt", [P, NT, NGROUP, NGROUP], F16)
        g_eq = sb("g_eq", [P, NT, NGROUP, NGROUP], F16)
        g_rank = sb("g_rank", [P, NT * NGROUP])
        g_in = sb("g_in", [P, NT * NGROUP, 1])
        masked = sb("masked", [P, NT, NE])
        e_gt = sb("e_gt", [P, NT, NE * NE], F16)
        e_eq = sb("e_eq", [P, NT, NE * NE], F16)
        e_rank = sb("e_rank", [P, NT * NE])
        e_in = sb("e_in", [P, NT * NE])
        chosen = sb("chosen", [P, NT, NE])
        w_sum = sb("w_sum", [P, NT])
        w_rec = sb("w_rec", [P, NT])
        w_rec2 = sb("w_rec2", [P, NT, 1])
        weight = sb("weight", [P, NT, NE])

        gu_w = ffn_mem[:, 0:1024].bitcast(F16).rearrange("p (r a c) -> p r a c", r=2, a=2)
        down_w = ffn_mem[:, 1024:2048].bitcast(F16).rearrange("p (r a c) -> p r a c", r=4, a=2)
        hid = ffn_mem[:, 2048:3072].rearrange("p (r t) -> p r t", r=2)
        fs_in = ffn_mem[:, 0:1536].rearrange("p (r c) -> p r c", r=2)
        fs_out = ffn_mem[:, 1536:3072].bitcast(F16).rearrange("p (r a c) -> p r a c", r=2, a=2)
        w_stage = xq[:, :, :].rearrange("p g t -> p (g t)").bitcast(F32).rearrange("p (r c) -> p r c", r=2)
        ctx_mem = probT[:, :, :, :].rearrange("p r c t -> p (r c t)")
        xwk_sb = ctx_mem[:, 0:512].rearrange("p (k n) -> p k n", k=KD)
        xwv_sb = ctx_mem[:, 512:1024].rearrange("p (k n) -> p k n", k=KD)
        ctx_sb = ctx_mem[:, 1024:1024 + KD * B * CTX].rearrange("p (k n) -> p k n", k=KD)
        prob_mem = prob[:, :, :].rearrange("p r t -> p (r t)")
        kb_hl = prob_mem[:, 0:4 * GN].bitcast(F16).rearrange("p (n a c) -> p n a c", n=2 * B, a=2)
        out_mem = out_buf[:, :, :].rearrange("p t d -> p (t d)")
        v_ext = out_mem[:, 0:B * XV * (XV + 1)].rearrange("p (b h d) -> p b h d", b=B, h=XV)
        kb_full = out_mem[:, 600:600 + GN].rearrange("p (j n) -> p j n", j=GH)
        own_half = sb("own_half", [P, P // XD])
        own_row = sb("own_row", [P, GH, 1])

        def psum(name):
            return stack.enter_context(nc.psum_tensor(name, [P, 512], F32))

        ps_a = [psum("ps_a0"), psum("ps_a1")]
        ps_qf, ps_kf = psum("ps_qf"), psum("ps_kf")
        ps_att = psum("ps_att")
        ps_turn = psum("ps_turn")
        ps_so = psum("ps_so")
        ps_xo = psum("ps_xo")

        ffn_scr = nc.dram_tensor("ffn_split", [EXPERTS, P, 2, FW], F16, kind="Internal").ap()
        xk_scr = nc.dram_tensor("xk_blocks", [B, 96, NG, GN], F16, kind="Internal").ap()
        xv_scr = nc.dram_tensor("xv_blocks", [B, P, NG, GC, GV], F32, kind="Internal").ap()

        consts = signal("consts", 4)
        own_ready = signal("own_ready"); v_ones = signal("v_ones"); zeros_v = signal("zeros_v")
        c_loaded = signal("c_loaded", 1, 16)
        ctx_loaded = signal("ctx_loaded", 1, 16)
        w_loaded = [signal("w_loaded0", 1, 16), signal("w_loaded1", 1, 16)]
        w_high = signal("w_high"); w_low = signal("w_low")
        xkv_done = signal("xkv_done"); kb_copied = signal("kb_copied"); kb_masked = signal("kb_masked")
        kb_high = signal("kb_high"); kb_low = signal("kb_low"); v_copied = signal("v_copied")
        lam_step = signal("lam_step"); lam_exped = signal("lam_exped"); coef_ready = signal("coef_ready")
        zero_stored = signal("zero_stored", 1, 16); ctx_stored = signal("ctx_stored", 1, 16)
        fs_loaded = [signal("fs_loaded0", 1, 16), signal("fs_loaded1", 1, 16)]
        fs_high = signal("fs_high"); fs_low = signal("fs_low")
        fs_stored = [signal("fs_stored0", 1, 16), signal("fs_stored1", 1, 16)]
        v_done = signal("v_done", 2 * NT); p_done = signal("p_done", H)
        turned_k = signal("turned_k", H); qf_done = signal("qf_done", H); kf_done = signal("kf_done", H)
        st_done = signal("st_done", H); att_done = signal("att_done", H); o_done = signal("o_done", H)
        yt_done = signal("yt_done", PAIRS)
        xs_loaded = signal("xs_loaded", 1, 16)
        x_high = signal("x_high"); x_low = signal("x_low")
        v_kept = signal("v_kept", 2 * NT)
        p_high = signal("p_high", H); p_low = signal("p_low", H); p_sq = signal("p_sq", H)
        p_sqh = signal("p_sqh", H); p_sql = signal("p_sql", H)
        qf_exp = signal("qf_exp", H); kf_exp = signal("kf_exp", H); kt_kept = signal("kt_kept", H)
        att_kept = signal("att_kept", H); run_step = signal("run_step", 4 * H); run_ready = signal("run_ready", H)
        o_den = signal("o_den", H); o_rec = signal("o_rec", H); o_kept = signal("o_kept", H)
        yt_high = signal("yt_high", PAIRS); yt_low = signal("yt_low", PAIRS)
        keep_set = signal("keep_set")
        xq_high = signal("xq_high", KD); xq_low = signal("xq_low", KD); xq_done = signal("xq_done", KD)
        xq_placed = signal("xq_placed", 12, 16); xkv_placed = signal("xkv_placed", 2, 16)
        sc_done = signal("sc_done", GROUPS); sc_max = signal("sc_max", GROUPS); sc_sub = signal("sc_sub", GROUPS)
        pr_exp = signal("pr_exp", GROUPS); pr_turned = signal("pr_turned", GROUPS)
        pr_kept_a = signal("pr_kept_a", GROUPS // 2); pr_kept_v = signal("pr_kept_v", GROUPS // 2)
        xo_done = signal("xo_done", 2 * NT); xo_rec = signal("xo_rec", 2 * NT); xo_coef = signal("xo_coef", 2 * NT)
        xo_kept = signal("xo_kept", 2 * NT); xo_sum = signal("xo_sum", 2 * NT); xo_added = signal("xo_added", 2 * NT)
        ln = [[signal(f"ln{i}_stats", NT), signal(f"ln{i}_mv", NT), signal(f"ln{i}_root", ROOT_STEPS * calls),
               signal(f"ln{i}_out", NT)] for i, calls in enumerate((1, NT, 1))]
        x2_turned = signal("x2_turned", NT); x2_high = signal("x2_high", NT); x2_low = signal("x2_low", NT)
        gl_done = signal("gl_done"); gl_exp = signal("gl_exp"); route = signal("route", ROUTE_STEPS)
        gw_loaded = [signal("gw_loaded0", 9, 16), signal("gw_loaded1", 8, 16)]
        dw_loaded = [signal("dw_loaded0", 5, 16)] + [signal(f"dw_loaded{r}", 4, 16) for r in (1, 2, 3)]
        g_done = signal("g_done", EXPERTS); u_done = signal("u_done", EXPERTS)
        silu = signal("silu", EXPERTS); hid_ready = signal("hid_ready", EXPERTS)
        h_high = signal("h_high", EXPERTS); h_low = signal("h_low", EXPERTS)
        down_done = signal("down_done", 2 * EXPERTS); summed = signal("summed", 2 * EXPERTS)
        out_stored = signal("out_stored", 1, 16)
        xin_loaded = signal("xin_loaded", 1, 16)
        wo_done = signal("wo_done", NT); x1_added = signal("x1_added", NT)
        x1_turned = signal("x1_turned", NT); x1_high = signal("x1_high", NT); x1_low = signal("x1_low", NT)

        def flat(t):
            return t.rearrange("p k n -> p (k n)") if len(t.shape) == 3 else t

        pieces = [(wv[0:P, :], w_v[:, 0, 0, :], w_v[:, 1, 0, :]), (wv[P:D, :], w_v[:, 0, 1, :], w_v[:, 1, 1, :]),
                  (wq[0:P, :], w_q[:, 0, 0, :], w_q[:, 1, 0, :]), (wq[P:D, :], w_q[:, 0, 1, :], w_q[:, 1, 1, :]),
                  (wk[0:P, :], w_k[:, 0, 0, :], w_k[:, 1, 0, :]), (wk[P:D, :], w_k[:, 0, 1, :], w_k[:, 1, 1, :])]
        for half in range(2):
            rows = wo.rearrange("(c p) n -> p c n", p=P)[:, 4 * half:4 * half + 4, :]
            pieces.append((rows, w_o[:, 0, 4 * half:4 * half + 4, :], w_o[:, 1, 4 * half:4 * half + 4, :]))
        pieces.append((xwqT.rearrange("(k p) n -> p k n", p=P), w_xq[:, 0, :, :], w_xq[:, 1, :, :]))
        pieces.append((gate_wT.rearrange("(k p) n -> p k n", p=P), w_gate[:, 0, :, :], w_gate[:, 1, :, :]))
        FEAT_PIECE = len(pieces)
        QKV_PIECES = 6

        def piece_stage(n, like):
            shape = like.shape
            cols = 1
            for d in shape[1:]:
                cols *= d
            v = w_stage[0:shape[0], n % 2, 0:cols]
            return v.rearrange("p (k n) -> p k n", k=shape[1]) if len(shape) == 3 else v

        block = stack.enter_context(nc.Block())

        @block.sync
        def _(sp):
            def load_piece(n):
                if n >= 2:
                    sp.wait_ge(*w_high(0, n - 1))
                    sp.wait_ge(*w_low(0, n - 1))
                if n == FEAT_PIECE:
                    for parity in range(2):
                        rows = slice(HD * parity, HD * parity + HD)
                        sp.dma_start(w_stage[rows, n % 2, 0:NF], wfeat).then_inc(w_loaded[n % 2].sem, 16)
                else:
                    src, high, _ = pieces[n]
                    sp.dma_start(piece_stage(n, high), src).then_inc(w_loaded[n % 2].sem, 16)

            def load_x(ab):
                sp.dma_start(x_stage[:, :, :], xT[:, :, bass.ts(ab, TB)]).then_inc(xs_loaded.sem, 16)

            sp.dma_start(x_stage[:, :, :], xT[:, :, 0:TB]).then_inc(xs_loaded.sem, 16)
            load_piece(0)
            load_piece(1)
            for src, dst in ((ctxT, ctx_sb), (xwkT, xwk_sb), (xwvT, xwv_sb)):
                sp.dma_start(dst, src.rearrange("(k p) n -> p k n", p=P)).then_inc(ctx_loaded.sem, 16)
            for n in range(2, 4):
                load_piece(n)
            for n, v in enumerate((lam_q1, lam_k1, lam_q2, lam_k2)):
                sp.dma_start(lam_in[:, n, :], v.partition_broadcast(P)).then_inc(c_loaded.sem, 16)
            sp.dma_start(bias[:, :], e_bias.partition_broadcast(P)).then_inc(c_loaded.sem, 16)
            for n in range(4, FEAT_PIECE + 1):
                load_piece(n)

            sp.wait_ge(*zeros_v(0, 1))
            for b in range(B):
                sp.dma_start(xv_scr[b], xv[:, :, :, :]).then_inc(zero_stored.sem, 16)
            sp.wait_ge(*kb_high(0, 2 * B))
            sp.wait_ge(*kb_low(0, 2 * B))
            n_ctx = 0
            for b in range(B):
                for m in range(KD):
                    for part, row in ((0, 0), (0, 32), (1, 64)):
                        for q in range(4):
                            sp.dma_start(xk_scr[b, row:row + 32, 4 * m + q, :],
                                         kb_hl[32 * q:32 * q + 32, KD * b + m, part, :]
                                         ).then_inc(ctx_stored.sem, 16)
                            n_ctx += 1
            sp.wait_ge(*v_copied(0, B + 1))
            sp.wait_ge(*zero_stored(0, B))
            for b in range(B):
                for j in range(GH):
                    n0 = 0
                    while n0 < CTX:
                        r = CTX * j + n0
                        rows = min(CTX - n0, P - r % P)
                        sp.dma_start(
                            xv_scr[b, r % P:r % P + rows, :, r // P, (XV + 1) * j:(XV + 1) * (j + 1)],
                            v_ext[n0:n0 + rows, b, :, :].rearrange("n (g i) d -> n g i d", i=2)[:, :, j // 2, :]
                        ).then_inc(ctx_stored.sem, 16)
                        n_ctx += 1
                        n0 += rows

            def attention(ab):
                sp.wait_ge(*x_high(ab, 1))
                sp.wait_ge(*x_low(ab, 1))
                load_x((ab + 1) % NBLK)

            def tail(ab, fb):
                if fb is not None:
                    sp.wait_ge(*ln[2][3](fb, NT))
                sp.dma_start(resid[:, :, :], x[:, ab, :, :]).then_inc(xin_loaded.sem, 16)
                if fb is None:
                    sp.wait_ge(*ctx_stored(0, n_ctx))
                else:
                    sp.wait_ge(*xo_done(fb, 2 * NT))
                sp.dma_start(xk[0:96, :, :], xk_scr[ab // BLK_PER_BATCH]).then_inc(xkv_placed.sem, 16)
                sp.dma_start(xv[:, :, :, :], xv_scr[ab // BLK_PER_BATCH]).then_inc(xkv_placed.sem, 16)
                if fb is not None:
                    sp.wait_ge(*out_stored(fb, 1))
                sp.wait_ge(*xq_high(ab, KD))
                sp.wait_ge(*xq_low(ab, KD))
                for part, row in ((0, 0), (1, 32), (0, 64)):
                    for q in range(4):
                        sp.dma_start(xq[row:row + 32, q:NG:4, :], xq_hl[32 * q:32 * q + 32, part, :, :]
                                     ).then_inc(xq_placed.sem, 16)

            def ffn(fb):
                for e in range(EXPERTS):
                    if e >= 2:
                        sp.wait_ge(*u_done(fb, e - 1))
                    sp.dma_start(gu_w[:, e % 2, :, :], ffn_scr[e, :, :, 0:2 * D]).then_inc(gw_loaded[e % 2].sem, 16)
                    if e >= 4:
                        sp.wait_ge(*down_done(fb, 2 * (e - 3)))
                    sp.dma_start(down_w[:, e % 4, :, :], ffn_scr[e, :, :, 2 * D:FW]).then_inc(dw_loaded[e % 4].sem, 16)

            def store(fb):
                sp.wait_ge(*ln[2][3](fb, NT))
                sp.dma_start(out[:, fb, :, :], out_buf[:, :, :]).then_inc(out_stored.sem, 16)

            attention(0)
            for e in range(EXPERTS):
                if e >= 2:
                    sp.wait_ge(*fs_high(0, e - 1))
                    sp.wait_ge(*fs_low(0, e - 1))
                sp.dma_start(fs_in[:, e % 2, :], ffn_w[e]).then_inc(fs_loaded[e % 2].sem, 16)
                if e >= 1:
                    sp.wait_ge(*fs_high(0, e))
                    sp.wait_ge(*fs_low(0, e))
                    sp.dma_start(ffn_scr[e - 1], fs_out[:, (e - 1) % 2, :, :]
                                 ).then_inc(fs_stored[(e - 1) % 2].sem, 16)
            sp.wait_ge(*fs_high(0, EXPERTS))
            sp.wait_ge(*fs_low(0, EXPERTS))
            sp.dma_start(ffn_scr[EXPERTS - 1], fs_out[:, (EXPERTS - 1) % 2, :, :]
                         ).then_inc(fs_stored[(EXPERTS - 1) % 2].sem, 16)
            sp.wait_ge(*fs_stored[0](0, (EXPERTS + 1) // 2))
            sp.wait_ge(*fs_stored[1](0, EXPERTS // 2))
            tail(0, None)
            with sp.Fori(0, NBLK - 1) as i:
                attention(i + 1)
                ffn(i)
                store(i)
                tail(i + 1, i)
            ffn(NBLK - 1)
            store(NBLK - 1)
            sp.wait_ge(*xs_loaded(0, NBLK + 1))
            sp.wait_ge(*out_stored(0, NBLK))

        @block.gpsimd
        def _(pool):
            pool.memset(ident[:, :], 0.0).then_inc(consts.sem, 1)
            pool.memset(causal[:, :], 1.0).then_inc(consts.sem, 1)
            pool.memset(before_e[:, :, :], 1.0).then_inc(consts.sem, 1)
            pool.memset(before_g[:, :, :], 1.0).then_inc(consts.sem, 1)
            pool.memset(own_half[:, :], 1.0).then_inc(consts.sem, 1)
            pool.wait_ge(consts.sem, 5)
            pool.affine_select(out=ident[:, :], in_=ident[:, :], compare_op=ALU.not_equal, fill=1.0, base=0,
                               pattern=[[-1, P]], channel_multiplier=1).then_inc(consts.sem, 1)
            pool.affine_select(out=causal[:, :], in_=causal[:, :], compare_op=ALU.is_ge, fill=0.0, base=0,
                               pattern=[[1, P]], channel_multiplier=-1).then_inc(consts.sem, 1)
            pool.affine_select(out=before_e[:, :, :], in_=before_e[:, :, :], compare_op=ALU.is_gt, fill=0.0, base=0,
                               pattern=[[1, NE], [-1, NE]], channel_multiplier=0).then_inc(consts.sem, 1)
            pool.affine_select(out=before_g[:, :, :], in_=before_g[:, :, :], compare_op=ALU.is_gt, fill=0.0, base=0,
                               pattern=[[1, NGROUP], [-1, NGROUP]], channel_multiplier=0).then_inc(consts.sem, 1)
            pool.affine_select(out=own_half[:, :], in_=own_half[:, :], compare_op=ALU.is_ge, fill=0.0, base=0,
                               pattern=[[-XD, P // XD]], channel_multiplier=1).then_inc(consts.sem, 1)
            pool.wait_ge(consts.sem, 10)
            pool.affine_select(out=own_half[:, :], in_=own_half[:, :], compare_op=ALU.is_ge, fill=0.0, base=XD - 1,
                               pattern=[[XD, P // XD]], channel_multiplier=-1).then_inc(consts.sem, 1)

            def shared(ab, cb):
                for s in range(LAST):
                    for kind, n in steps(s, ab is not None, cb is not None):
                        if kind == "project":
                            pool.wait_ge(*p_sqh(ab, n + 1))
                            pool.tensor_tensor(qk[:, n % 2, n // 2 % 2, 3, :], square[:, n % 2, :],
                                               qk[:, n % 2, n // 2 % 2, 2, :], ALU.subtract).then_inc(p_sql.sem, 1)
                        elif kind == "values" and n % GH == GH - 1:
                            half = n // GH
                            cols = slice(P * (half % 2), P * (half % 2) + P)
                            pool.wait_ge(*xo_kept(cb, half + 1))
                            pool.tensor_tensor(xsum[:, half % 2, :, :], xterm[:, half % 2, :, 0, :],
                                               xterm[:, half % 2, :, 1, :], ALU.add).then_inc(xo_sum.sem, 1)
                            pool.wait_ge(*xo_sum(cb, half + 1))
                            pool.tensor_tensor(resid[:, half // 2, cols], resid[:, half // 2, cols],
                                               xsum[:, half % 2, :, :].rearrange("p h d -> p (h d)"),
                                               ALU.add).then_inc(xo_added.sem, 1)

            def ffn(fb):
                for e in range(EXPERTS):
                    pool.wait_ge(*h_high(fb, e + 1))
                    pool.tensor_tensor(hT[:, e % 3, 1, :], hid[:, e % 2, :], hT[:, e % 3, 0, :],
                                       ALU.subtract).then_inc(h_low.sem, 1)

            shared(0, None)
            with pool.Fori(0, NBLK - 1) as i:
                shared(i + 1, i)
                ffn(i)
            shared(None, NBLK - 1)
            ffn(NBLK - 1)

        @block.scalar
        def _(act):
            def split_high(n, dst, src, scale):
                act.wait_ge(*w_loaded[n % 2](0, n // 2 + 1))
                act.activation(dst, src, ACT.Copy, scale=scale).then_inc(w_high.sem, 1)

            for n in range(2):
                split_high(n, pieces[n][1], piece_stage(n, pieces[n][1]), W_SCALE)
            for n in range(2, FEAT_PIECE):
                split_high(n, pieces[n][1], piece_stage(n, pieces[n][1]), W_SCALE)
            act.wait_ge(*w_loaded[FEAT_PIECE % 2](0, FEAT_PIECE // 2 + 2))
            act.wait_ge(*zeros_v(0, 2))
            for parity in range(2):
                rows = slice(HD * parity, HD * parity + HD)
                last = act.activation(w_feat[rows, parity, 0, :], w_stage[rows, FEAT_PIECE % 2, 0:NF], ACT.Copy)
            last.then_inc(w_high.sem, 1)
            act.wait_ge(*lam_step(0, 2))
            act.activation(lam_exp[:, :], lam_sum[:, :], ACT.Exp).then_inc(lam_exped.sem, 1)

            def shared(ab, cb):
                for v in range(2 * NT if ab is not None else 0):
                    act.wait_ge(*v_done(ab, v + 1))
                    act.activation(v1[:, v // 2, H // 2 * (v % 2):H // 2 * (v % 2 + 1), 0:HD],
                                   ps_a[v % 2][:, :].rearrange("p (h d) -> p h d", d=HD), ACT.Copy,
                                   scale=1 / W_SCALE).then_inc(v_kept.sem, 1)
                a_jobs = 2 * NT if ab is not None else 0
                for s in range(LAST):
                    for kind, n in steps(s, ab is not None, cb is not None):
                        if kind == "project":
                            bank = ps_a[a_jobs % 2]
                            act.wait_ge(*p_done(ab, n + 1))
                            act.activation(qk[:, n % 2, n // 2 % 2, 0, :], bank[:, :], ACT.Copy,
                                           scale=1 / W_SCALE).then_inc(p_high.sem, 1)
                            if n >= 2:
                                act.wait_ge(*p_sql(ab, n - 1))
                            act.activation(square[:, n % 2, :], bank[:, :], ACT.Square,
                                           scale=1 / W_SCALE).then_inc(p_sq.sem, 1)
                        elif kind == "turn keys":
                            act.wait_ge(*turned_k(ab, n + 1))
                            act.activation(kt[:, n % 2, :, :].rearrange("p c f -> p (c f)"), ps_turn[:, :],
                                           ACT.Copy).then_inc(kt_kept.sem, 1)
                        elif kind == "q features":
                            act.wait_ge(*qf_done(ab, n + 1))
                            act.activation(qf[:, n % 4, :], ps_qf[:, :], ACT.Exp).then_inc(qf_exp.sem, 1)
                        elif kind == "k features":
                            act.wait_ge(*kf_done(ab, n + 1))
                            act.activation(kf[:, n % 2, :], ps_kf[:, :], ACT.Exp).then_inc(kf_exp.sem, 1)
                        elif kind == "exp":
                            act.wait_ge(*sc_sub(cb, n + 1))
                            act.activation(prob[:, n % 4, 0:GN], prob[:, n % 4, 0:GN], ACT.Exp,
                                           scale=float(XD) ** -0.5).then_inc(pr_exp.sem, 1)
                        elif kind == "turn probs" and n % 2 == 0:
                            act.wait_ge(*pr_turned(cb, n + 1))
                            act.activation(probT[:, n % 4, :, :].rearrange("p c t -> p (c t)"),
                                           ps_turn[:, 0:GC * P], ACT.Copy).then_inc(pr_kept_a.sem, 1)
                        elif kind == "turn output":
                            act.wait_ge(*yt_done(ab, n + 1))
                            act.activation(yT[:, 0, n, :], ps_turn[:, :], ACT.Copy).then_inc(yt_high.sem, 1)
                        elif kind == "turn cross":
                            act.wait_ge(*x2_turned(cb, n + 1))
                            act.activation(turned[:, 0, :, P * n:P * n + P],
                                           ps_turn[:, 0:D].rearrange("p (k t) -> p k t", k=KD),
                                           ACT.Copy).then_inc(x2_high.sem, 1)
                        if kind in ("project", "scores"):
                            a_jobs += 1
                    if ab is not None and cb is None and s < EXPERTS:
                        act.wait_ge(*fs_loaded[s % 2](0, s // 2 + 1))
                        if s >= 2:
                            act.wait_ge(*fs_stored[s % 2](0, s // 2))
                        act.activation(fs_out[:, s % 2, 0, :], fs_in[:, s % 2, :], ACT.Copy,
                                       scale=W_SCALE).then_inc(fs_high.sem, 1)

            def ffn(fb):
                act.wait_ge(*gl_done(fb, 1))
                act.activation(ge[:, :], ps_turn[:, 0:NT * NE], ACT.Exp, scale=-1 / W_SCALE).then_inc(gl_exp.sem, 1)
                for e in range(EXPERTS + 1):
                    if e < EXPERTS:
                        act.wait_ge(*g_done(fb, e + 1))
                        if e >= 2:
                            act.wait_ge(*h_low(fb, e - 1))
                        act.activation(hid[:, e % 2, :], (ps_a[0], ps_qf)[e % 2][:, :], ACT.Silu,
                                       scale=1 / W_SCALE).then_inc(silu.sem, 1)
                    if e >= 1:
                        act.wait_ge(*hid_ready(fb, e))
                        if e >= 4:
                            act.wait_ge(*down_done(fb, 2 * (e - 3)))
                        act.activation(hT[:, (e - 1) % 3, 0, :], hid[:, (e - 1) % 2, :],
                                       ACT.Copy).then_inc(h_high.sem, 1)

            def tail(ab):
                for c in range(NT):
                    act.wait_ge(*x1_turned(ab, c + 1))
                    act.activation(turned[:, 0, :, P * c:P * c + P],
                                   (ps_att, ps_so, ps_turn, ps_xo)[c][:, 0:D].rearrange("p (k t) -> p k t", k=KD),
                                   ACT.Copy).then_inc(x1_high.sem, 1)
                for m in range(KD):
                    act.wait_ge(*xq_done(ab, m + 1))
                    act.activation(xq_hl[:, 0, m, :], ps_a[m][:, :], ACT.Copy, scale=1 / W_SCALE).then_inc(xq_high.sem, 1)

            shared(0, None)
            tail(0)
            with act.Fori(0, NBLK - 1) as i:
                shared(i + 1, i)
                ffn(i)
                tail(i + 1)
            shared(None, NBLK - 1)
            ffn(NBLK - 1)

        @block.vector
        def _(dve):
            dve.memset(xv[:, :, :, :], 0.0).then_inc(zeros_v.sem, 1)
            dve.memset(w_feat[:, :, :, :], 0.0).then_inc(zeros_v.sem, 1)
            dve.memset(neg_half[:, :, :], 0.0).then_inc(v_ones.sem, 1)
            dve.memset(v1[:, :, :, HD:V1], 1.0).then_inc(v_ones.sem, 1)
            dve.memset(state[:, :, :], 0.0).then_inc(v_ones.sem, 1)
            dve.memset(keep[:, :], 0.0).then_inc(v_ones.sem, 1)
            dve.memset(coef[:, :, :], 1.0).then_inc(v_ones.sem, 1)
            dve.wait_ge(*v_ones(0, 5))
            for parity in range(2):
                dve.memset(neg_half[HD * parity:HD * parity + HD, parity, :], -0.5).then_inc(v_ones.sem, 1)

            def split_x(ab):
                dve.wait_ge(*xs_loaded(ab, 1))
                dve.tensor_copy(x_split[:, 0, :, :], x_stage[:, :, :]).then_inc(x_high.sem, 1)
                dve.wait_ge(*x_high(ab, 1))
                dve.tensor_tensor(x_split[:, 1, :, :], x_stage[:, :, :], x_split[:, 0, :, :],
                                  ALU.subtract).then_inc(x_low.sem, 1)

            def split_low(n):
                _, high, low = pieces[n]
                dve.wait_ge(*w_high(0, n + 1))
                dve.scalar_tensor_tensor(low, piece_stage(n, high), W_SCALE, high, ALU.mult,
                                         ALU.subtract).then_inc(w_low.sem, 1)

            split_x(0)
            for n in range(QKV_PIECES):
                split_low(n)

            dve.wait_ge(consts.sem, 11)
            dve.tensor_reduce(own_row[:, :, 0], own_half[:, :].rearrange("p (q j) -> p j q", j=GH), AX.X,
                              ALU.add).then_inc(own_ready.sem, 1)
            dve.wait_ge(*own_ready(0, 1))
            dve.memset(v_ext[0:CTX, :, :, XV:XV + 1], 1.0).then_inc(v_copied.sem, 1)
            for b in range(B):
                for m in range(KD):
                    n = KD * b + m
                    dve.wait_ge(*xkv_done(0, 1))
                    if n:
                        dve.wait_ge(*kb_low(0, n))
                    dve.tensor_tensor(kb_full, ps_att[:, CTX * n:CTX * n + CTX].unsqueeze(1).to_broadcast([P, GH, CTX]),
                                      own_row[:, :, :].to_broadcast([P, GH, CTX]), ALU.mult).then_inc(kb_masked.sem, 1)
                    dve.wait_ge(*kb_masked(0, n + 1))
                    flat_full = kb_full.rearrange("p j n -> p (j n)")
                    dve.tensor_copy(kb_hl[:, n, 0, :], flat_full).then_inc(kb_high.sem, 1)
                    dve.wait_ge(*kb_high(0, n + 1))
                    dve.tensor_tensor(kb_hl[:, n, 1, :], flat_full, kb_hl[:, n, 0, :],
                                      ALU.subtract).then_inc(kb_low.sem, 1)
                dve.tensor_copy(v_ext[0:CTX, b, :, 0:XV],
                                ps_so[0:CTX, D * b:D * b + D].rearrange("p (h d) -> p h d", d=XV)
                                ).then_inc(v_copied.sem, 1)
            for n in range(QKV_PIECES, FEAT_PIECE):
                split_low(n)
            dve.wait_ge(*w_high(0, FEAT_PIECE + 1))
            for parity in range(2):
                rows = slice(HD * parity, HD * parity + HD)
                last = dve.tensor_tensor(w_feat[rows, parity, 1, :], w_stage[rows, FEAT_PIECE % 2, 0:NF],
                                         w_feat[rows, parity, 0, :], ALU.subtract)
            last.then_inc(w_low.sem, 1)
            dve.wait_ge(*c_loaded(0, 5))
            dve.tensor_tensor(lam_prod[:, :, :], lam_in[:, 0:4:2, :], lam_in[:, 1:4:2, :], ALU.mult).then_inc(lam_step.sem, 1)
            dve.wait_ge(*lam_step(0, 1))
            dve.tensor_reduce(lam_sum[:, :], lam_prod[:, :, :], AX.X, ALU.add).then_inc(lam_step.sem, 1)
            dve.wait_ge(*lam_exped(0, 1))
            dve.tensor_tensor(lam_sum[:, 0:1], lam_exp[:, 1:2], lam_exp[:, 0:1], ALU.subtract).then_inc(lam_step.sem, 1)
            dve.wait_ge(*lam_step(0, 3))
            dve.tensor_scalar(coef[:, 1:XV:2, 0], lam_sum[:, 0:1].to_broadcast([P, XV // 2]), -LAMBDA_INIT, None,
                              ALU.add).then_inc(coef_ready.sem, 1)

            def statistics(which, blk, c):
                stats, mean_var = ln[which][:2]
                dve.bn_stats(st[:, c, :], resid[:, c, :]).then_inc(stats.sem, 1)
                dve.wait_ge(*stats(blk, c + 1))
                dve.sem_inc(held.sem, 1)
                dve.bn_aggr(mv[:, c, :], st[:, c, :]).then_inc(mean_var.sem, 1)

            def inverse_root(which, blk, tiles, call):
                step = ln[which][2]
                n = [ROOT_STEPS * call]

                def link(ins):
                    n[0] += 1
                    ins.then_inc(step.sem, 1)
                    dve.wait_ge(*step(blk, n[0]))

                v, a, r = root_v[:, tiles, 0], root_a[:, tiles, 0], rstd[:, tiles, 0]
                link(dve.tensor_scalar(v, mv[:, tiles, 1], LN_EPS, None, ALU.add))
                link(dve.tensor_scalar(a.bitcast(I32), v.bitcast(I32), 1, None, ALU.logical_shift_right))
                link(dve.tensor_scalar(r.bitcast(I32), a.bitcast(I32), -1.0, float(0x5F3759DF), ALU.mult, ALU.add))
                for _ in range(3):
                    link(dve.tensor_tensor(a, r, r, ALU.mult))
                    link(dve.scalar_tensor_tensor(a, a, -0.5, v, ALU.mult, ALU.mult))
                    link(dve.scalar_tensor_tensor(r, a, 1.5, r, ALU.add, ALU.mult))

            def normed(which, c, dst):
                dve.tensor_scalar(dst, resid[:, c, :], mv[:, c, 0:1], rstd[:, c, :], ALU.subtract,
                                  ALU.mult).then_inc(ln[which][3].sem, 1)

            def shared(ab, cb):
                first = cb is None
                a_jobs = 2 * NT if ab is not None else 0
                if ab is not None and not first:
                    split_x(ab)
                for s in range(LAST):
                    for kind, n in steps(s, ab is not None, cb is not None):
                        if kind == "project":
                            bank = ps_a[a_jobs % 2]
                            half = qk[:, n % 2, n // 2 % 2, :, :]
                            dve.wait_ge(*p_sq(ab, n + 1))
                            dve.scalar_tensor_tensor(half[:, 1, :], bank[:, :], 1 / W_SCALE, half[:, 0, :], ALU.mult,
                                                     ALU.subtract).then_inc(p_low.sem, 1)
                            dve.tensor_copy(half[:, 2, :], square[:, n % 2, :]).then_inc(p_sqh.sem, 1)
                        elif kind == "attend":
                            dve.wait_ge(*att_done(ab, n + 1))
                            dve.tensor_tensor(att[:, n % 3, :, :], ps_att[:, :].rearrange("p (c t) -> p c t", t=P),
                                              causal[:, :].unsqueeze(1).to_broadcast([P, NT, P]),
                                              ALU.mult).then_inc(att_kept.sem, 1)
                        elif kind == "state":
                            r = run[:, n % 2, :, :]
                            if n == 0:
                                if ab is first:
                                    pass
                            dve.wait_ge(*st_done(ab, n + 1))
                            dve.tensor_scalar(r[:, 0, :], state[:, n, :], keep[:, 0:1], None, ALU.mult
                                              ).then_inc(run_step.sem, 1)
                            for c in range(1, NT + 1):
                                dve.wait_ge(*run_step(ab, 4 * n + c))
                                dst = r[:, c, :] if c < NT else state[:, n, :]
                                dve.tensor_tensor(dst, r[:, c - 1, :], ps_so[:, V1 * (c - 1):V1 * c], ALU.add
                                                  ).then_inc((run_step if c < NT else run_ready).sem, 1)
                        elif kind == "output":
                            o = ps_so[:, 0:NT * V1].rearrange("p (c v) -> p c v", v=V1)
                            dve.wait_ge(*o_done(ab, n + 1))
                            dve.tensor_scalar(den[:, n % 2, :, :], o[:, :, HD:V1], EPS, None, ALU.add
                                              ).then_inc(o_den.sem, 1)
                            dve.wait_ge(*o_den(ab, n + 1))
                            dve.reciprocal(rec[:, n % 2, :, :], den[:, n % 2, :, :]).then_inc(o_rec.sem, 1)
                            dve.wait_ge(*o_rec(ab, n + 1))
                            dve.tensor_tensor(y[:, n // 2 % 2, :, HD * (n % 2):HD * (n % 2) + HD], o[:, :, 0:HD],
                                              rec[:, n % 2, :, :].to_broadcast([P, NT, HD]), ALU.mult
                                              ).then_inc(o_kept.sem, 1)
                        elif kind == "turn output":
                            dve.wait_ge(*yt_high(ab, n + 1))
                            dve.tensor_tensor(yT[:, 1, n, :], ps_turn[:, :], yT[:, 0, n, :], ALU.subtract
                                              ).then_inc(yt_low.sem, 1)
                        elif kind == "scores":
                            sc = ps_a[a_jobs % 2][:, 0:GN].rearrange("p (j n) -> p j n", j=GH)
                            dve.wait_ge(*sc_done(cb, n + 1))
                            dve.tensor_reduce(xmax[:, n % 4, :, 0], sc, AX.X, ALU.max).then_inc(sc_max.sem, 1)
                            dve.wait_ge(*sc_max(cb, n + 1))
                            if n >= 4:
                                dve.wait_ge(*pr_turned(cb, n - 3))
                            dve.tensor_tensor(prob[:, n % 4, 0:GN].rearrange("p (j n) -> p j n", j=GH), sc,
                                              xmax[:, n % 4, :, :].to_broadcast([P, GH, CTX]), ALU.subtract
                                              ).then_inc(sc_sub.sem, 1)
                        elif kind == "turn probs" and n % 2 == 1:
                            dve.wait_ge(*pr_turned(cb, n + 1))
                            dve.tensor_copy(probT[:, n % 4, :, :].rearrange("p c t -> p (c t)"),
                                            ps_turn[:, 0:GC * P]).then_inc(pr_kept_v.sem, 1)
                        elif kind == "values" and n % GH == GH - 1:
                            half = n // GH
                            o = ps_xo[:, 0:GH * GV].rearrange("p (h v) -> p h v", v=XV + 1)
                            dve.wait_ge(*xo_done(cb, half + 1))
                            dve.reciprocal(xrec[:, half % 2, :, :], o[:, :, XV:XV + 1]).then_inc(xo_rec.sem, 1)
                            dve.wait_ge(*xo_rec(cb, half + 1))
                            dve.tensor_tensor(xrec2[:, half % 2, :, :], xrec[:, half % 2, :, :], coef[:, :, :],
                                              ALU.mult).then_inc(xo_coef.sem, 1)
                            dve.wait_ge(*xo_coef(cb, half + 1))
                            if half >= 2:
                                dve.wait_ge(*xo_sum(cb, half - 1))
                            dve.tensor_tensor(xterm[:, half % 2, :, :, :].rearrange("p h i d -> p (h i) d"),
                                              o[:, :, 0:XV], xrec2[:, half % 2, :, :].to_broadcast([P, XV, XV]),
                                              ALU.mult).then_inc(xo_kept.sem, 1)
                        elif kind == "norm":
                            dve.wait_ge(*xo_added(cb, 2 * n + 2))
                            statistics(1, cb, n)
                            dve.wait_ge(*ln[1][1](cb, n + 1))
                            inverse_root(1, cb, slice(n, n + 1), n)
                            normed(1, n, resid[:, n, :])
                        elif kind == "turn cross":
                            dve.wait_ge(*x2_high(cb, n + 1))
                            dve.tensor_tensor(turned[:, 1, :, P * n:P * n + P],
                                              ps_turn[:, 0:D].rearrange("p (k t) -> p k t", k=KD),
                                              turned[:, 0, :, P * n:P * n + P], ALU.subtract).then_inc(x2_low.sem, 1)
                        if kind in ("project", "scores"):
                            a_jobs += 1
                    if ab is not None and first and s < EXPERTS:
                        dve.wait_ge(*fs_high(0, s + 1))
                        dve.scalar_tensor_tensor(fs_out[:, s % 2, 1, :], fs_in[:, s % 2, :], W_SCALE,
                                                 fs_out[:, s % 2, 0, :], ALU.mult, ALU.subtract).then_inc(fs_low.sem, 1)
                if ab is not None:
                    dve.tensor_scalar(keep[:, :], keep[:, :], -1.0, 1.0, ALU.mult, ALU.add).then_inc(keep_set.sem, 1)

            def ffn(fb):
                done = [0]

                def link(ins):
                    done[0] += 1
                    ins.then_inc(route.sem, 1)
                    dve.wait_ge(*route(fb, done[0]))

                def routing():
                    f = "p t e -> p (t e)"
                    dve.wait_ge(*gl_exp(fb, 1))
                    link(dve.tensor_scalar(gd[:, :], ge[:, :], 1.0, None, ALU.add))
                    link(dve.reciprocal(score[:, :, :].rearrange(f), gd[:, :]))
                    link(dve.tensor_tensor(choice[:, :, :], score[:, :, :],
                                           bias[:, :].unsqueeze(1).to_broadcast([P, NT, NE]), ALU.add))
                    two = choice[:, :, :].rearrange("p t (g q i) -> p (t g) q i", g=NGROUP, i=2)
                    link(dve.tensor_tensor(g_max[:, :, :], two[:, :, :, 0], two[:, :, :, 1], ALU.max))
                    link(dve.tensor_tensor(g_min[:, :, :], two[:, :, :, 0], two[:, :, :, 1], ALU.min))
                    link(dve.tensor_tensor(g_a[:, :], g_max[:, :, 0], g_max[:, :, 1], ALU.max))
                    link(dve.tensor_tensor(g_b[:, :], g_max[:, :, 0], g_max[:, :, 1], ALU.min))
                    link(dve.tensor_tensor(g_c[:, :], g_min[:, :, 0], g_min[:, :, 1], ALU.max))
                    link(dve.tensor_tensor(g_d[:, :], g_b[:, :], g_c[:, :], ALU.max))
                    link(dve.tensor_tensor(g_sum[:, :, :].rearrange("p t g -> p (t g)"), g_a[:, :], g_d[:, :], ALU.add))

                    def ranks(v, gt, eq, before, n, rank):
                        other = v.unsqueeze(2).to_broadcast([P, NT, n, n])
                        own = v.unsqueeze(3).to_broadcast([P, NT, n, n])
                        link(dve.tensor_tensor(gt, other, own, ALU.is_gt))
                        link(dve.tensor_tensor(eq, other, own, ALU.is_equal))
                        link(dve.tensor_tensor(eq, eq, before.unsqueeze(1).to_broadcast([P, NT, n, n]), ALU.mult))
                        link(dve.tensor_tensor(gt, gt, eq, ALU.add))
                        link(dve.tensor_reduce(rank, gt.rearrange("p t i j -> p (t i) j"), AX.X, ALU.add))

                    ranks(g_sum[:, :, :], g_gt[:, :, :, :], g_eq[:, :, :, :], before_g[:, :, :], NGROUP, g_rank[:, :])
                    link(dve.tensor_scalar(g_in[:, :, 0], g_rank[:, :], TOPK_GROUP - 0.5, None, ALU.is_lt))
                    link(dve.tensor_tensor(masked[:, :, :].rearrange("p t (g i) -> p (t g) i", g=NGROUP),
                                           choice[:, :, :].rearrange("p t (g i) -> p (t g) i", g=NGROUP),
                                           g_in[:, :, :].to_broadcast([P, NT * NGROUP, PER_GROUP]), ALU.mult))
                    ranks(masked[:, :, :], e_gt[:, :, :].rearrange("p t (i j) -> p t i j", i=NE),
                          e_eq[:, :, :].rearrange("p t (i j) -> p t i j", i=NE), before_e[:, :, :], NE, e_rank[:, :])
                    link(dve.scalar_tensor_tensor(chosen[:, :, :].rearrange(f), e_rank[:, :], TOPK - 0.5,
                                                  score[:, :, :].rearrange(f), ALU.is_lt, ALU.mult))
                    link(dve.tensor_reduce(w_sum[:, :], chosen[:, :, :], AX.X, ALU.add))
                    link(dve.tensor_scalar(w_sum[:, :], w_sum[:, :], 1e-20, None, ALU.add))
                    link(dve.reciprocal(w_rec[:, :], w_sum[:, :]))
                    link(dve.tensor_scalar(w_rec2[:, :, 0], w_rec[:, :], SCALING / W_SCALE, None, ALU.mult))
                    link(dve.tensor_tensor(weight[:, :, :], chosen[:, :, :],
                                           w_rec2[:, :, :].to_broadcast([P, NT, NE]), ALU.mult))
                    assert done[0] == ROUTE_STEPS

                for e in range(EXPERTS + 2):
                    if e < EXPERTS:
                        dve.wait_ge(*u_done(fb, e + 1))
                        dve.wait_ge(*silu(fb, e + 1))
                        dve.scalar_tensor_tensor(hid[:, e % 2, :], (ps_a[1], ps_kf)[e % 2][:, :], 1 / W_SCALE,
                                                 hid[:, e % 2, :], ALU.mult, ALU.mult).then_inc(hid_ready.sem, 1)
                    if e == 1:
                        routing()
                    if e >= 2:
                        d = e - 2
                        for half in range(2):
                            bank = ((ps_att, ps_so), (ps_turn, ps_xo))[d % 2][half]
                            dve.wait_ge(*down_done(fb, 2 * d + half + 1))
                            if d >= 1:
                                dve.wait_ge(*summed(fb, 2 * (d - 1) + half + 1))
                            for k in range(2):
                                c = 2 * half + k
                                by = 1 / W_SCALE if d == 0 else weight[:, c, d - 1:d]
                                last = dve.scalar_tensor_tensor(resid[:, c, :], bank[:, D * k:D * k + D], by,
                                                                resid[:, c, :], ALU.mult, ALU.add)
                            last.then_inc(summed.sem, 1)
                dve.wait_ge(*summed(fb, 2 * EXPERTS))
                for c in range(NT):
                    statistics(2, fb, c)
                dve.wait_ge(*ln[2][1](fb, NT))
                inverse_root(2, fb, slice(0, NT), 0)
                for c in range(NT):
                    normed(2, c, out_buf[:, c, :])

            def tail(ab):
                for c in range(NT):
                    bank = (ps_a[0], ps_a[1], ps_qf, ps_kf)[c]
                    if c == 0:
                        dve.wait_ge(*xin_loaded(ab, 1))
                    dve.wait_ge(*wo_done(ab, c + 1))
                    dve.scalar_tensor_tensor(resid[:, c, :], bank[:, 0:D], 1 / W_SCALE, resid[:, c, :], ALU.mult,
                                             ALU.add).then_inc(x1_added.sem, 1)
                    dve.wait_ge(*x1_added(ab, c + 1))
                    statistics(0, ab, c)
                dve.wait_ge(*ln[0][1](ab, NT))
                inverse_root(0, ab, slice(0, NT), 0)
                for c in range(NT):
                    normed(0, c, resid[:, c, :])
                for c in range(NT):
                    dve.wait_ge(*x1_high(ab, c + 1))
                    dve.tensor_tensor(turned[:, 1, :, P * c:P * c + P],
                                      (ps_att, ps_so, ps_turn, ps_xo)[c][:, 0:D].rearrange("p (k t) -> p k t", k=KD),
                                      turned[:, 0, :, P * c:P * c + P], ALU.subtract).then_inc(x1_low.sem, 1)
                for m in range(KD):
                    dve.wait_ge(*xq_high(ab, m + 1))
                    dve.scalar_tensor_tensor(xq_hl[:, 1, m, :], ps_a[m][:, :], 1 / W_SCALE, xq_hl[:, 0, m, :], ALU.mult,
                                             ALU.subtract).then_inc(xq_low.sem, 1)

            pads = signal("pads")
            held = signal("held")
            shared(0, None)
            dve.wait_ge(*ctx_stored(0, 4 * 12 + 2 * 6))
            dve.memset(prob[:, :, GN:GC * P], 0.0).then_inc(pads.sem, 1)
            tail(0)
            with dve.Fori(0, NBLK - 1) as i:
                shared(i + 1, i)
                ffn(i)
                tail(i + 1)
            shared(None, NBLK - 1)
            ffn(NBLK - 1)

        @block.tensor
        def _(pe):
            def three_pass(dst, lhs, rhs, first=True, last=True):
                for n, (i, j) in enumerate(((0, 0), (0, 1), (1, 0))):
                    ins = pe.matmul(dst, lhs(i), rhs(j), start=first and n == 0, stop=last and n == 2)
                return ins

            pe.wait_ge(*ctx_loaded(0, 3))
            for b in range(B):
                for m in range(KD):
                    n = KD * b + m
                    for k in range(KD):
                        pe.matmul(ps_att[:, CTX * n:CTX * n + CTX], xwk_sb[:, k, P * m:P * m + P],
                                  ctx_sb[:, k, CTX * b:CTX * b + CTX], start=(k == 0), stop=(k == KD - 1))
            for b in range(B):
                for k in range(KD):
                    last = pe.matmul(ps_so[0:CTX, D * b:D * b + D], ctx_sb[:, k, CTX * b:CTX * b + CTX],
                                     xwv_sb[:, k, :], start=(k == 0), stop=(k == KD - 1))
            last.then_inc(xkv_done.sem, 1)

            def values(ab, cb):
                pe.wait_ge(*x_high(ab, 1))
                pe.wait_ge(*x_low(ab, 1))
                for v in range(2 * NT):
                    c, n = v // 2, v % 2
                    if v >= 2:
                        pe.wait_ge(*v_kept(ab, v - 1))
                    if cb is None and v == 0:
                        pe.wait_ge(*w_low(0, 2))
                    for k in range(KD):
                        last = three_pass(ps_a[n][:, :], lambda i: x_split[:, i, k, P * c:P * c + P],
                                          lambda j: w_v[:, j, k, 512 * n:512 * n + 512], k == 0, k == KD - 1)
                    last.then_inc(v_done.sem, 1)

            def shared(ab, cb):
                tb = ab - 1 if ab is not None else cb
                if cb is not None:
                    pe.wait_ge(*xq_high(tb, KD))
                    pe.wait_ge(*xq_low(tb, KD))
                a_jobs = 0
                a_free = [[], []]
                turn_free = []
                if ab is not None:
                    values(ab, cb)
                    a_jobs = 2 * NT
                    a_free = [[v_kept(ab, 2 * NT - 1)], [v_kept(ab, 2 * NT)]]
                for s in range(LAST):
                    for kind, n in steps(s, ab is not None, cb is not None):
                        if kind in ("project", "scores"):
                            bank = ps_a[a_jobs % 2]
                            for free in a_free[a_jobs % 2]:
                                pe.wait_ge(*free)
                        if kind.startswith("turn"):
                            for free in turn_free:
                                pe.wait_ge(*free)
                        if kind == "project":
                            w = (w_q, w_k)[n % 2]
                            if cb is None and n < 2:
                                pe.wait_ge(*w_low(0, 4 + 2 * n))
                            for k in range(KD):
                                last = three_pass(bank[:, :], lambda i: w[:, i, k, P * (n // 2):P * (n // 2) + P],
                                                  lambda j: x_split[:, j, k, :], k == 0, k == KD - 1)
                            last.then_inc(p_done.sem, 1)
                            a_free[a_jobs % 2] = [p_sq(ab, n + 1), p_low(ab, n + 1)]
                        elif kind == "turn keys":
                            if n == 0 and cb is None:
                                pe.wait_ge(consts.sem, 11)
                            pe.wait_ge(*kf_exp(ab, n + 1))
                            for c in range(NT):
                                last = pe.transpose(ps_turn[:, P * c:P * c + P], kf[:, n % 2, P * c:P * c + P], ident[:, :])
                            last.then_inc(turned_k.sem, 1)
                            turn_free = [kt_kept(ab, n + 1)]
                        elif kind in ("q features", "k features"):
                            w, to = (0, ps_qf) if kind == "q features" else (1, ps_kf)
                            source = qk[:, w, n // 2 % 2, :, :]
                            job = 2 * (n // 2) + w + 1
                            if n == 0 and w == 0 and cb is None:
                                pe.wait_ge(*w_low(0, FEAT_PIECE + 1))
                                pe.wait_ge(*v_ones(0, 7))
                            pe.wait_ge(*p_low(ab, job))
                            pe.wait_ge(*p_sql(ab, job))
                            if n:
                                pe.wait_ge(*(qf_exp, kf_exp)[w](ab, n))
                            wf = w_feat[:, n % 2, :, :]
                            pe.matmul(to[:, :], wf[:, 0, :], source[:, 0, :], start=True, stop=False)
                            pe.matmul(to[:, :], wf[:, 0, :], source[:, 1, :], start=False, stop=False)
                            pe.matmul(to[:, :], wf[:, 1, :], source[:, 0, :], start=False, stop=False)
                            pe.matmul(to[:, :], neg_half[:, n % 2, :], source[:, 2, :], start=False, stop=False)
                            pe.matmul(to[:, :], neg_half[:, n % 2, :], source[:, 3, :], start=False, stop=True
                                      ).then_inc((qf_done, kf_done)[w].sem, 1)
                        elif kind == "attend":
                            pe.wait_ge(*qf_exp(ab, n + 1))
                            if n:
                                pe.wait_ge(*att_kept(ab, n))
                            for c in range(NT):
                                t = slice(P * c, P * c + P)
                                last = pe.matmul(ps_att[:, t], kf[:, n % 2, t], qf[:, n % 4, t], start=True, stop=True)
                            last.then_inc(att_done.sem, 1)
                        elif kind == "state":
                            pe.wait_ge(*kt_kept(ab, n + 1))
                            if n == 0:
                                pe.wait_ge(*v_kept(ab, 2 * NT))
                            if n == 1:
                                pe.wait_ge(*run_ready(ab, 1))
                            if n >= 2:
                                pe.wait_ge(*o_kept(ab, n - 1))
                            for c in range(NT):
                                last = pe.matmul(ps_so[:, V1 * c:V1 * c + V1], kt[:, n % 2, c, :], v1[:, c, n, :],
                                                 start=True, stop=True)
                            last.then_inc(st_done.sem, 1)
                        elif kind == "output":
                            pe.wait_ge(*att_kept(ab, n + 1))
                            if n + 1 < H:
                                pe.wait_ge(*run_ready(ab, n + 2))
                            else:
                                pe.wait_ge(*o_kept(ab, n))
                            for c in range(NT):
                                o = ps_so[:, V1 * c:V1 * c + V1]
                                pe.matmul(o, att[:, n % 3, c, :], v1[:, c, n, :], start=True, stop=False)
                                last = pe.matmul(o, qf[:, n % 4, P * c:P * c + P], run[:, n % 2, c, :],
                                                 start=False, stop=True)
                            last.then_inc(o_done.sem, 1)
                        elif kind == "turn output":
                            pe.wait_ge(*o_kept(ab, 2 * n + 2))
                            for c in range(NT):
                                last = pe.transpose(ps_turn[:, P * c:P * c + P], y[:, n % 2, c, :], ident[:, :])
                            last.then_inc(yt_done.sem, 1)
                            turn_free = [yt_high(ab, n + 1), yt_low(ab, n + 1)]
                        elif kind == "scores":
                            if n == 0:
                                pe.wait_ge(*xq_placed(cb, 12))
                                pe.wait_ge(*xkv_placed(cb, 2))
                            c, g = n // NG, n % NG
                            pe.matmul(bank[:, 0:GN], xq[0:96, g, P * c:P * c + P], xk[0:96, g, :], start=True,
                                      stop=True).then_inc(sc_done.sem, 1)
                            a_free[a_jobs % 2] = [sc_sub(cb, n + 1)]
                        elif kind == "turn probs":
                            pe.wait_ge(*pr_exp(cb, n + 1))
                            for c in range(GC):
                                last = pe.transpose(ps_turn[:, P * c:P * c + P], prob[:, n % 4, P * c:P * c + P],
                                                    ident[:, :])
                            last.then_inc(pr_turned.sem, 1)
                            turn_free = [(pr_kept_a, pr_kept_v)[n % 2](cb, n // 2 + 1)]
                        elif kind == "values":
                            pe.wait_ge(*(pr_kept_a, pr_kept_v)[n % 2](cb, n // 2 + 1))
                            if n % GH == 0 and n:
                                pe.wait_ge(*xo_kept(cb, n // GH))
                            for c in range(GC):
                                last = pe.matmul(ps_xo[:, GV * (n % GH):GV * (n % GH) + GV], probT[:, n % 4, c, :],
                                                 xv[:, n % NG, c, :], start=(c == 0), stop=(c == GC - 1))
                            if n % GH == GH - 1:
                                last.then_inc(xo_done.sem, 1)
                        elif kind == "turn cross":
                            pe.wait_ge(*ln[1][3](cb, n + 1))
                            for k in range(KD):
                                last = pe.transpose(ps_turn[:, P * k:P * k + P], resid[:, n, P * k:P * k + P], ident[:, :])
                            last.then_inc(x2_turned.sem, 1)
                            turn_free = [x2_high(cb, n + 1), x2_low(cb, n + 1)]
                        if kind in ("project", "scores"):
                            a_jobs += 1

            def ffn(fb, ab):
                pe.wait_ge(*x2_high(fb, NT))
                pe.wait_ge(*x2_low(fb, NT))
                for c in range(NT):
                    for k in range(KD):
                        last = three_pass(ps_turn[:, NE * c:NE * c + NE], lambda i: turned[:, i, k, P * c:P * c + P],
                                          lambda j: w_gate[:, j, k, :], k == 0, k == KD - 1)
                last.then_inc(gl_done.sem, 1)
                for e in range(EXPERTS + 2):
                    if e < EXPERTS:
                        pe.wait_ge(*gw_loaded[e % 2](fb, e // 2 + 1))
                        for half, (banks, free, done) in enumerate((((ps_a[0], ps_qf), silu, g_done),
                                                                    ((ps_a[1], ps_kf), hid_ready, u_done))):
                            if e >= 2:
                                pe.wait_ge(*free(fb, e - 1))
                            for k in range(KD):
                                cols = slice(D * half + P * k, D * half + P * k + P)
                                last = three_pass(banks[e % 2][:, :], lambda i: gu_w[:, e % 2, i, cols],
                                                  lambda j: turned[:, j, k, :], k == 0, k == KD - 1)
                            last.then_inc(done.sem, 1)
                    if e >= 2:
                        d = e - 2
                        pe.wait_ge(*dw_loaded[d % 4](fb, d // 4 + 1))
                        pe.wait_ge(*h_high(fb, d + 1))
                        pe.wait_ge(*h_low(fb, d + 1))
                        for half in range(2):
                            bank = ((ps_att, ps_so), (ps_turn, ps_xo))[d % 2][half]
                            if d >= 2:
                                pe.wait_ge(*summed(fb, 2 * (d - 2) + half + 1))
                            if d == 0 and ab is not None:
                                pe.wait_ge(*(att_kept, o_kept)[half](ab, H))
                            if d == 1:
                                pe.wait_ge(*(gl_exp(fb, 1), xo_kept(fb, 2 * NT))[half])
                            for t in range(2):
                                c = 2 * half + t
                                last = three_pass(bank[:, D * t:D * t + D], lambda i: hT[:, d % 3, i, P * c:P * c + P],
                                                  lambda j: down_w[:, d % 4, j, :])
                            last.then_inc(down_done.sem, 1)

            def tail(ab, fb):
                pe.wait_ge(*yt_high(ab, PAIRS))
                pe.wait_ge(*yt_low(ab, PAIRS))
                if fb is None:
                    pe.wait_ge(*w_low(0, QKV_PIECES + 3))
                for c in range(NT):
                    bank = (ps_a[0], ps_a[1], ps_qf, ps_kf)[c]
                    for p in range(PAIRS):
                        last = three_pass(bank[:, 0:D], lambda i: yT[:, i, p, P * c:P * c + P],
                                          lambda j: w_o[:, j, p, :], p == 0, p == PAIRS - 1)
                    last.then_inc(wo_done.sem, 1)
                if fb is not None:
                    pe.wait_ge(*summed(fb, 2 * EXPERTS))
                for c in range(NT):
                    bank = (ps_att, ps_so, ps_turn, ps_xo)[c]
                    pe.wait_ge(*ln[0][3](ab, c + 1))
                    for k in range(KD):
                        last = pe.transpose(bank[:, P * k:P * k + P], resid[:, c, P * k:P * k + P], ident[:, :])
                    last.then_inc(x1_turned.sem, 1)
                pe.wait_ge(*x1_high(ab, NT))
                pe.wait_ge(*x1_low(ab, NT))
                for m in range(KD):
                    for k in range(KD):
                        last = three_pass(ps_a[m][:, :], lambda i: w_xq[:, i, k, P * m:P * m + P],
                                          lambda j: turned[:, j, k, :], k == 0, k == KD - 1)
                    last.then_inc(xq_done.sem, 1)

            shared(0, None)
            tail(0, None)
            with pe.Fori(0, NBLK - 1) as i:
                shared(i + 1, i)
                ffn(i, i + 1)
                tail(i + 1, i)
            shared(None, NBLK - 1)
            ffn(NBLK - 1, None)


def kernel(x, ctx_1024, L0_attn_Wq, L0_attn_Wk, L0_attn_Wv, L0_attn_Wo, L0_attn_W_feat, L0_xattn_Wq, L0_xattn_Wk,
           L0_xattn_Wv, L0_xattn_lambda_q1, L0_xattn_lambda_q2, L0_xattn_lambda_k1, L0_xattn_lambda_k2,
           L0_ffn_gate_w, L0_ffn_e_bias, L0_ffn_gate_proj, L0_ffn_up_proj, L0_ffn_down_proj,
           L0_ffn_shared_gate_w, L0_ffn_shared_up_w, L0_ffn_shared_down_w):
    import concourse.bacc as bacc
    from concourse.bass_utils import run_bass_kernel_spmd

    def by_rows(w):
        w = np.swapaxes(np.asarray(w), -1, -2)
        w = w.reshape(*w.shape[:-2], KD, P, w.shape[-1])
        return np.swapaxes(w, -3, -2).reshape(*w.shape[:-3], P, -1)

    def with_shared(shared, experts):
        return np.concatenate([np.asarray(shared)[None], np.asarray(experts)], 0)

    gate = by_rows(with_shared(L0_ffn_shared_gate_w, L0_ffn_gate_proj))
    up = by_rows(with_shared(L0_ffn_shared_up_w, L0_ffn_up_proj))
    down = np.swapaxes(with_shared(L0_ffn_shared_down_w, L0_ffn_down_proj), 1, 2)
    tokens = np.asarray(x).reshape(B * S, D)
    arrays = {
        "x": tokens.reshape(NBLK, NT, P, D).transpose(2, 0, 1, 3),
        "xT": tokens.T.reshape(KD, P, B * S).transpose(1, 0, 2),
        "ctxT": np.asarray(ctx_1024).reshape(B * CTX, D).T,
        "wq": L0_attn_Wq, "wk": L0_attn_Wk, "wv": L0_attn_Wv, "wo": L0_attn_Wo, "wfeat": L0_attn_W_feat,
        "xwqT": np.asarray(L0_xattn_Wq).T, "xwkT": np.asarray(L0_xattn_Wk).T, "xwvT": np.asarray(L0_xattn_Wv).T,
        "lam_q1": L0_xattn_lambda_q1, "lam_q2": L0_xattn_lambda_q2,
        "lam_k1": L0_xattn_lambda_k1, "lam_k2": L0_xattn_lambda_k2,
        "gate_wT": np.asarray(L0_ffn_gate_w).T, "e_bias": L0_ffn_e_bias,
        "ffn_w": np.concatenate([gate, up, down], -1),
    }
    arrays = {name: np.ascontiguousarray(a) for name, a in arrays.items()}
    nc = bacc.Bacc("TRN2", target_bir_lowering=False, num_devices=1)
    args = {name: nc.dram_tensor(name, a.shape, mybir.dt.from_np(a.dtype), kind="ExternalInput").ap()
            for name, a in arrays.items()}
    args["out"] = nc.dram_tensor("out", (P, NBLK, NT, D), F32, kind="ExternalOutput").ap()
    decoder_layer(nc, **args)
    got = run_bass_kernel_spmd(nc, [arrays], core_ids=[0]).results[0]["out"]
    return np.asarray(got).transpose(1, 2, 0, 3).reshape(B, S, D)
```

```python
from contextlib import ExitStack

import numpy as np

import concourse.bass as bass
from concourse import mybir

ALU = mybir.AluOpType
ACT = mybir.ActivationFunctionType
AX = mybir.AxisListType
F32 = mybir.dt.float32
F16 = mybir.dt.float16
I32 = mybir.dt.int32

P = 128
B, S, D = 2, 1024, 256
CTX = 77
H, HD, NF = 16, 64, 128
PAIRS = H // 2
XHALVES, XD = 32, 8
XV = 16
NE, INTER, NGROUP, PER_GROUP, TOPK_GROUP, TOPK = 16, 128, 4, 4, 2, 4
SCALING = 2.5
LN_EPS = 1e-5
EPS = 1e-6 * NF
LAMBDA_INIT = 0.8
W_SCALE = 64.0

TB = 512
NT = TB // P
NBLK = B * S // TB
BLK_PER_BATCH = S // TB
KD = D // P
V1 = HD + 1
GH = 4
NG = XHALVES // GH
GN = GH * CTX
GC = 3
CHUNKS = NG * GC
RING = 2 * GC
MAX_SCALE = 64.0
GV = GH * (XV + 1)
EXPERTS = NE + 1
FW = 2 * D + D
ROUTE_STEPS = 28
ROOT_STEPS = 12
LAST = 18


def opening(attn, cross):
    jobs = []
    for v in range(2 * NT):
        if attn:
            jobs.append(("values", v))
        if cross and v:
            jobs += [("scores", n) for n in range(5 * (v - 1), min(5 * v, NT * NG))]
    return jobs


def steps(s, attn, cross):
    jobs = []

    def add(on, kind, n, count):
        if on and 0 <= n < count:
            jobs.append((kind, n))

    if s == 0:
        add(attn, "project", 0, H)
        add(attn, "project", 1, H)
    add(attn, "project", s + 2, H)
    if s == 0:
        add(cross, "turn maxima", 0, 1)
    add(attn, "turn keys", s - 1, H)
    add(attn, "q features", s, H)
    add(cross, "probs", 2 * s - 2, CHUNKS)
    add(attn, "state", s - 2, H)
    add(attn, "attend", s - 1, H)
    add(attn, "k features", s, H)
    add(cross, "probs", 2 * s - 1, CHUNKS)
    add(attn, "output", s - 3, H)
    for m in range(2 * NG):
        if s == 3 + 3 * m // 4:
            add(cross, "weigh", m, 2 * NG)
    if s % 2 == 1:
        add(attn, "turn output", (s - 5) // 2, PAIRS)
    if s == 15:
        add(cross, "norm", 0, 1)
    if s >= 16:
        add(cross, "turn cross", 2 * s - 32, NT)
        add(cross, "turn cross", 2 * s - 31, NT)
    return jobs


def late_jobs(e):
    return {0: [("output", H - 1)], 1: [("turn output", PAIRS - 1)]}.get(e, [])


def tail_jobs(e):
    if e is None:
        return [job for e in range(EXPERTS) for job in late_jobs(e) + tail_jobs(e)]
    if 3 <= e < 3 + NT:
        return [("project out", e - 3)] + ([("norm", 0)] if e == 2 + NT else [])
    return {8: [("turn stream", 0)], 10: [("turn stream", 1)],
            12: [("queries", 0)], 13: [("queries", 1)], 14: [("split", 0)]}.get(e, [])


class Signal:

    def __init__(self, sem, per, unit):
        self.sem, self.per, self.unit = sem, per, unit

    def __call__(self, block, n):
        return self.sem, (block * self.per + n) * self.unit


def decoder_layer(nc, x, xT, ctxT, wq, wk, wv, wo, wfeat, xwqT, xwkT, xwvT, lam_q1, lam_q2, lam_k1,
                  lam_k2, gate_wT, e_bias, ffn_w, out):
    with ExitStack() as stack:
        def sb(name, shape, dt=F32):
            return stack.enter_context(nc.sbuf_tensor(name, shape, dt))

        def signal(name, per=1, unit=1):
            return Signal(stack.enter_context(nc.semaphore(name)), per, unit)

        w_q = sb("w_q", [P, 2, KD, H * HD], F16)
        w_k = sb("w_k", [P, 2, KD, H * HD], F16)
        w_v = sb("w_v", [P, 2, KD, H * HD], F16)
        w_o = sb("w_o", [P, 2, PAIRS, D], F16)
        w_xq = sb("w_xq", [P, 2, KD, D], F16)
        w_gate = sb("w_gate", [P, 2, KD, NE], F16)
        w_feat = sb("w_feat", [P, 2, 2, NF], F16)
        neg_half = sb("neg_half", [P, 2, NF], F16)
        ident = sb("ident", [P, P])
        causal = sb("causal", [P, P])
        before_e = sb("before_e", [P, NE, NE], F16)
        before_g = sb("before_g", [P, NGROUP, NGROUP], F16)
        bias = sb("bias", [P, NE])
        lam_in = sb("lam_in", [P, 4, XD])
        lam_prod = sb("lam_prod", [P, 2, XD])
        lam_sum = sb("lam_sum", [P, 2])
        lam_exp = sb("lam_exp", [P, 2])
        coef = sb("coef", [P, 2 * XV // 2, 1])
        x_stage = sb("x_stage", [P, KD, TB])
        x_split = sb("x_split", [P, 2, KD, TB], F16)
        resid = sb("resid", [P, NT, D])
        nxt = sb("nxt", [P, NT, D])
        turned = sb("turned", [P, 2, KD, TB], F16)
        turned_next = x_split
        qk = sb("qk", [P, 2, 2, 4, TB], F16)
        square = sb("square", [P, 2, TB])
        v1 = sb("v1", [P, NT, H, V1])
        qf = sb("qf", [P, 4, TB])
        kf = sb("kf", [P, 2, TB])
        kt = sb("kt", [P, 2, NT, NF])
        att = sb("att", [P, 3, NT, P])
        state = sb("state", [P, H, V1])
        keep = sb("keep", [P, 1])
        run = sb("run", [P, 2, NT, V1])
        den = sb("den", [P, 2, NT, 1])
        rec = sb("rec", [P, 2, NT, 1])
        y = sb("y", [P, 2, NT, P])
        yT = sb("yT", [P, 2, PAIRS, TB], F16)
        xq_hl = sb("xq_hl", [P, 2, KD, TB], F16)
        xq = sb("xq", [P, NG, TB], F16)
        xk = sb("xk", [P, NG, GC * P], F16)
        xv = sb("xv", [P, NG, GC, 2, GV], F16)
        xmax = sb("xmax", [P, NT, XHALVES])
        prob = sb("prob", [P, RING, 2, TB], F16)
        xrec = sb("xrec", [P, 2, XHALVES // 2, 1])
        xrec2 = sb("xrec2", [P, 2, XHALVES // 2, 1])
        xterm = sb("xterm", [P, 2, XHALVES // 4, 2, XV])
        xsum = sb("xsum", [P, 2, XHALVES // 4, XV])
        st = sb("st", [P, NT, 6])
        mv = sb("mv", [P, NT, 2])
        rstd = sb("rstd", [P, NT, 1])
        root_v = sb("root_v", [P, NT, 1])
        root_a = sb("root_a", [P, NT, 1])
        ffn_mem = sb("ffn_mem", [P, 3072])
        hT = sb("hT", [P, 3, 2, TB], F16)
        ge = sb("ge", [P, NT * NE])
        gd = sb("gd", [P, NT * NE])
        score = sb("score", [P, NT, NE])
        choice = sb("choice", [P, NT, NE])
        g_max = sb("g_max", [P, NT * NGROUP, 2])
        g_min = sb("g_min", [P, NT * NGROUP, 2])
        g_a = sb("g_a", [P, NT * NGROUP])
        g_b = sb("g_b", [P, NT * NGROUP])
        g_c = sb("g_c", [P, NT * NGROUP])
        g_d = sb("g_d", [P, NT * NGROUP])
        g_sum = sb("g_sum", [P, NT, NGROUP])
        g_gt = sb("g_gt", [P, NT, NGROUP, NGROUP], F16)
        g_eq = sb("g_eq", [P, NT, NGROUP, NGROUP], F16)
        g_rank = sb("g_rank", [P, NT * NGROUP])
        g_in = sb("g_in", [P, NT * NGROUP, 1])
        masked = sb("masked", [P, NT, NE])
        e_gt = sb("e_gt", [P, NT, NE * NE], F16)
        e_eq = sb("e_eq", [P, NT, NE * NE], F16)
        e_rank = sb("e_rank", [P, NT * NE])
        e_in = sb("e_in", [P, NT * NE])
        chosen = sb("chosen", [P, NT, NE])
        w_sum = sb("w_sum", [P, NT])
        w_rec = sb("w_rec", [P, NT])
        w_rec2 = sb("w_rec2", [P, NT, 1])
        weight = sb("weight", [P, NT, NE])

        gu_w = ffn_mem[:, 0:1024].bitcast(F16).rearrange("p (r a c) -> p r a c", r=2, a=2)
        down_w = ffn_mem[:, 1024:2048].bitcast(F16).rearrange("p (r a c) -> p r a c", r=4, a=2)
        hid = ffn_mem[:, 2048:3072].rearrange("p (r t) -> p r t", r=2)
        prob_full = hid
        fs_in = ffn_mem[:, 0:1536].rearrange("p (r c) -> p r c", r=2)
        fs_out = ffn_mem[:, 1536:3072].bitcast(F16).rearrange("p (r a c) -> p r a c", r=2, a=2)
        prob_mem = prob[:, :, :, :].rearrange("p r a t -> p (r a t)").bitcast(F32)
        w_stage = xq[:, :, :].rearrange("p g t -> p (g t)").bitcast(F32).rearrange("p (r c) -> p r c", r=2)
        ctx_mem = prob_mem[:, 4 * GN:]
        xwk_sb = ctx_mem[:, 0:512].rearrange("p (k n) -> p k n", k=KD)
        xwv_sb = ctx_mem[:, 512:1024].rearrange("p (k n) -> p k n", k=KD)
        ctx_sb = ctx_mem[:, 1024:1024 + KD * B * CTX].rearrange("p (k n) -> p k n", k=KD)
        kb_hl = prob_mem[:, 0:4 * GN].bitcast(F16).rearrange("p (n a c) -> p n a c", n=2 * B, a=2)
        nxt_mem = nxt[:, :, :].rearrange("p t d -> p (t d)")
        VEXT = B * XV * (XV + 1)
        v_ext = nxt_mem[:, 0:VEXT].bitcast(F16).rearrange("p (a b h d) -> p a b h d", a=2, b=B, h=XV)
        kb_full = nxt_mem[:, VEXT:VEXT + GN].rearrange("p (j n) -> p j n", j=GH)
        own_half = sb("own_half", [P, P // XD])
        own_row = sb("own_row", [P, GH, 1])

        def psum(name):
            return stack.enter_context(nc.psum_tensor(name, [P, 512], F32))

        ps_a = [psum("ps_a0"), psum("ps_a1")]
        ps_qf, ps_kf = psum("ps_qf"), psum("ps_kf")
        ps_att = psum("ps_att")
        ps_turn = psum("ps_turn")
        ps_so = psum("ps_so")
        ps_xo = psum("ps_xo")

        score_banks = (ps_qf, ps_kf, ps_att, ps_so)

        def ring_banks(ab):
            return (ps_a[0], ps_a[1]) if ab is not None else (ps_a[0], ps_a[1], ps_qf, ps_kf)

        def tail_bank(kind, n, alone):
            if not alone:
                return ps_xo
            return {"project out": (ps_a[0], ps_a[1], ps_qf, ps_kf), "turn stream": (ps_att, ps_so),
                    "queries": (ps_turn, ps_xo)}[kind][n]

        def stream_cols(j):
            return slice(2 * P * j, 2 * P * (j + 1))

        down_banks = (ps_att, ps_so, ps_turn)

        def weigh_bank(ab, g):
            return ps_xo if ab is not None or g % 2 == 0 else ps_so

        ffn_scr = nc.dram_tensor("ffn_split", [EXPERTS, P, 2, FW], F16, kind="Internal").ap()
        xk_scr = nc.dram_tensor("xk_blocks", [B, 96, NG, GN], F16, kind="Internal").ap()
        xv_scr = nc.dram_tensor("xv_blocks", [B, P, NG, GC, 2, GV], F16, kind="Internal").ap()

        consts = signal("consts", 4)
        own_ready = signal("own_ready"); v_ones = signal("v_ones"); zeros_v = signal("zeros_v")
        c_loaded = signal("c_loaded", 1, 16)
        ctx_loaded = signal("ctx_loaded", 1, 16)
        w_loaded = [signal("w_loaded0", 1, 16), signal("w_loaded1", 1, 16)]
        w_high = signal("w_high"); w_low = signal("w_low")
        xkv_done = signal("xkv_done"); kb_copied = signal("kb_copied"); kb_masked = signal("kb_masked")
        kb_high = signal("kb_high"); kb_low = signal("kb_low"); v_copied = signal("v_copied")
        lam_step = signal("lam_step"); lam_exped = signal("lam_exped"); coef_ready = signal("coef_ready")
        zero_stored = signal("zero_stored", 1, 16); ctx_stored = signal("ctx_stored", 1, 16)
        fs_loaded = [signal("fs_loaded0", 1, 16), signal("fs_loaded1", 1, 16)]
        fs_high = signal("fs_high"); fs_low = signal("fs_low")
        fs_stored = [signal("fs_stored0", 1, 16), signal("fs_stored1", 1, 16)]
        v_done = signal("v_done", 2 * NT); p_done = signal("p_done", H)
        turned_k = signal("turned_k", H); qf_done = signal("qf_done", H); kf_done = signal("kf_done", H)
        st_done = signal("st_done", H); att_done = signal("att_done", H); o_done = signal("o_done", H)
        yt_done = signal("yt_done", PAIRS)
        xs_loaded = signal("xs_loaded", 1, 16)
        x_high = signal("x_high"); x_low = signal("x_low")
        v_kept = signal("v_kept", 2 * NT)
        p_high = signal("p_high", H); p_low = signal("p_low", H); p_sq = signal("p_sq", H)
        p_sqh = signal("p_sqh", H); p_sql = signal("p_sql", H)
        qf_exp = signal("qf_exp", H); kf_exp = signal("kf_exp", H); kt_kept = signal("kt_kept", H)
        att_kept = signal("att_kept", H); run_step = signal("run_step", 4 * H); run_ready = signal("run_ready", H)
        o_den = signal("o_den", H); o_rec = signal("o_rec", H); o_kept = signal("o_kept", H)
        yt_high = signal("yt_high", PAIRS); yt_low = signal("yt_low", PAIRS)
        keep_set = signal("keep_set")
        xq_high = signal("xq_high", KD); xq_low = signal("xq_low", KD); xq_done = signal("xq_done", KD)
        xq_placed = signal("xq_placed", 12, 16); xkv_placed = signal("xkv_placed", 2, 16)
        sc_done = signal("sc_done", NT * NG); sc_max = signal("sc_max", NT * NG)
        mx_turned = signal("mx_turned"); mx_kept = signal("mx_kept"); mx_spread = signal("mx_spread")
        pr_done = signal("pr_done", CHUNKS); pr_exp = signal("pr_exp", CHUNKS)
        pr_high = signal("pr_high", CHUNKS); pr_low = signal("pr_low", CHUNKS)
        xk_const = signal("xk_const"); weighed = signal("weighed", 2 * NG)
        xo_rec = signal("xo_rec", NG); xo_coef = signal("xo_coef", NG)
        xo_kept = signal("xo_kept", NG); xo_sum = signal("xo_sum", NG); xo_added = signal("xo_added", NG)
        ln = [[signal(f"ln{i}_stats", NT), signal(f"ln{i}_mv", NT), signal(f"ln{i}_root", ROOT_STEPS),
               signal(f"ln{i}_out", NT)] for i in range(3)]
        x2_turned = signal("x2_turned", NT); x2_high = signal("x2_high", NT); x2_low = signal("x2_low", NT)
        gl_done = signal("gl_done"); gl_exp = signal("gl_exp"); route = signal("route", ROUTE_STEPS)
        gw_loaded = [signal("gw_loaded0", 9, 16), signal("gw_loaded1", 8, 16)]
        dw_loaded = [signal("dw_loaded0", 5, 16)] + [signal(f"dw_loaded{r}", 4, 16) for r in (1, 2, 3)]
        g_done = signal("g_done", EXPERTS); u_done = signal("u_done", EXPERTS)
        silu = signal("silu", EXPERTS); hid_ready = signal("hid_ready", EXPERTS)
        h_high = signal("h_high", EXPERTS); h_low = signal("h_low", EXPERTS)
        down_done = signal("down_done", 2 * EXPERTS); summed = signal("summed", 2 * EXPERTS)
        out_stored = signal("out_stored", 1, 16)
        xin_loaded = signal("xin_loaded", 1, 16)
        wo_done = signal("wo_done", NT); x1_added = signal("x1_added", NT)
        x1_turned = signal("x1_turned", 2); x1_high = signal("x1_high", 2); x1_low = signal("x1_low", 2)
        resid_set = signal("resid_set")

        def flat(t):
            return t.rearrange("p k n -> p (k n)") if len(t.shape) == 3 else t

        pieces = [(wv[0:P, :], w_v[:, 0, 0, :], w_v[:, 1, 0, :]), (wv[P:D, :], w_v[:, 0, 1, :], w_v[:, 1, 1, :]),
                  (wq[0:P, :], w_q[:, 0, 0, :], w_q[:, 1, 0, :]), (wq[P:D, :], w_q[:, 0, 1, :], w_q[:, 1, 1, :]),
                  (wk[0:P, :], w_k[:, 0, 0, :], w_k[:, 1, 0, :]), (wk[P:D, :], w_k[:, 0, 1, :], w_k[:, 1, 1, :]),
                  None]
        QKV_PIECES = FEAT_PIECE = len(pieces) - 1
        for half in range(2):
            rows = wo.rearrange("(c p) n -> p c n", p=P)[:, 4 * half:4 * half + 4, :]
            pieces.append((rows, w_o[:, 0, 4 * half:4 * half + 4, :], w_o[:, 1, 4 * half:4 * half + 4, :]))
        pieces.append((xwqT.rearrange("(k p) n -> p k n", p=P), w_xq[:, 0, :, :], w_xq[:, 1, :, :]))
        pieces.append((gate_wT.rearrange("(k p) n -> p k n", p=P), w_gate[:, 0, :, :], w_gate[:, 1, :, :]))
        LATE_PIECES = len(pieces) - FEAT_PIECE - 1

        def loads_before(n):
            return n // 2 + 1 + (n >= FEAT_PIECE and n % 2 == FEAT_PIECE % 2)

        def piece_stage(n, like):
            shape = like.shape
            cols = 1
            for d in shape[1:]:
                cols *= d
            v = w_stage[0:shape[0], n % 2, 0:cols]
            return v.rearrange("p (k n) -> p k n", k=shape[1]) if len(shape) == 3 else v

        block = stack.enter_context(nc.Block())

        @block.sync
        def _(sp):
            def load_piece(n):
                if n >= 2:
                    sp.wait_ge(*w_high(0, n - 1))
                    sp.wait_ge(*w_low(0, n - 1))
                if n == FEAT_PIECE:
                    for parity in range(2):
                        rows = slice(HD * parity, HD * parity + HD)
                        sp.dma_start(w_stage[rows, n % 2, 0:NF], wfeat).then_inc(w_loaded[n % 2].sem, 16)
                else:
                    src, high, _ = pieces[n]
                    sp.dma_start(piece_stage(n, high), src).then_inc(w_loaded[n % 2].sem, 16)

            def load_x(ab):
                sp.dma_start(x_stage[:, :, :], xT[:, :, bass.ts(ab, TB)]).then_inc(xs_loaded.sem, 16)

            sp.dma_start(x_stage[:, :, :], xT[:, :, 0:TB]).then_inc(xs_loaded.sem, 16)
            for n in range(4):
                load_piece(n)
            for src, dst in ((ctxT, ctx_sb), (xwkT, xwk_sb), (xwvT, xwv_sb)):
                sp.dma_start(dst, src.rearrange("(k p) n -> p k n", p=P)).then_inc(ctx_loaded.sem, 16)
            for n in range(4, FEAT_PIECE + 1):
                load_piece(n)
            for n, v in enumerate((lam_q1, lam_k1, lam_q2, lam_k2)):
                sp.dma_start(lam_in[:, n, :], v.partition_broadcast(P)).then_inc(c_loaded.sem, 16)
            sp.dma_start(bias[:, :], e_bias.partition_broadcast(P)).then_inc(c_loaded.sem, 16)

            sp.wait_ge(*zeros_v(0, 1))
            for b in range(B):
                sp.dma_start(xv_scr[b], xv[:, :, :, :, :]).then_inc(zero_stored.sem, 16)
            key_parts, value_parts = [], []
            for b in range(B):
                for m in range(KD):
                    for part, row in ((0, 0), (0, 32), (1, 64)):
                        for q in range(4):
                            key_parts.append((xk_scr[b, row:row + 32, 4 * m + q, :],
                                              kb_hl[32 * q:32 * q + 32, KD * b + m, part, :]))
                for j in range(GH):
                    n0 = 0
                    while n0 < CTX:
                        r = CTX * j + n0
                        rows = min(CTX - n0, P - r % P)
                        for part in range(2):
                            value_parts.append((
                                xv_scr[b, r % P:r % P + rows, :, r // P, part, (XV + 1) * j:(XV + 1) * (j + 1)],
                                v_ext[n0:n0 + rows, part, b, :, :].rearrange("n (g i) d -> n g i d", i=2)[:, :, j // 2, :]))
                        n0 += rows
            ctx_parts = key_parts + value_parts
            n_ctx = len(ctx_parts)

            def attention(ab):
                sp.wait_ge(*x_high(ab, 1))
                sp.wait_ge(*x_low(ab, 1))
                load_x((ab + 1) % NBLK)

            def load_tail(ab, fb):
                if fb is not None:
                    sp.wait_ge(*resid_set(fb, 1))
                    sp.dma_start(nxt[:, :, :], x[:, ab, :, :]).then_inc(xin_loaded.sem, 16)
                    sp.wait_ge(*weighed(fb, 2 * NG))
                else:
                    sp.wait_ge(*ctx_stored(0, n_ctx))
                    sp.wait_ge(*xk_const(0, 2))
                    sp.dma_start(nxt[:, :, :], x[:, ab, :, :]).then_inc(xin_loaded.sem, 16)
                sp.dma_start(xk[0:96, :, 0:GN], xk_scr[ab // BLK_PER_BATCH]).then_inc(xkv_placed.sem, 16)
                sp.dma_start(xv[:, :, :, :, :], xv_scr[ab // BLK_PER_BATCH]).then_inc(xkv_placed.sem, 16)

            def place_queries(ab):
                sp.wait_ge(*xq_high(ab, KD))
                sp.wait_ge(*xq_low(ab, KD))
                for part, row in ((0, 0), (1, 32), (0, 64)):
                    for q in range(4):
                        sp.dma_start(xq[row:row + 32, q:NG:4, :], xq_hl[32 * q:32 * q + 32, part, :, :]
                                     ).then_inc(xq_placed.sem, 16)

            def ffn(fb, ab):
                for e in range(EXPERTS):
                    if e >= 2:
                        sp.wait_ge(*u_done(fb, e - 1))
                    sp.dma_start(gu_w[:, e % 2, :, :], ffn_scr[e, :, :, 0:2 * D]).then_inc(gw_loaded[e % 2].sem, 16)
                    if e >= 4:
                        sp.wait_ge(*down_done(fb, 2 * (e - 3)))
                    sp.dma_start(down_w[:, e % 4, :, :], ffn_scr[e, :, :, 2 * D:FW]).then_inc(dw_loaded[e % 4].sem, 16)
                    if e == 1 and ab is not None:
                        load_tail(ab, fb)
                if ab is not None:
                    place_queries(ab)

            def store(fb):
                sp.wait_ge(*ln[2][3](fb, NT))
                sp.dma_start(out[:, fb, :, :], resid[:, :, :]).then_inc(out_stored.sem, 16)

            attention(0)
            for e in range(EXPERTS):
                if e >= 2:
                    sp.wait_ge(*fs_high(0, e - 1))
                    sp.wait_ge(*fs_low(0, e - 1))
                sp.dma_start(fs_in[:, e % 2, :], ffn_w[e]).then_inc(fs_loaded[e % 2].sem, 16)
                if e < LATE_PIECES:
                    load_piece(FEAT_PIECE + 1 + e)
                if e >= 1:
                    sp.wait_ge(*fs_high(0, e))
                    sp.wait_ge(*fs_low(0, e))
                    sp.dma_start(ffn_scr[e - 1], fs_out[:, (e - 1) % 2, :, :]
                                 ).then_inc(fs_stored[(e - 1) % 2].sem, 16)
                if e == 3:
                    sp.wait_ge(*kb_high(0, 2 * B))
                    sp.wait_ge(*kb_low(0, 2 * B))
                    sp.wait_ge(*v_copied(0, 2 * B + 2))
                    sp.wait_ge(*zero_stored(0, B))
                if e >= 3:
                    each = -(-n_ctx // (EXPERTS - 3))
                    for to, part in ctx_parts[each * (e - 3):each * (e - 2)]:
                        sp.dma_start(to, part).then_inc(ctx_stored.sem, 16)
            sp.wait_ge(*fs_high(0, EXPERTS))
            sp.wait_ge(*fs_low(0, EXPERTS))
            sp.dma_start(ffn_scr[EXPERTS - 1], fs_out[:, (EXPERTS - 1) % 2, :, :]
                         ).then_inc(fs_stored[(EXPERTS - 1) % 2].sem, 16)
            sp.wait_ge(*fs_stored[0](0, (EXPERTS + 1) // 2))
            sp.wait_ge(*fs_stored[1](0, EXPERTS // 2))
            load_tail(0, None)
            place_queries(0)
            sp.sem_inc(out_stored.sem, 16)
            with sp.Fori(0, NBLK - 1) as i:
                attention(i + 1)
                ffn(i, i + 1)
                store(i)
            ffn(NBLK - 1, None)
            store(NBLK - 1)
            sp.wait_ge(*xs_loaded(0, NBLK + 1))
            sp.wait_ge(*out_stored(0, NBLK + 1))

        @block.gpsimd
        def _(pool):
            pool.memset(ident[:, :], 0.0).then_inc(consts.sem, 1)
            pool.memset(causal[:, :], 1.0).then_inc(consts.sem, 1)
            pool.memset(before_e[:, :, :], 1.0).then_inc(consts.sem, 1)
            pool.memset(before_g[:, :, :], 1.0).then_inc(consts.sem, 1)
            pool.memset(own_half[:, :], 1.0).then_inc(consts.sem, 1)
            pool.wait_ge(consts.sem, 5)
            pool.affine_select(out=ident[:, :], in_=ident[:, :], compare_op=ALU.not_equal, fill=1.0, base=0,
                               pattern=[[-1, P]], channel_multiplier=1).then_inc(consts.sem, 1)
            pool.affine_select(out=causal[:, :], in_=causal[:, :], compare_op=ALU.is_ge, fill=0.0, base=0,
                               pattern=[[1, P]], channel_multiplier=-1).then_inc(consts.sem, 1)
            pool.affine_select(out=before_e[:, :, :], in_=before_e[:, :, :], compare_op=ALU.is_gt, fill=0.0, base=0,
                               pattern=[[1, NE], [-1, NE]], channel_multiplier=0).then_inc(consts.sem, 1)
            pool.affine_select(out=before_g[:, :, :], in_=before_g[:, :, :], compare_op=ALU.is_gt, fill=0.0, base=0,
                               pattern=[[1, NGROUP], [-1, NGROUP]], channel_multiplier=0).then_inc(consts.sem, 1)
            pool.affine_select(out=own_half[:, :], in_=own_half[:, :], compare_op=ALU.is_ge, fill=0.0, base=0,
                               pattern=[[-XD, P // XD]], channel_multiplier=1).then_inc(consts.sem, 1)
            pool.wait_ge(consts.sem, 10)
            pool.affine_select(out=own_half[:, :], in_=own_half[:, :], compare_op=ALU.is_ge, fill=0.0, base=XD - 1,
                               pattern=[[XD, P // XD]], channel_multiplier=-1).then_inc(consts.sem, 1)

            pool.memset(xk[:, :, :], 0.0).then_inc(xk_const.sem, 1)
            pool.wait_ge(*xk_const(0, 1))
            pool.affine_select(out=xk[:, :, 0:GN].rearrange("p g (j n) -> p g j n", j=GH),
                               in_=xk[:, :, 0:GN].rearrange("p g (j n) -> p g j n", j=GH),
                               compare_op=ALU.not_equal, fill=-MAX_SCALE, base=-96,
                               pattern=[[-GH, NG], [-1, GH], [0, CTX]], channel_multiplier=1).then_inc(xk_const.sem, 1)

            def shared(ab, cb):
                for s in range(LAST):
                    for kind, n in steps(s, ab is not None, cb is not None):
                        if kind == "project":
                            pool.wait_ge(*p_sqh(ab, n + 1))
                            pool.tensor_tensor(qk[:, n % 2, n // 2 % 2, 3, :], square[:, n % 2, :],
                                               qk[:, n % 2, n // 2 % 2, 2, :], ALU.subtract).then_inc(p_sql.sem, 1)
                        elif kind == "probs":
                            pool.wait_ge(*pr_exp(cb, n + 1))
                            pool.tensor_tensor(prob[:, n % RING, 1, :], prob_full[:, n % 2, :], prob[:, n % RING, 0, :],
                                               ALU.subtract).then_inc(pr_low.sem, 1)
                        elif kind == "weigh" and n % 2 == 1:
                            g = n // 2
                            if g == 0:
                                pool.wait_ge(*resid_set(cb, 1))
                            pool.wait_ge(*xo_kept(cb, g + 1))
                            pool.tensor_tensor(xsum[:, g % 2, :, :], xterm[:, g % 2, :, 0, :],
                                               xterm[:, g % 2, :, 1, :], ALU.add).then_inc(xo_sum.sem, 1)
                            pool.wait_ge(*xo_sum(cb, g + 1))
                            cols = slice(32 * g, 32 * g + 32)
                            pool.tensor_tensor(resid[:, :, cols], resid[:, :, cols],
                                               xsum[:, g % 2, :, :].rearrange("p (c h) d -> p c (h d)", c=NT),
                                               ALU.add).then_inc(xo_added.sem, 1)

            def ffn(fb):
                for e in range(EXPERTS):
                    pool.wait_ge(*h_high(fb, e + 1))
                    pool.tensor_tensor(hT[:, e % 3, 1, :], hid[:, e % 2, :], hT[:, e % 3, 0, :],
                                       ALU.subtract).then_inc(h_low.sem, 1)

            shared(0, None)
            with pool.Fori(0, NBLK - 1) as i:
                shared(i + 1, i)
                ffn(i)
            shared(None, NBLK - 1)
            ffn(NBLK - 1)

        @block.scalar
        def _(act):
            def keep_values(n, ab):
                act.wait_ge(*v_done(ab, n + 1))
                act.activation(v1[:, n // 2, H // 2 * (n % 2):H // 2 * (n % 2 + 1), 0:HD],
                               ps_a[n % 2][:, :].rearrange("p (h d) -> p h d", d=HD), ACT.Copy,
                               scale=1 / W_SCALE).then_inc(v_kept.sem, 1)

            def split_piece(n):
                act.wait_ge(*w_loaded[n % 2](0, loads_before(n)))
                if n == FEAT_PIECE:
                    act.wait_ge(*zeros_v(0, 2))
                    for parity in range(2):
                        rows = slice(HD * parity, HD * parity + HD)
                        last = act.activation(w_feat[rows, parity, 0, :], w_stage[rows, n % 2, 0:NF], ACT.Copy)
                    last.then_inc(w_high.sem, 1)
                else:
                    act.activation(pieces[n][1], piece_stage(n, pieces[n][1]), ACT.Copy,
                                   scale=W_SCALE).then_inc(w_high.sem, 1)

            for n in range(2):
                split_piece(n)
            for n in range(2, QKV_PIECES + 1):
                keep_values(n - 2, 0)
                split_piece(n)
            for n in range(QKV_PIECES - 1, 2 * NT):
                keep_values(n, 0)

            def turn_output_job(n, ab):
                act.wait_ge(*yt_done(ab, n + 1))
                act.activation(yT[:, 0, n, :], ps_turn[:, :], ACT.Copy).then_inc(yt_high.sem, 1)

            def shared(ab, cb):
                for kind, n in opening(ab is not None, cb is not None) if cb is not None else []:
                    if kind == "values":
                        keep_values(n, ab)
                ring = ring_banks(ab)
                a_jobs = 0
                for s in range(LAST):
                    for kind, n in steps(s, ab is not None, cb is not None):
                        if kind == "project":
                            bank = ring[a_jobs % len(ring)]
                            act.wait_ge(*p_done(ab, n + 1))
                            act.activation(qk[:, n % 2, n // 2 % 2, 0, :], bank[:, :], ACT.Copy,
                                           scale=1 / W_SCALE).then_inc(p_high.sem, 1)
                            if n >= 2:
                                act.wait_ge(*p_sql(ab, n - 1))
                            act.activation(square[:, n % 2, :], bank[:, :], ACT.Square,
                                           scale=1 / W_SCALE).then_inc(p_sq.sem, 1)
                        elif kind == "turn keys":
                            act.wait_ge(*turned_k(ab, n + 1))
                            act.activation(kt[:, n % 2, :, :].rearrange("p c f -> p (c f)"), ps_turn[:, :],
                                           ACT.Copy).then_inc(kt_kept.sem, 1)
                        elif kind == "q features":
                            act.wait_ge(*qf_done(ab, n + 1))
                            act.activation(qf[:, n % 4, :], ps_qf[:, :], ACT.Exp).then_inc(qf_exp.sem, 1)
                        elif kind == "k features":
                            act.wait_ge(*kf_done(ab, n + 1))
                            act.activation(kf[:, n % 2, :], ps_kf[:, :], ACT.Exp).then_inc(kf_exp.sem, 1)
                        elif kind == "turn maxima":
                            act.wait_ge(*out_stored(cb, 1))
                            act.activation(resid[:, :, :], nxt[:, :, :], ACT.Copy).then_inc(resid_set.sem, 1)
                        elif kind == "probs":
                            act.wait_ge(*pr_done(cb, n + 1))
                            if n >= RING:
                                act.wait_ge(*weighed(cb, 2 * (n // GC - 1)))
                            bank = ring[a_jobs % len(ring)]
                            act.activation(prob[:, n % RING, 0, :], bank[:, :], ACT.Exp,
                                           scale=float(XD) ** -0.5).then_inc(pr_high.sem, 1)
                            if n >= 2:
                                act.wait_ge(*pr_low(cb, n - 1))
                            act.activation(prob_full[:, n % 2, :], bank[:, :], ACT.Exp,
                                           scale=float(XD) ** -0.5).then_inc(pr_exp.sem, 1)
                        elif kind == "turn output":
                            turn_output_job(n, ab)
                        elif kind == "turn cross":
                            act.wait_ge(*x2_turned(cb, n + 1))
                            act.activation(turned[:, 0, :, P * n:P * n + P],
                                           ps_turn[:, 0:D].rearrange("p (k t) -> p k t", k=KD),
                                           ACT.Copy).then_inc(x2_high.sem, 1)
                        if kind in ("project", "probs"):
                            a_jobs += 1
                    if cb is None:
                        if 1 <= s < 1 + LATE_PIECES:
                            split_piece(QKV_PIECES + s)
                        if s == 1 + LATE_PIECES:
                            act.wait_ge(*lam_step(0, 2))
                            act.activation(lam_exp[:, :], lam_sum[:, :], ACT.Exp).then_inc(lam_exped.sem, 1)
                        if 1 <= s <= EXPERTS:
                            e = s - 1
                            act.wait_ge(*fs_loaded[e % 2](0, e // 2 + 1))
                            if e >= 2:
                                act.wait_ge(*fs_stored[e % 2](0, e // 2))
                            act.activation(fs_out[:, e % 2, 0, :], fs_in[:, e % 2, :], ACT.Copy,
                                           scale=W_SCALE).then_inc(fs_high.sem, 1)

            def ffn(fb, ab):
                act.wait_ge(*gl_done(fb, 1))
                act.activation(ge[:, :], ps_turn[:, 0:NT * NE], ACT.Exp, scale=-1 / W_SCALE).then_inc(gl_exp.sem, 1)
                for e in range(EXPERTS + 1):
                    if e < EXPERTS:
                        act.wait_ge(*g_done(fb, e + 1))
                        if e >= 2:
                            act.wait_ge(*h_low(fb, e - 1))
                        act.activation(hid[:, e % 2, :], (ps_a[0], ps_qf)[e % 2][:, :], ACT.Silu,
                                       scale=1 / W_SCALE).then_inc(silu.sem, 1)
                    if e >= 1:
                        act.wait_ge(*hid_ready(fb, e))
                        if e >= 4:
                            act.wait_ge(*down_done(fb, 2 * (e - 3)))
                        act.activation(hT[:, (e - 1) % 3, 0, :], hid[:, (e - 1) % 2, :],
                                       ACT.Copy).then_inc(h_high.sem, 1)
                    if ab is not None:
                        for kind, n in late_jobs(e) + tail_jobs(e):
                            tail_job(kind, n, ab, False)

            def tail_job(kind, n, ab, alone):
                if kind == "turn output":
                    turn_output_job(n, ab)
                elif kind == "turn stream":
                    act.wait_ge(*x1_turned(ab, n + 1))
                    act.activation(turned_next[:, 0, :, stream_cols(n)],
                                   tail_bank(kind, n, alone)[:, :].rearrange("p (k t) -> p k t", k=KD),
                                   ACT.Copy).then_inc(x1_high.sem, 1)
                elif kind == "queries":
                    act.wait_ge(*xq_done(ab, n + 1))
                    act.activation(xq_hl[:, 0, n, :], tail_bank(kind, n, alone)[:, :], ACT.Copy,
                                   scale=1 / W_SCALE).then_inc(xq_high.sem, 1)

            shared(0, None)
            for kind, n in tail_jobs(None):
                tail_job(kind, n, 0, True)
            with act.Fori(0, NBLK - 1) as i:
                shared(i + 1, i)
                ffn(i, i + 1)
            shared(None, NBLK - 1)
            ffn(NBLK - 1, None)

        @block.vector
        def _(dve):
            dve.memset(xv[:, :, :, :, :], 0.0).then_inc(zeros_v.sem, 1)
            dve.memset(w_feat[:, :, :, :], 0.0).then_inc(zeros_v.sem, 1)
            dve.memset(neg_half[:, :, :], 0.0).then_inc(v_ones.sem, 1)
            dve.memset(v1[:, :, :, HD:V1], 1.0).then_inc(v_ones.sem, 1)
            dve.memset(state[:, :, :], 0.0).then_inc(v_ones.sem, 1)
            dve.memset(keep[:, :], 0.0).then_inc(v_ones.sem, 1)
            dve.memset(coef[:, :, :], 1.0).then_inc(v_ones.sem, 1)
            dve.wait_ge(*v_ones(0, 5))
            for parity in range(2):
                dve.memset(neg_half[HD * parity:HD * parity + HD, parity, :], -0.5).then_inc(v_ones.sem, 1)

            def split_x(ab):
                dve.wait_ge(*xs_loaded(ab, 1))
                dve.tensor_copy(x_split[:, 0, :, :], x_stage[:, :, :]).then_inc(x_high.sem, 1)
                dve.wait_ge(*x_high(ab, 1))
                dve.tensor_tensor(x_split[:, 1, :, :], x_stage[:, :, :], x_split[:, 0, :, :],
                                  ALU.subtract).then_inc(x_low.sem, 1)

            def split_low(n):
                _, high, low = pieces[n]
                dve.wait_ge(*w_high(0, n + 1))
                dve.scalar_tensor_tensor(low, piece_stage(n, high), W_SCALE, high, ALU.mult,
                                         ALU.subtract).then_inc(w_low.sem, 1)

            def setup_step(s):
                if s == 0:
                    dve.memset(v_ext[0:CTX, 0, :, :, XV:XV + 1], 1.0).then_inc(v_copied.sem, 1)
                    dve.memset(v_ext[0:CTX, 1, :, :, XV:XV + 1], 0.0).then_inc(v_copied.sem, 1)
                    dve.wait_ge(*xkv_done(0, 1))
                    for b in range(B):
                        v_full = ps_so[0:CTX, D * b:D * b + D].rearrange("p (h d) -> p h d", d=XV)
                        dve.tensor_copy(v_ext[0:CTX, 0, b, :, 0:XV], v_full).then_inc(v_copied.sem, 1)
                        dve.wait_ge(*v_copied(0, 2 * b + 3))
                        dve.tensor_tensor(v_ext[0:CTX, 1, b, :, 0:XV], v_full, v_ext[0:CTX, 0, b, :, 0:XV],
                                          ALU.subtract).then_inc(v_copied.sem, 1)
                    dve.wait_ge(consts.sem, 11)
                    dve.tensor_reduce(own_row[:, :, 0], own_half[:, :].rearrange("p (q j) -> p j q", j=GH), AX.X,
                                      ALU.add).then_inc(own_ready.sem, 1)
                    dve.wait_ge(*own_ready(0, 1))
                if s in (1, 2):
                    for n in (2 * s - 2, 2 * s - 1):
                        if n:
                            dve.wait_ge(*kb_low(0, n))
                        dve.tensor_tensor(kb_full, ps_xo[:, CTX * n:CTX * n + CTX].unsqueeze(1).to_broadcast([P, GH, CTX]),
                                          own_row[:, :, :].to_broadcast([P, GH, CTX]), ALU.mult).then_inc(kb_masked.sem, 1)
                        dve.wait_ge(*kb_masked(0, n + 1))
                        flat_full = kb_full.rearrange("p j n -> p (j n)")
                        dve.tensor_copy(kb_hl[:, n, 0, :], flat_full).then_inc(kb_high.sem, 1)
                        dve.wait_ge(*kb_high(0, n + 1))
                        dve.tensor_tensor(kb_hl[:, n, 1, :], flat_full, kb_hl[:, n, 0, :],
                                          ALU.subtract).then_inc(kb_low.sem, 1)
                if 1 <= s < 1 + LATE_PIECES:
                    split_low(QKV_PIECES + s)
                if s == LATE_PIECES:
                    dve.wait_ge(*c_loaded(0, 5))
                    dve.tensor_tensor(lam_prod[:, :, :], lam_in[:, 0:4:2, :], lam_in[:, 1:4:2, :], ALU.mult
                                      ).then_inc(lam_step.sem, 1)
                    dve.wait_ge(*lam_step(0, 1))
                    dve.tensor_reduce(lam_sum[:, :], lam_prod[:, :, :], AX.X, ALU.add).then_inc(lam_step.sem, 1)
                if s == 2 + LATE_PIECES:
                    dve.wait_ge(*lam_exped(0, 1))
                    dve.tensor_tensor(lam_sum[:, 0:1], lam_exp[:, 1:2], lam_exp[:, 0:1], ALU.subtract
                                      ).then_inc(lam_step.sem, 1)
                    dve.wait_ge(*lam_step(0, 3))
                    dve.tensor_scalar(coef[:, 1:XV:2, 0], lam_sum[:, 0:1].to_broadcast([P, XV // 2]), -LAMBDA_INIT,
                                      None, ALU.add).then_inc(coef_ready.sem, 1)
                if 1 <= s <= EXPERTS:
                    e = s - 1
                    dve.wait_ge(*fs_high(0, e + 1))
                    dve.scalar_tensor_tensor(fs_out[:, e % 2, 1, :], fs_in[:, e % 2, :], W_SCALE,
                                             fs_out[:, e % 2, 0, :], ALU.mult, ALU.subtract).then_inc(fs_low.sem, 1)

            split_x(0)
            for n in range(QKV_PIECES):
                split_low(n)
            dve.wait_ge(*w_high(0, FEAT_PIECE + 1))
            for parity in range(2):
                rows = slice(HD * parity, HD * parity + HD)
                last = dve.tensor_tensor(w_feat[rows, parity, 1, :], w_stage[rows, FEAT_PIECE % 2, 0:NF],
                                         w_feat[rows, parity, 0, :], ALU.subtract)
            last.then_inc(w_low.sem, 1)

            def statistics(which, blk, c, stream):
                stats, mean_var = ln[which][:2]
                dve.bn_stats(st[:, c, :], stream[:, c, :]).then_inc(stats.sem, 1)
                dve.wait_ge(*stats(blk, c + 1))
                dve.sem_inc(held.sem, 1)
                dve.bn_aggr(mv[:, c, :], st[:, c, :]).then_inc(mean_var.sem, 1)

            def inverse_root(which, blk):
                step = ln[which][2]
                n = [0]

                def link(ins):
                    n[0] += 1
                    ins.then_inc(step.sem, 1)
                    dve.wait_ge(*step(blk, n[0]))

                v, a, r = root_v[:, :, 0], root_a[:, :, 0], rstd[:, :, 0]
                link(dve.tensor_scalar(v, mv[:, :, 1], LN_EPS, None, ALU.add))
                link(dve.tensor_scalar(a.bitcast(I32), v.bitcast(I32), 1, None, ALU.logical_shift_right))
                link(dve.tensor_scalar(r.bitcast(I32), a.bitcast(I32), -1.0, float(0x5F3759DF), ALU.mult, ALU.add))
                for _ in range(3):
                    link(dve.tensor_tensor(a, r, r, ALU.mult))
                    link(dve.scalar_tensor_tensor(a, a, -0.5, v, ALU.mult, ALU.mult))
                    link(dve.scalar_tensor_tensor(r, a, 1.5, r, ALU.add, ALU.mult))

            def norm(which, blk, stream, have_statistics=False):
                if not have_statistics:
                    for c in range(NT):
                        statistics(which, blk, c, stream)
                dve.wait_ge(*ln[which][1](blk, NT))
                inverse_root(which, blk)
                for c in range(NT):
                    dve.tensor_scalar(stream[:, c, :], stream[:, c, :], mv[:, c, 0:1], rstd[:, c, :], ALU.subtract,
                                      ALU.mult).then_inc(ln[which][3].sem, 1)

            def shared(ab, cb):
                first = cb is None
                ring = ring_banks(ab)
                a_jobs = 0
                for kind, n in opening(ab is not None, cb is not None):
                    if kind == "scores":
                        c, g = n // NG, n % NG
                        dve.wait_ge(*sc_done(cb, n + 1))
                        dve.tensor_reduce(xmax[:, c, GH * g:GH * g + GH],
                                          score_banks[n % 4][:, 0:GN].rearrange("p (j n) -> p j n", j=GH),
                                          AX.X, ALU.max).then_inc(sc_max.sem, 1)
                for s in range(LAST):
                    for kind, n in steps(s, ab is not None, cb is not None):
                        if kind == "project":
                            bank = ring[a_jobs % len(ring)]
                            half = qk[:, n % 2, n // 2 % 2, :, :]
                            dve.wait_ge(*p_sq(ab, n + 1))
                            dve.scalar_tensor_tensor(half[:, 1, :], bank[:, :], 1 / W_SCALE, half[:, 0, :], ALU.mult,
                                                     ALU.subtract).then_inc(p_low.sem, 1)
                            dve.tensor_copy(half[:, 2, :], square[:, n % 2, :]).then_inc(p_sqh.sem, 1)
                        elif kind == "attend":
                            dve.wait_ge(*att_done(ab, n + 1))
                            dve.tensor_tensor(att[:, n % 3, :, :], ps_att[:, :].rearrange("p (c t) -> p c t", t=P),
                                              causal[:, :].unsqueeze(1).to_broadcast([P, NT, P]),
                                              ALU.mult).then_inc(att_kept.sem, 1)
                        elif kind == "state":
                            r = run[:, n % 2, :, :]
                            dve.wait_ge(*st_done(ab, n + 1))
                            dve.tensor_scalar(r[:, 0, :], state[:, n, :], keep[:, 0:1], None, ALU.mult
                                              ).then_inc(run_step.sem, 1)
                            for c in range(1, NT + 1):
                                dve.wait_ge(*run_step(ab, 4 * n + c))
                                dst = r[:, c, :] if c < NT else state[:, n, :]
                                dve.tensor_tensor(dst, r[:, c - 1, :], ps_so[:, V1 * (c - 1):V1 * c], ALU.add
                                                  ).then_inc((run_step if c < NT else run_ready).sem, 1)
                        elif kind == "output":
                            output_job(n, ab)
                        elif kind == "turn output":
                            turn_output_job(n, ab)
                        elif kind == "turn maxima":
                            dve.wait_ge(*mx_turned(cb, 1))
                            dve.tensor_scalar(xq[96:P, 0, :], ps_turn[0:XHALVES, :], 1 / MAX_SCALE, None, ALU.mult
                                              ).then_inc(mx_kept.sem, 1)
                            dve.wait_ge(*mx_kept(cb, 1))
                            dve.tensor_copy(xq[96:P, 1:NG, :], xq[96:P, 0:1, :].to_broadcast([P - 96, NG - 1, TB])
                                            ).then_inc(mx_spread.sem, 1)
                        elif kind == "weigh" and n % 2 == 1:
                            g = n // 2
                            o = weigh_bank(ab, g)[:, 0:NT * GV].rearrange("p (h v) -> p h v", v=XV + 1)
                            dve.wait_ge(*weighed(cb, 2 * g + 2))
                            dve.reciprocal(xrec[:, g % 2, :, :], o[:, :, XV:XV + 1]).then_inc(xo_rec.sem, 1)
                            dve.wait_ge(*xo_rec(cb, g + 1))
                            dve.tensor_tensor(xrec2[:, g % 2, :, :], xrec[:, g % 2, :, :], coef[:, :, :],
                                              ALU.mult).then_inc(xo_coef.sem, 1)
                            dve.wait_ge(*xo_coef(cb, g + 1))
                            if g >= 2:
                                dve.wait_ge(*xo_sum(cb, g - 1))
                            dve.tensor_tensor(xterm[:, g % 2, :, :, :].rearrange("p h i d -> p (h i) d"),
                                              o[:, :, 0:XV], xrec2[:, g % 2, :, :].to_broadcast([P, XV, XV]),
                                              ALU.mult).then_inc(xo_kept.sem, 1)
                        elif kind == "norm":
                            dve.wait_ge(*xo_added(cb, NG))
                            norm(1, cb, resid)
                        elif kind == "turn cross":
                            dve.wait_ge(*x2_high(cb, n + 1))
                            dve.tensor_tensor(turned[:, 1, :, P * n:P * n + P],
                                              ps_turn[:, 0:D].rearrange("p (k t) -> p k t", k=KD),
                                              turned[:, 0, :, P * n:P * n + P], ALU.subtract).then_inc(x2_low.sem, 1)
                        if kind in ("project", "probs"):
                            a_jobs += 1
                    if first:
                        setup_step(s)

            def output_job(n, ab):
                o = ps_so[:, 0:NT * V1].rearrange("p (c v) -> p c v", v=V1)
                dve.wait_ge(*o_done(ab, n + 1))
                dve.tensor_scalar(den[:, n % 2, :, :], o[:, :, HD:V1], EPS, None, ALU.add).then_inc(o_den.sem, 1)
                dve.wait_ge(*o_den(ab, n + 1))
                dve.reciprocal(rec[:, n % 2, :, :], den[:, n % 2, :, :]).then_inc(o_rec.sem, 1)
                dve.wait_ge(*o_rec(ab, n + 1))
                dve.tensor_tensor(y[:, n // 2 % 2, :, HD * (n % 2):HD * (n % 2) + HD], o[:, :, 0:HD],
                                  rec[:, n % 2, :, :].to_broadcast([P, NT, HD]), ALU.mult).then_inc(o_kept.sem, 1)

            def turn_output_job(n, ab):
                dve.wait_ge(*yt_high(ab, n + 1))
                dve.tensor_tensor(yT[:, 1, n, :], ps_turn[:, :], yT[:, 0, n, :], ALU.subtract).then_inc(yt_low.sem, 1)

            def toggle_keep():
                dve.tensor_scalar(keep[:, :], keep[:, :], -1.0, 1.0, ALU.mult, ALU.add).then_inc(keep_set.sem, 1)

            def ffn(fb, ab):
                done = [0]

                def link(ins):
                    done[0] += 1
                    ins.then_inc(route.sem, 1)
                    dve.wait_ge(*route(fb, done[0]))

                def routing():
                    f = "p t e -> p (t e)"
                    dve.wait_ge(*gl_exp(fb, 1))
                    link(dve.tensor_scalar(gd[:, :], ge[:, :], 1.0, None, ALU.add))
                    link(dve.reciprocal(score[:, :, :].rearrange(f), gd[:, :]))
                    link(dve.tensor_tensor(choice[:, :, :], score[:, :, :],
                                           bias[:, :].unsqueeze(1).to_broadcast([P, NT, NE]), ALU.add))
                    two = choice[:, :, :].rearrange("p t (g q i) -> p (t g) q i", g=NGROUP, i=2)
                    link(dve.tensor_tensor(g_max[:, :, :], two[:, :, :, 0], two[:, :, :, 1], ALU.max))
                    link(dve.tensor_tensor(g_min[:, :, :], two[:, :, :, 0], two[:, :, :, 1], ALU.min))
                    link(dve.tensor_tensor(g_a[:, :], g_max[:, :, 0], g_max[:, :, 1], ALU.max))
                    link(dve.tensor_tensor(g_b[:, :], g_max[:, :, 0], g_max[:, :, 1], ALU.min))
                    link(dve.tensor_tensor(g_c[:, :], g_min[:, :, 0], g_min[:, :, 1], ALU.max))
                    link(dve.tensor_tensor(g_d[:, :], g_b[:, :], g_c[:, :], ALU.max))
                    link(dve.tensor_tensor(g_sum[:, :, :].rearrange("p t g -> p (t g)"), g_a[:, :], g_d[:, :], ALU.add))

                    def ranks(v, gt, eq, before, n, rank):
                        other = v.unsqueeze(2).to_broadcast([P, NT, n, n])
                        own = v.unsqueeze(3).to_broadcast([P, NT, n, n])
                        link(dve.tensor_tensor(gt, other, own, ALU.is_gt))
                        link(dve.tensor_tensor(eq, other, own, ALU.is_equal))
                        link(dve.tensor_tensor(eq, eq, before.unsqueeze(1).to_broadcast([P, NT, n, n]), ALU.mult))
                        link(dve.tensor_tensor(gt, gt, eq, ALU.add))
                        link(dve.tensor_reduce(rank, gt.rearrange("p t i j -> p (t i) j"), AX.X, ALU.add))

                    ranks(g_sum[:, :, :], g_gt[:, :, :, :], g_eq[:, :, :, :], before_g[:, :, :], NGROUP, g_rank[:, :])
                    link(dve.tensor_scalar(g_in[:, :, 0], g_rank[:, :], TOPK_GROUP - 0.5, None, ALU.is_lt))
                    link(dve.tensor_tensor(masked[:, :, :].rearrange("p t (g i) -> p (t g) i", g=NGROUP),
                                           choice[:, :, :].rearrange("p t (g i) -> p (t g) i", g=NGROUP),
                                           g_in[:, :, :].to_broadcast([P, NT * NGROUP, PER_GROUP]), ALU.mult))
                    ranks(masked[:, :, :], e_gt[:, :, :].rearrange("p t (i j) -> p t i j", i=NE),
                          e_eq[:, :, :].rearrange("p t (i j) -> p t i j", i=NE), before_e[:, :, :], NE, e_rank[:, :])
                    link(dve.scalar_tensor_tensor(chosen[:, :, :].rearrange(f), e_rank[:, :], TOPK - 0.5,
                                                  score[:, :, :].rearrange(f), ALU.is_lt, ALU.mult))
                    link(dve.tensor_reduce(w_sum[:, :], chosen[:, :, :], AX.X, ALU.add))
                    link(dve.tensor_scalar(w_sum[:, :], w_sum[:, :], 1e-20, None, ALU.add))
                    link(dve.reciprocal(w_rec[:, :], w_sum[:, :]))
                    link(dve.tensor_scalar(w_rec2[:, :, 0], w_rec[:, :], SCALING / W_SCALE, None, ALU.mult))
                    link(dve.tensor_tensor(weight[:, :, :], chosen[:, :, :],
                                           w_rec2[:, :, :].to_broadcast([P, NT, NE]), ALU.mult))
                    assert done[0] == ROUTE_STEPS

                for e in range(EXPERTS + 2):
                    if e < EXPERTS:
                        dve.wait_ge(*u_done(fb, e + 1))
                        dve.wait_ge(*silu(fb, e + 1))
                        dve.scalar_tensor_tensor(hid[:, e % 2, :], (ps_a[1], ps_kf)[e % 2][:, :], 1 / W_SCALE,
                                                 hid[:, e % 2, :], ALU.mult, ALU.mult).then_inc(hid_ready.sem, 1)
                    if e == 1:
                        routing()
                    if e >= 2:
                        d = e - 2
                        for half in range(2):
                            bank = down_banks[(2 * d + half) % 3]
                            dve.wait_ge(*down_done(fb, 2 * d + half + 1))
                            if d >= 1:
                                dve.wait_ge(*summed(fb, 2 * (d - 1) + half + 1))
                            for k in range(2):
                                c = 2 * half + k
                                by = 1 / W_SCALE if d == 0 else weight[:, c, d - 1:d]
                                last = dve.scalar_tensor_tensor(resid[:, c, :], bank[:, D * k:D * k + D], by,
                                                                resid[:, c, :], ALU.mult, ALU.add)
                            last.then_inc(summed.sem, 1)
                    if ab is not None:
                        for kind, n in late_jobs(e) + tail_jobs(e):
                            tail_job(kind, n, ab, False)
                dve.wait_ge(*summed(fb, 2 * EXPERTS))
                toggle_keep()
                norm(2, fb, resid)

            def tail_job(kind, n, ab, alone):
                if kind == "output":
                    output_job(n, ab)
                elif kind == "turn output":
                    turn_output_job(n, ab)
                elif kind == "project out":
                    if n == 0:
                        dve.wait_ge(*xin_loaded(ab, 1))
                    dve.wait_ge(*wo_done(ab, n + 1))
                    dve.scalar_tensor_tensor(nxt[:, n, :], tail_bank(kind, n, alone)[:, 0:D], 1 / W_SCALE,
                                             nxt[:, n, :], ALU.mult, ALU.add).then_inc(x1_added.sem, 1)
                    dve.wait_ge(*x1_added(ab, n + 1))
                    statistics(0, ab, n, nxt)
                elif kind == "norm":
                    norm(0, ab, nxt, have_statistics=True)
                elif kind == "turn stream":
                    dve.wait_ge(*x1_high(ab, n + 1))
                    dve.tensor_tensor(turned_next[:, 1, :, stream_cols(n)],
                                      tail_bank(kind, n, alone)[:, :].rearrange("p (k t) -> p k t", k=KD),
                                      turned_next[:, 0, :, stream_cols(n)], ALU.subtract).then_inc(x1_low.sem, 1)
                elif kind == "queries":
                    dve.wait_ge(*xq_high(ab, n + 1))
                    dve.scalar_tensor_tensor(xq_hl[:, 1, n, :], tail_bank(kind, n, alone)[:, :], 1 / W_SCALE,
                                             xq_hl[:, 0, n, :], ALU.mult, ALU.subtract).then_inc(xq_low.sem, 1)
                elif kind == "split":
                    split_x(ab + 1)

            held = signal("held")
            shared(0, None)
            for kind, n in tail_jobs(None):
                tail_job(kind, n, 0, True)
            toggle_keep()
            with dve.Fori(0, NBLK - 1) as i:
                shared(i + 1, i)
                ffn(i, i + 1)
            shared(None, NBLK - 1)
            ffn(NBLK - 1, None)

        @block.tensor
        def _(pe):
            def three_pass(dst, lhs, rhs, first=True, last=True):
                for n, (i, j) in enumerate(((0, 0), (0, 1), (1, 0))):
                    ins = pe.matmul(dst, lhs(i), rhs(j), start=first and n == 0, stop=last and n == 2)
                return ins

            def cross_keys_values():
                pe.wait_ge(*ctx_loaded(0, 3))
                for b in range(B):
                    for m in range(KD):
                        n = KD * b + m
                        for k in range(KD):
                            pe.matmul(ps_xo[:, CTX * n:CTX * n + CTX], xwk_sb[:, k, P * m:P * m + P],
                                      ctx_sb[:, k, CTX * b:CTX * b + CTX], start=(k == 0), stop=(k == KD - 1))
                for b in range(B):
                    for k in range(KD):
                        last = pe.matmul(ps_so[0:CTX, D * b:D * b + D], ctx_sb[:, k, CTX * b:CTX * b + CTX],
                                         xwv_sb[:, k, :], start=(k == 0), stop=(k == KD - 1))
                last.then_inc(xkv_done.sem, 1)

            def output_job(n, ab):
                pe.wait_ge(*att_kept(ab, n + 1))
                if n + 1 < H:
                    pe.wait_ge(*run_ready(ab, n + 2))
                else:
                    pe.wait_ge(*o_kept(ab, n))
                for c in range(NT):
                    o = ps_so[:, V1 * c:V1 * c + V1]
                    pe.matmul(o, att[:, n % 3, c, :], v1[:, c, n, :], start=True, stop=False)
                    last = pe.matmul(o, qf[:, n % 4, P * c:P * c + P], run[:, n % 2, c, :], start=False, stop=True)
                last.then_inc(o_done.sem, 1)

            def turn_output_job(n, ab):
                pe.wait_ge(*o_kept(ab, 2 * n + 2))
                for c in range(NT):
                    last = pe.transpose(ps_turn[:, P * c:P * c + P], y[:, n % 2, c, :], ident[:, :])
                last.then_inc(yt_done.sem, 1)

            def open_block(ab, cb):
                if ab is not None:
                    pe.wait_ge(*x_high(ab, 1))
                    pe.wait_ge(*x_low(ab, 1))
                for kind, n in opening(ab is not None, cb is not None):
                    if kind == "values":
                        c, half = n // 2, n % 2
                        if n >= 2:
                            pe.wait_ge(*v_kept(ab, n - 1))
                        if cb is None and n == 0:
                            pe.wait_ge(*w_low(0, 2))
                        for k in range(KD):
                            last = three_pass(ps_a[half][:, :], lambda i: x_split[:, i, k, P * c:P * c + P],
                                              lambda j: w_v[:, j, k, 512 * half:512 * half + 512], k == 0, k == KD - 1)
                        last.then_inc(v_done.sem, 1)
                    else:
                        if n == 0:
                            pe.wait_ge(*keep_set(cb, 1))
                            pe.wait_ge(*xq_placed(cb, 12))
                            pe.wait_ge(*xkv_placed(cb, 2))
                        if n >= 4:
                            pe.wait_ge(*sc_max(cb, n - 3))
                        c, g = n // NG, n % NG
                        pe.matmul(score_banks[n % 4][:, 0:GN], xq[0:96, g, P * c:P * c + P], xk[0:96, g, 0:GN],
                                  start=True, stop=True).then_inc(sc_done.sem, 1)

            def shared(ab, cb):
                open_block(ab, cb)
                if cb is None:
                    cross_keys_values()
                ring = ring_banks(ab)
                a_jobs = 0
                a_free = [[] for _ in ring]
                turn_free = []
                if ab is not None:
                    a_free = [[v_kept(ab, 2 * NT - 1)], [v_kept(ab, 2 * NT)]]
                for s in range(LAST):
                    for kind, n in steps(s, ab is not None, cb is not None):
                        if kind in ("project", "probs"):
                            bank = ring[a_jobs % len(ring)]
                            for free in a_free[a_jobs % len(ring)]:
                                pe.wait_ge(*free)
                        if kind.startswith("turn"):
                            for free in turn_free:
                                pe.wait_ge(*free)
                        if kind == "project":
                            w = (w_q, w_k)[n % 2]
                            if cb is None and n < 2:
                                pe.wait_ge(*w_low(0, 4 + 2 * n))
                            for k in range(KD):
                                last = three_pass(bank[:, :], lambda i: w[:, i, k, P * (n // 2):P * (n // 2) + P],
                                                  lambda j: x_split[:, j, k, :], k == 0, k == KD - 1)
                            last.then_inc(p_done.sem, 1)
                            a_free[a_jobs % len(ring)] = [p_sq(ab, n + 1), p_low(ab, n + 1)]
                        elif kind == "turn keys":
                            if n == 0 and cb is None:
                                pe.wait_ge(consts.sem, 11)
                            pe.wait_ge(*kf_exp(ab, n + 1))
                            for c in range(NT):
                                last = pe.transpose(ps_turn[:, P * c:P * c + P], kf[:, n % 2, P * c:P * c + P], ident[:, :])
                            last.then_inc(turned_k.sem, 1)
                            turn_free = [kt_kept(ab, n + 1)]
                        elif kind in ("q features", "k features"):
                            w, to = (0, ps_qf) if kind == "q features" else (1, ps_kf)
                            source = qk[:, w, n // 2 % 2, :, :]
                            job = 2 * (n // 2) + w + 1
                            if n == 0 and w == 0 and cb is None:
                                pe.wait_ge(*w_low(0, FEAT_PIECE + 1))
                                pe.wait_ge(*v_ones(0, 7))
                            pe.wait_ge(*p_low(ab, job))
                            pe.wait_ge(*p_sql(ab, job))
                            if n:
                                pe.wait_ge(*(qf_exp, kf_exp)[w](ab, n))
                            wf = w_feat[:, n % 2, :, :]
                            pe.matmul(to[:, :], wf[:, 0, :], source[:, 0, :], start=True, stop=False)
                            pe.matmul(to[:, :], wf[:, 0, :], source[:, 1, :], start=False, stop=False)
                            pe.matmul(to[:, :], wf[:, 1, :], source[:, 0, :], start=False, stop=False)
                            pe.matmul(to[:, :], neg_half[:, n % 2, :], source[:, 2, :], start=False, stop=False)
                            pe.matmul(to[:, :], neg_half[:, n % 2, :], source[:, 3, :], start=False, stop=True
                                      ).then_inc((qf_done, kf_done)[w].sem, 1)
                        elif kind == "attend":
                            pe.wait_ge(*qf_exp(ab, n + 1))
                            if n:
                                pe.wait_ge(*att_kept(ab, n))
                            for c in range(NT):
                                t = slice(P * c, P * c + P)
                                last = pe.matmul(ps_att[:, t], kf[:, n % 2, t], qf[:, n % 4, t], start=True, stop=True)
                            last.then_inc(att_done.sem, 1)
                        elif kind == "state":
                            pe.wait_ge(*kt_kept(ab, n + 1))
                            if n == 0:
                                pe.wait_ge(*v_kept(ab, 2 * NT))
                                if cb is None:
                                    pe.wait_ge(*v_copied(0, 2 * B + 2))
                            if n == 1:
                                pe.wait_ge(*run_ready(ab, 1))
                            if n >= 2:
                                pe.wait_ge(*o_kept(ab, n - 1))
                            for c in range(NT):
                                last = pe.matmul(ps_so[:, V1 * c:V1 * c + V1], kt[:, n % 2, c, :], v1[:, c, n, :],
                                                 start=True, stop=True)
                            last.then_inc(st_done.sem, 1)
                        elif kind == "output":
                            output_job(n, ab)
                        elif kind == "turn output":
                            turn_output_job(n, ab)
                            turn_free = [yt_high(ab, n + 1), yt_low(ab, n + 1)]
                        elif kind == "turn maxima":
                            pe.wait_ge(*sc_max(cb, NT * NG))
                            for c in range(NT):
                                last = pe.transpose(ps_turn[0:XHALVES, P * c:P * c + P], xmax[:, c, :], ident[:, :])
                            last.then_inc(mx_turned.sem, 1)
                            turn_free = [mx_kept(cb, 1)]
                        elif kind == "probs":
                            if n == 0:
                                pe.wait_ge(*mx_spread(cb, 1))
                            g, chunk = n // GC, n % GC
                            pe.matmul(bank[:, :], xk[:, g, P * chunk:P * chunk + P], xq[:, g, :], start=True,
                                      stop=True).then_inc(pr_done.sem, 1)
                            a_free[a_jobs % len(ring)] = [pr_exp(cb, n + 1)]
                        elif kind == "weigh":
                            g, half = n // 2, n % 2
                            banks = 1 if ab is not None else 2
                            if half == 0:
                                pe.wait_ge(*pr_low(cb, GC * (g + 1)))
                                if g >= banks:
                                    pe.wait_ge(*xo_kept(cb, g - banks + 1))
                            for c in (2 * half, 2 * half + 1):
                                for chunk in range(GC):
                                    last = three_pass(
                                        weigh_bank(ab, g)[:, GV * c:GV * c + GV],
                                        lambda i: prob[:, (GC * g + chunk) % RING, i, P * c:P * c + P],
                                        lambda j: xv[:, g, chunk, j, :], chunk == 0, chunk == GC - 1)
                            last.then_inc(weighed.sem, 1)
                        elif kind == "turn cross":
                            pe.wait_ge(*ln[1][3](cb, n + 1))
                            for k in range(KD):
                                last = pe.transpose(ps_turn[:, P * k:P * k + P], resid[:, n, P * k:P * k + P], ident[:, :])
                            last.then_inc(x2_turned.sem, 1)
                            turn_free = [x2_high(cb, n + 1), x2_low(cb, n + 1)]
                        if kind in ("project", "probs"):
                            a_jobs += 1

            def ffn(fb, ab):
                pe.wait_ge(*x2_high(fb, NT))
                pe.wait_ge(*x2_low(fb, NT))
                for c in range(NT):
                    for k in range(KD):
                        last = three_pass(ps_turn[:, NE * c:NE * c + NE], lambda i: turned[:, i, k, P * c:P * c + P],
                                          lambda j: w_gate[:, j, k, :], k == 0, k == KD - 1)
                last.then_inc(gl_done.sem, 1)
                for e in range(EXPERTS + 2):
                    if e < EXPERTS:
                        pe.wait_ge(*gw_loaded[e % 2](fb, e // 2 + 1))
                        for half, (banks, free, done) in enumerate((((ps_a[0], ps_qf), silu, g_done),
                                                                    ((ps_a[1], ps_kf), hid_ready, u_done))):
                            if e >= 2:
                                pe.wait_ge(*free(fb, e - 1))
                            for k in range(KD):
                                cols = slice(D * half + P * k, D * half + P * k + P)
                                last = three_pass(banks[e % 2][:, :], lambda i: gu_w[:, e % 2, i, cols],
                                                  lambda j: turned[:, j, k, :], k == 0, k == KD - 1)
                            last.then_inc(done.sem, 1)
                        if ab is not None:
                            for kind, n in late_jobs(e) + tail_jobs(e):
                                tail_job(kind, n, ab, fb)
                    if e >= 2:
                        d = e - 2
                        pe.wait_ge(*dw_loaded[d % 4](fb, d // 4 + 1))
                        pe.wait_ge(*h_high(fb, d + 1))
                        pe.wait_ge(*h_low(fb, d + 1))
                        for half in range(2):
                            u = 2 * d + half
                            bank = down_banks[u % 3]
                            if u >= 3:
                                pe.wait_ge(*summed(fb, u - 2))
                            elif u == 2 and ab is None:
                                pe.wait_ge(*gl_exp(fb, 1))
                            elif ab is not None:
                                pe.wait_ge(*(att_kept(ab, H), o_kept(ab, H), yt_low(ab, PAIRS))[u])
                            for t in range(2):
                                c = 2 * half + t
                                last = three_pass(bank[:, D * t:D * t + D], lambda i: hT[:, d % 3, i, P * c:P * c + P],
                                                  lambda j: down_w[:, d % 4, j, :])
                            last.then_inc(down_done.sem, 1)

            def tail_job(kind, n, ab, fb):
                alone = fb is None
                if kind == "norm" or kind == "split":
                    return
                if kind == "output":
                    output_job(n, ab)
                    return
                if kind == "turn output":
                    pe.wait_ge(*(yt_low(ab, n) if alone else gl_exp(fb, 1)))
                    turn_output_job(n, ab)
                    return
                bank = tail_bank(kind, n, alone)
                if kind == "project out":
                    if n == 0:
                        pe.wait_ge(*yt_high(ab, PAIRS))
                        pe.wait_ge(*yt_low(ab, PAIRS))
                        if alone:
                            pe.wait_ge(*w_low(0, len(pieces) - 1))
                        else:
                            pe.wait_ge(*xo_kept(fb, NG))
                    elif not alone:
                        pe.wait_ge(*x1_added(ab, n))
                    for p in range(PAIRS):
                        last = three_pass(bank[:, 0:D], lambda i: yT[:, i, p, P * n:P * n + P],
                                          lambda j: w_o[:, j, p, :], p == 0, p == PAIRS - 1)
                    last.then_inc(wo_done.sem, 1)
                elif kind == "turn stream":
                    pe.wait_ge(*ln[0][3](ab, 2 * n + 2))
                    if n and not alone:
                        pe.wait_ge(*x1_low(ab, n))
                    for k in range(KD):
                        for c in range(2):
                            last = pe.transpose(bank[:, P * (2 * k + c):P * (2 * k + c) + P],
                                                nxt[:, 2 * n + c, P * k:P * k + P], ident[:, :])
                    last.then_inc(x1_turned.sem, 1)
                elif kind == "queries":
                    if n == 0:
                        pe.wait_ge(*x1_high(ab, 2))
                        pe.wait_ge(*x1_low(ab, 2))
                    elif not alone:
                        pe.wait_ge(*xq_low(ab, n))
                    for k in range(KD):
                        last = three_pass(bank[:, :], lambda i: w_xq[:, i, k, P * n:P * n + P],
                                          lambda j: turned_next[:, j, k, :], k == 0, k == KD - 1)
                    last.then_inc(xq_done.sem, 1)

            shared(0, None)
            for kind, n in tail_jobs(None):
                tail_job(kind, n, 0, None)
            pe.wait_ge(*xq_high(0, KD))
            pe.wait_ge(*xq_low(0, KD))
            with pe.Fori(0, NBLK - 1) as i:
                shared(i + 1, i)
                ffn(i, i + 1)
            shared(None, NBLK - 1)
            ffn(NBLK - 1, None)


def kernel(x, ctx_1024, L0_attn_Wq, L0_attn_Wk, L0_attn_Wv, L0_attn_Wo, L0_attn_W_feat, L0_xattn_Wq, L0_xattn_Wk,
           L0_xattn_Wv, L0_xattn_lambda_q1, L0_xattn_lambda_q2, L0_xattn_lambda_k1, L0_xattn_lambda_k2,
           L0_ffn_gate_w, L0_ffn_e_bias, L0_ffn_gate_proj, L0_ffn_up_proj, L0_ffn_down_proj,
           L0_ffn_shared_gate_w, L0_ffn_shared_up_w, L0_ffn_shared_down_w):
    import concourse.bacc as bacc
    from concourse.bass_utils import run_bass_kernel_spmd

    def by_rows(w):
        w = np.swapaxes(np.asarray(w), -1, -2)
        w = w.reshape(*w.shape[:-2], KD, P, w.shape[-1])
        return np.swapaxes(w, -3, -2).reshape(*w.shape[:-3], P, -1)

    def with_shared(shared, experts):
        return np.concatenate([np.asarray(shared)[None], np.asarray(experts)], 0)

    gate = by_rows(with_shared(L0_ffn_shared_gate_w, L0_ffn_gate_proj))
    up = by_rows(with_shared(L0_ffn_shared_up_w, L0_ffn_up_proj))
    down = np.swapaxes(with_shared(L0_ffn_shared_down_w, L0_ffn_down_proj), 1, 2)
    tokens = np.asarray(x).reshape(B * S, D)
    arrays = {
        "x": tokens.reshape(NBLK, NT, P, D).transpose(2, 0, 1, 3),
        "xT": tokens.T.reshape(KD, P, B * S).transpose(1, 0, 2),
        "ctxT": np.asarray(ctx_1024).reshape(B * CTX, D).T,
        "wq": L0_attn_Wq, "wk": L0_attn_Wk, "wv": L0_attn_Wv, "wo": L0_attn_Wo, "wfeat": L0_attn_W_feat,
        "xwqT": np.asarray(L0_xattn_Wq).T, "xwkT": np.asarray(L0_xattn_Wk).T, "xwvT": np.asarray(L0_xattn_Wv).T,
        "lam_q1": L0_xattn_lambda_q1, "lam_q2": L0_xattn_lambda_q2,
        "lam_k1": L0_xattn_lambda_k1, "lam_k2": L0_xattn_lambda_k2,
        "gate_wT": np.asarray(L0_ffn_gate_w).T, "e_bias": L0_ffn_e_bias,
        "ffn_w": np.concatenate([gate, up, down], -1),
    }
    arrays = {name: np.ascontiguousarray(a) for name, a in arrays.items()}
    nc = bacc.Bacc("TRN2", target_bir_lowering=False, num_devices=1)
    args = {name: nc.dram_tensor(name, a.shape, mybir.dt.from_np(a.dtype), kind="ExternalInput").ap()
            for name, a in arrays.items()}
    args["out"] = nc.dram_tensor("out", (P, NBLK, NT, D), F32, kind="ExternalOutput").ap()
    decoder_layer(nc, **args)
    got = run_bass_kernel_spmd(nc, [arrays], core_ids=[0]).results[0]["out"]
    return np.asarray(got).transpose(1, 2, 0, 3).reshape(B, S, D)
```

```python
from contextlib import ExitStack

import numpy as np

import concourse.bass as bass
from concourse import mybir

ALU = mybir.AluOpType
ACT = mybir.ActivationFunctionType
AX = mybir.AxisListType
F32 = mybir.dt.float32
F16 = mybir.dt.float16
I32 = mybir.dt.int32

P = 128
B, S, D = 2, 1024, 256
CTX = 77
H, HD, NF = 16, 64, 128
PAIRS = H // 2
XHALVES, XD = 32, 8
XV = 16
NE, INTER, NGROUP, PER_GROUP, TOPK_GROUP, TOPK = 16, 128, 4, 4, 2, 4
SCALING = 2.5
LN_EPS = 1e-5
EPS = 1e-6 * NF
LAMBDA_INIT = 0.8
W_SCALE = 64.0

TB = 512
NT = TB // P
NBLK = B * S // TB
BLK_PER_BATCH = S // TB
KD = D // P
V1 = HD + 1
GH = 4
NG = XHALVES // GH
GN = GH * CTX
GC = 3
CHUNKS = NG * GC
RING = 2 * GC
MAX_SCALE = 64.0
GV = GH * (XV + 1)
EXPERTS = NE + 1
FW = 2 * D + D
ROUTE_STEPS = 28
ROOT_STEPS = 12
LAST = 18


def opening(attn, cross):
    jobs = []
    for v in range(2 * NT):
        if attn:
            jobs.append(("values", v))
        if attn and cross and v == 3:
            jobs += [("project", 0), ("project", 1)]
        if cross and v >= 3:
            jobs += [("scores", n) for n in range(5 * (v - 3), 5 * (v - 2))]
    if attn and not cross:
        jobs += [("project", 0), ("project", 1)]
    return jobs


def steps(s, attn, cross):
    jobs = []

    def add(on, kind, n, count):
        if on and 0 <= n < count:
            jobs.append((kind, n))

    if s == 0:
        for n in range(5 * (2 * NT - 3), NT * NG):
            add(cross, "scores", n, NT * NG)
    if s == 1:
        add(cross, "turn maxima", 0, 1)
    if s == 15:
        add(cross, "norm", 0, 1)
    add(attn, "project", s + 2, H)
    add(attn, "turn keys", s - 1, H)
    add(attn, "q features", s, H)
    add(attn, "state", s - 2, H)
    add(attn, "attend", s - 1, H)
    if s % 2 == 1:
        add(attn, "turn output", (s - 5) // 2, PAIRS)
    add(cross, "probs", 2 * s - 2, CHUNKS)
    add(attn, "k features", s, H)
    add(attn, "output", s - 3, H)
    add(cross, "probs", 2 * s - 1, CHUNKS)
    for m in range(2 * NG):
        if s == 3 + 3 * m // 4:
            add(cross, "weigh", m, 2 * NG)
    add(cross, "turn cross", s - 16, 2)
    return jobs


def late_jobs(e):
    return {0: [("output", H - 1)], 1: [("turn output", PAIRS - 1)]}.get(e, [])


def tail_jobs(e):
    if e is None:
        return [job for e in range(EXPERTS) for job in late_jobs(e) + tail_jobs(e)]
    if 3 <= e < 3 + NT:
        return [("project out", e - 3)] + ([("norm", 0)] if e == 2 + NT else [])
    return {8: [("turn stream", 0)], 10: [("turn stream", 1)],
            12: [("queries", 0)], 13: [("queries", 1)], 14: [("split", 0)]}.get(e, [])


class Signal:

    def __init__(self, sem, per, unit):
        self.sem, self.per, self.unit = sem, per, unit

    def __call__(self, block, n):
        return self.sem, (block * self.per + n) * self.unit


def decoder_layer(nc, x, xT, ctxT, wq, wk, wv, wo, wfeat, xwqT, xwkT, xwvT, lam_q1, lam_q2, lam_k1,
                  lam_k2, gate_wT, e_bias, ffn_w, out):
    with ExitStack() as stack:
        def sb(name, shape, dt=F32):
            return stack.enter_context(nc.sbuf_tensor(name, shape, dt))

        def signal(name, per=1, unit=1):
            return Signal(stack.enter_context(nc.semaphore(name)), per, unit)

        w_q = sb("w_q", [P, 2, KD, H * HD], F16)
        w_k = sb("w_k", [P, 2, KD, H * HD], F16)
        w_v = sb("w_v", [P, 2, KD, H * HD], F16)
        w_o = sb("w_o", [P, 2, PAIRS, D], F16)
        w_xq = sb("w_xq", [P, 2, KD, D], F16)
        w_gate = sb("w_gate", [P, 2, KD, NE], F16)
        w_feat_high = sb("w_feat_high", [P, NF], F16)
        w_feat_low = sb("w_feat_low", [P, 2, NF], F16)
        neg_half = sb("neg_half", [P, NF], F16)
        ident = sb("ident", [P, P])
        causal = sb("causal", [P, P])
        before_e = sb("before_e", [P, NE, NE], F16)
        before_g = sb("before_g", [P, NGROUP, NGROUP], F16)
        bias = sb("bias", [P, NE])
        lam_in = sb("lam_in", [P, 4, XD])
        lam_prod = sb("lam_prod", [P, 2, XD])
        lam_sum = sb("lam_sum", [P, 2])
        lam_exp = sb("lam_exp", [P, 2])
        coef = sb("coef", [P, 2 * XV // 2, 1])
        x_stage = sb("x_stage", [P, KD, TB])
        x_split = sb("x_split", [P, 2, KD, TB], F16)
        resid = sb("resid", [P, NT, D])
        nxt = sb("nxt", [P, NT, D])
        turned = sb("turned", [P, 2, KD, TB], F16)
        turned_next = x_split
        qk = sb("qk", [P, 2, 2, 2, 2, TB], F16)
        square = sb("square", [P, 2, TB])
        v1 = sb("v1", [P, NT, H, V1])
        qf = sb("qf", [P, 4, TB])
        kf = sb("kf", [P, 2, TB])
        kt = sb("kt", [P, 2, NT, NF])
        att = sb("att", [P, 3, NT, P])
        state = sb("state", [P, H, V1])
        keep = sb("keep", [P, 1])
        run = sb("run", [P, 2, NT, V1])
        den = sb("den", [P, 2, NT, 1])
        rec = sb("rec", [P, 2, NT, 1])
        y = sb("y", [P, 2, NT, P])
        yT = sb("yT", [P, 2, PAIRS, TB], F16)
        xq_hl = sb("xq_hl", [P, 2, KD, TB], F16)
        xq = sb("xq", [P, NG, TB], F16)
        xk = sb("xk", [P, NG, GC * P], F16)
        xv = sb("xv", [P, NG, GC, 2, GV], F16)
        xmax = sb("xmax", [P, NT, XHALVES])
        prob = sb("prob", [P, RING, 2, TB], F16)
        xrec = sb("xrec", [P, 2, XHALVES // 2, 1])
        xrec2 = sb("xrec2", [P, 2, XHALVES // 2, 1])
        xterm = sb("xterm", [P, 2, XHALVES // 4, 2, XV])
        xsum = sb("xsum", [P, 2, XHALVES // 4, XV])
        st = sb("st", [P, NT, 6])
        mv = sb("mv", [P, NT, 2])
        rstd = sb("rstd", [P, NT, 1])
        root_v = sb("root_v", [P, NT, 1])
        root_a = sb("root_a", [P, NT, 1])
        ffn_mem = sb("ffn_mem", [P, 3072])
        hT = sb("hT", [P, 3, 2, TB], F16)
        ge = sb("ge", [P, NT * NE])
        gd = sb("gd", [P, NT * NE])
        score = sb("score", [P, NT, NE])
        choice = sb("choice", [P, NT, NE])
        g_max = sb("g_max", [P, NT * NGROUP, 2])
        g_min = sb("g_min", [P, NT * NGROUP, 2])
        g_a = sb("g_a", [P, NT * NGROUP])
        g_b = sb("g_b", [P, NT * NGROUP])
        g_c = sb("g_c", [P, NT * NGROUP])
        g_d = sb("g_d", [P, NT * NGROUP])
        g_sum = sb("g_sum", [P, NT, NGROUP])
        g_gt = sb("g_gt", [P, NT, NGROUP, NGROUP], F16)
        g_eq = sb("g_eq", [P, NT, NGROUP, NGROUP], F16)
        g_rank = sb("g_rank", [P, NT * NGROUP])
        g_in = sb("g_in", [P, NT * NGROUP, 1])
        masked = sb("masked", [P, NT, NE])
        e_gt = sb("e_gt", [P, NT, NE * NE], F16)
        e_eq = sb("e_eq", [P, NT, NE * NE], F16)
        e_rank = sb("e_rank", [P, NT * NE])
        e_in = sb("e_in", [P, NT * NE])
        chosen = sb("chosen", [P, NT, NE])
        w_sum = sb("w_sum", [P, NT])
        w_rec = sb("w_rec", [P, NT])
        w_rec2 = sb("w_rec2", [P, NT, 1])
        weight = sb("weight", [P, NT, NE])

        gu_w = ffn_mem[:, 0:1024].bitcast(F16).rearrange("p (r a c) -> p r a c", r=2, a=2)
        down_w = ffn_mem[:, 1024:2048].bitcast(F16).rearrange("p (r a c) -> p r a c", r=4, a=2)
        hid = ffn_mem[:, 2048:3072].rearrange("p (r t) -> p r t", r=2)
        prob_full = hid
        low_parts = hT[:, :, :, :].rearrange("p r a t -> p (r a) t")[:, 0:4, :].rearrange("p (r a) t -> p r a t", r=2)
        fs_in = ffn_mem[:, 0:1536].rearrange("p (r c) -> p r c", r=2)
        fs_out = ffn_mem[:, 1536:3072].bitcast(F16).rearrange("p (r a c) -> p r a c", r=2, a=2)
        prob_mem = prob[:, :, :, :].rearrange("p r a t -> p (r a t)").bitcast(F32)
        w_stage = xq[:, :, :].rearrange("p g t -> p (g t)").bitcast(F32).rearrange("p (r c) -> p r c", r=2)
        ctx_mem = prob_mem[:, 4 * GN:]
        xwk_sb = ctx_mem[:, 0:512].rearrange("p (k n) -> p k n", k=KD)
        xwv_sb = ctx_mem[:, 512:1024].rearrange("p (k n) -> p k n", k=KD)
        ctx_sb = ctx_mem[:, 1024:1024 + KD * B * CTX].rearrange("p (k n) -> p k n", k=KD)
        kb_hl = prob_mem[:, 0:4 * GN].bitcast(F16).rearrange("p (n a c) -> p n a c", n=2 * B, a=2)
        nxt_mem = nxt[:, :, :].rearrange("p t d -> p (t d)")
        VEXT = B * XV * (XV + 1)
        v_ext = nxt_mem[:, 0:VEXT].bitcast(F16).rearrange("p (a b h d) -> p a b h d", a=2, b=B, h=XV)
        kb_full = nxt_mem[:, VEXT:VEXT + GN].rearrange("p (j n) -> p j n", j=GH)
        own_half = sb("own_half", [P, P // XD])
        own_row = sb("own_row", [P, GH, 1])

        def psum(name):
            return stack.enter_context(nc.psum_tensor(name, [P, 512], F32))

        ps_a = [psum("ps_a0"), psum("ps_a1")]
        ps_f = psum("ps_f")
        ps_o = psum("ps_o")
        ps_att = psum("ps_att")
        ps_turn = psum("ps_turn")
        ps_st = psum("ps_st")
        ps_xo = psum("ps_xo")

        high_rows = (slice(0, HD), slice(HD, P))
        low_rows = high_rows[::-1]
        score_banks = (ps_xo, ps_turn, ps_att, ps_st)

        def ring_banks(ab):
            return (ps_a[0], ps_a[1]) if ab is not None else (ps_a[0], ps_a[1], ps_f, ps_o)

        def tail_bank(kind, n, alone):
            if not alone:
                return ps_xo
            return {"project out": (ps_a[0], ps_a[1], ps_f, ps_o), "turn stream": (ps_att, ps_st),
                    "queries": (ps_turn, ps_xo)}[kind][n]

        def stream_cols(j):
            return slice(2 * P * j, 2 * P * (j + 1))

        down_banks = (ps_att, ps_st, ps_turn)

        def output_bank(n):
            return ps_o if n < H - 1 else ps_st

        def weigh_bank(ab, g):
            return ps_xo if ab is not None or g % 2 == 0 else ps_st

        ffn_scr = nc.dram_tensor("ffn_split", [EXPERTS, P, 2, FW], F16, kind="Internal").ap()
        xk_scr = nc.dram_tensor("xk_blocks", [B, 96, NG, GN], F16, kind="Internal").ap()
        xv_scr = nc.dram_tensor("xv_blocks", [B, P, NG, GC, 2, GV], F16, kind="Internal").ap()

        consts = signal("consts", 4)
        own_ready = signal("own_ready"); v_ones = signal("v_ones"); zeros_v = signal("zeros_v")
        c_loaded = signal("c_loaded", 1, 16)
        ctx_loaded = signal("ctx_loaded", 1, 16)
        w_loaded = [signal("w_loaded0", 1, 16), signal("w_loaded1", 1, 16)]
        w_high = signal("w_high"); w_low = signal("w_low")
        xkv_done = signal("xkv_done"); kb_copied = signal("kb_copied"); kb_masked = signal("kb_masked")
        kb_high = signal("kb_high"); kb_low = signal("kb_low"); v_copied = signal("v_copied")
        lam_step = signal("lam_step"); lam_exped = signal("lam_exped"); coef_ready = signal("coef_ready")
        zero_stored = signal("zero_stored", 1, 16); ctx_stored = signal("ctx_stored", 1, 16)
        fs_loaded = [signal("fs_loaded0", 1, 16), signal("fs_loaded1", 1, 16)]
        fs_high = signal("fs_high"); fs_low = signal("fs_low")
        fs_stored = [signal("fs_stored0", 1, 16), signal("fs_stored1", 1, 16)]
        v_done = signal("v_done", 2 * NT); p_done = signal("p_done", H)
        turned_k = signal("turned_k", H); qf_done = signal("qf_done", H); kf_done = signal("kf_done", H)
        st_done = signal("st_done", H); att_done = signal("att_done", H); o_done = signal("o_done", H)
        yt_done = signal("yt_done", PAIRS)
        xs_loaded = signal("xs_loaded", 1, 16)
        x_high = signal("x_high"); x_low = signal("x_low")
        v_kept = signal("v_kept", 2 * NT)
        low_moved = [signal(f"low_moved{n}", H // 4 * 2, 16) for n in range(4)]
        p_low = signal("p_low", H); p_sq = signal("p_sq", H)
        p_sqh = signal("p_sqh", H); p_sql = signal("p_sql", H)
        qf_exp = signal("qf_exp", H); kf_exp = signal("kf_exp", H); kt_kept = signal("kt_kept", H)
        att_kept = signal("att_kept", H); run_step = signal("run_step", 4 * H); run_ready = signal("run_ready", H)
        o_den = signal("o_den", H); o_rec = signal("o_rec", H); o_kept = signal("o_kept", H)
        yt_high = signal("yt_high", PAIRS); yt_low = signal("yt_low", PAIRS)
        keep_set = signal("keep_set")
        xq_high = signal("xq_high", KD); xq_low = signal("xq_low", KD); xq_done = signal("xq_done", KD)
        xq_placed = signal("xq_placed", 12, 16); xkv_placed = signal("xkv_placed", 2, 16)
        sc_done = signal("sc_done", NT * NG); sc_max = signal("sc_max", NT * NG)
        mx_turned = signal("mx_turned"); mx_kept = signal("mx_kept"); mx_spread = signal("mx_spread")
        pr_done = signal("pr_done", CHUNKS); pr_exp = signal("pr_exp", CHUNKS)
        pr_high = signal("pr_high", CHUNKS)
        pr_low = [signal(f"pr_low{n}", CHUNKS // 2) for n in range(2)]
        xk_const = signal("xk_const"); weighed = signal("weighed", 2 * NG)
        xo_rec = signal("xo_rec", NG); xo_coef = signal("xo_coef", NG)
        xo_kept = signal("xo_kept", NG); xo_sum = signal("xo_sum", NG); xo_added = signal("xo_added", NG)
        ln = [[signal(f"ln{i}_stats", NT), signal(f"ln{i}_mv", NT), signal(f"ln{i}_root", ROOT_STEPS),
               signal(f"ln{i}_out", NT)] for i in range(3)]
        x2_turned = signal("x2_turned", 2); x2_high = signal("x2_high", 2); x2_low = signal("x2_low", 2)
        gl_done = signal("gl_done"); gl_exp = signal("gl_exp"); route = signal("route", ROUTE_STEPS)
        gw_loaded = [signal("gw_loaded0", 9, 16), signal("gw_loaded1", 8, 16)]
        dw_loaded = [signal("dw_loaded0", 5, 16)] + [signal(f"dw_loaded{r}", 4, 16) for r in (1, 2, 3)]
        g_done = signal("g_done", EXPERTS); u_done = signal("u_done", EXPERTS)
        silu = signal("silu", EXPERTS); hid_ready = signal("hid_ready", EXPERTS)
        h_high = signal("h_high", EXPERTS); h_low = signal("h_low", EXPERTS)
        down_done = signal("down_done", 2 * EXPERTS); summed = signal("summed", 2 * EXPERTS)
        out_stored = signal("out_stored", 1, 16)
        xin_loaded = signal("xin_loaded", 1, 16)
        wo_done = signal("wo_done", NT); x1_added = signal("x1_added", NT)
        x1_turned = signal("x1_turned", 2); x1_high = signal("x1_high", 2); x1_low = signal("x1_low", 2)
        resid_set = signal("resid_set")

        def flat(t):
            return t.rearrange("p k n -> p (k n)") if len(t.shape) == 3 else t

        pieces = [(wv[0:P, :], w_v[:, 0, 0, :], w_v[:, 1, 0, :]), (wv[P:D, :], w_v[:, 0, 1, :], w_v[:, 1, 1, :]),
                  (wq[0:P, :], w_q[:, 0, 0, :], w_q[:, 1, 0, :]), (wq[P:D, :], w_q[:, 0, 1, :], w_q[:, 1, 1, :]),
                  (wk[0:P, :], w_k[:, 0, 0, :], w_k[:, 1, 0, :]), (wk[P:D, :], w_k[:, 0, 1, :], w_k[:, 1, 1, :]),
                  None]
        QKV_PIECES = FEAT_PIECE = len(pieces) - 1
        for half in range(2):
            rows = wo.rearrange("(c p) n -> p c n", p=P)[:, 4 * half:4 * half + 4, :]
            pieces.append((rows, w_o[:, 0, 4 * half:4 * half + 4, :], w_o[:, 1, 4 * half:4 * half + 4, :]))
        pieces.append((xwqT.rearrange("(k p) n -> p k n", p=P), w_xq[:, 0, :, :], w_xq[:, 1, :, :]))
        pieces.append((gate_wT.rearrange("(k p) n -> p k n", p=P), w_gate[:, 0, :, :], w_gate[:, 1, :, :]))
        LATE_PIECES = len(pieces) - FEAT_PIECE - 1

        def loads_before(n):
            return n // 2 + 1 + (n >= FEAT_PIECE and n % 2 == FEAT_PIECE % 2)

        def piece_stage(n, like):
            shape = like.shape
            cols = 1
            for d in shape[1:]:
                cols *= d
            v = w_stage[0:shape[0], n % 2, 0:cols]
            return v.rearrange("p (k n) -> p k n", k=shape[1]) if len(shape) == 3 else v

        block = stack.enter_context(nc.Block())

        @block.sync
        def _(sp):
            def load_piece(n):
                if n >= 2:
                    sp.wait_ge(*w_high(0, n - 1))
                    sp.wait_ge(*w_low(0, n - 1))
                if n == FEAT_PIECE:
                    for parity in range(2):
                        rows = slice(HD * parity, HD * parity + HD)
                        sp.dma_start(w_stage[rows, n % 2, 0:NF], wfeat).then_inc(w_loaded[n % 2].sem, 16)
                else:
                    src, high, _ = pieces[n]
                    sp.dma_start(piece_stage(n, high), src).then_inc(w_loaded[n % 2].sem, 16)

            def load_x(ab):
                sp.dma_start(x_stage[:, :, :], xT[:, :, bass.ts(ab, TB)]).then_inc(xs_loaded.sem, 16)

            sp.dma_start(x_stage[:, :, :], xT[:, :, 0:TB]).then_inc(xs_loaded.sem, 16)
            for n in range(4):
                load_piece(n)
            for src, dst in ((ctxT, ctx_sb), (xwkT, xwk_sb), (xwvT, xwv_sb)):
                sp.dma_start(dst, src.rearrange("(k p) n -> p k n", p=P)).then_inc(ctx_loaded.sem, 16)
            for n in range(4, FEAT_PIECE + 1):
                load_piece(n)
            for n, v in enumerate((lam_q1, lam_k1, lam_q2, lam_k2)):
                sp.dma_start(lam_in[:, n, :], v.partition_broadcast(P)).then_inc(c_loaded.sem, 16)
            sp.dma_start(bias[:, :], e_bias.partition_broadcast(P)).then_inc(c_loaded.sem, 16)

            sp.wait_ge(*zeros_v(0, 1))
            for b in range(B):
                sp.dma_start(xv_scr[b], xv[:, :, :, :, :]).then_inc(zero_stored.sem, 16)
            key_parts, value_parts = [], []
            for b in range(B):
                for m in range(KD):
                    for part, row in ((0, 0), (0, 32), (1, 64)):
                        for q in range(4):
                            key_parts.append((xk_scr[b, row:row + 32, 4 * m + q, :],
                                              kb_hl[32 * q:32 * q + 32, KD * b + m, part, :]))
                for j in range(GH):
                    n0 = 0
                    while n0 < CTX:
                        r = CTX * j + n0
                        rows = min(CTX - n0, P - r % P)
                        for part in range(2):
                            value_parts.append((
                                xv_scr[b, r % P:r % P + rows, :, r // P, part, (XV + 1) * j:(XV + 1) * (j + 1)],
                                v_ext[n0:n0 + rows, part, b, :, :].rearrange("n (g i) d -> n g i d", i=2)[:, :, j // 2, :]))
                        n0 += rows
            ctx_parts = key_parts + value_parts
            n_ctx = len(ctx_parts)

            def attention(ab):
                sp.wait_ge(*x_high(ab, 1))
                sp.wait_ge(*x_low(ab, 1))
                load_x((ab + 1) % NBLK)

            def load_tail(ab, fb):
                if fb is not None:
                    sp.wait_ge(*resid_set(fb, 1))
                    sp.dma_start(nxt[:, :, :], x[:, ab, :, :]).then_inc(xin_loaded.sem, 16)
                    sp.wait_ge(*weighed(fb, 2 * NG))
                else:
                    sp.wait_ge(*ctx_stored(0, n_ctx))
                    sp.wait_ge(*xk_const(0, 2))
                    sp.dma_start(nxt[:, :, :], x[:, ab, :, :]).then_inc(xin_loaded.sem, 16)
                sp.dma_start(xk[0:96, :, 0:GN], xk_scr[ab // BLK_PER_BATCH]).then_inc(xkv_placed.sem, 16)
                sp.dma_start(xv[:, :, :, :, :], xv_scr[ab // BLK_PER_BATCH]).then_inc(xkv_placed.sem, 16)

            def place_queries(ab):
                sp.wait_ge(*xq_high(ab, KD))
                sp.wait_ge(*xq_low(ab, KD))
                for part, row in ((0, 0), (1, 32), (0, 64)):
                    for q in range(4):
                        sp.dma_start(xq[row:row + 32, q:NG:4, :], xq_hl[32 * q:32 * q + 32, part, :, :]
                                     ).then_inc(xq_placed.sem, 16)

            def ffn(fb, ab):
                for e in range(EXPERTS):
                    if e >= 2:
                        sp.wait_ge(*u_done(fb, e - 1))
                    sp.dma_start(gu_w[:, e % 2, :, :], ffn_scr[e, :, :, 0:2 * D]).then_inc(gw_loaded[e % 2].sem, 16)
                    if e >= 4:
                        sp.wait_ge(*down_done(fb, 2 * (e - 3)))
                    sp.dma_start(down_w[:, e % 4, :, :], ffn_scr[e, :, :, 2 * D:FW]).then_inc(dw_loaded[e % 4].sem, 16)
                    if e == 1 and ab is not None:
                        load_tail(ab, fb)
                if ab is not None:
                    place_queries(ab)

            def store(fb):
                sp.wait_ge(*ln[2][3](fb, NT))
                sp.dma_start(out[:, fb, :, :], resid[:, :, :]).then_inc(out_stored.sem, 16)

            def move_low(n, ab):
                sp.wait_ge(*p_sql(ab, n + 1))
                pair = qk[:, n % 2, n // 2 % 2, :, :, :]
                for head in range(2):
                    sp.dma_start(pair[low_rows[head], head, :, :], low_parts[high_rows[head], n % 2, :, :]
                                 ).then_inc(low_moved[n % 4].sem, 16)

            attention(0)
            for n in range(2):
                move_low(n, 0)
            for e in range(EXPERTS):
                if e >= 2:
                    sp.wait_ge(*fs_high(0, e - 1))
                    sp.wait_ge(*fs_low(0, e - 1))
                sp.dma_start(fs_in[:, e % 2, :], ffn_w[e]).then_inc(fs_loaded[e % 2].sem, 16)
                if e < LATE_PIECES:
                    load_piece(FEAT_PIECE + 1 + e)
                if e + 2 < H:
                    move_low(e + 2, 0)
                if e >= 1:
                    sp.wait_ge(*fs_high(0, e))
                    sp.wait_ge(*fs_low(0, e))
                    sp.dma_start(ffn_scr[e - 1], fs_out[:, (e - 1) % 2, :, :]
                                 ).then_inc(fs_stored[(e - 1) % 2].sem, 16)
                if e == 3:
                    sp.wait_ge(*kb_high(0, 2 * B))
                    sp.wait_ge(*kb_low(0, 2 * B))
                    sp.wait_ge(*v_copied(0, 2 * B + 2))
                    sp.wait_ge(*zero_stored(0, B))
                if e >= 3:
                    each = -(-n_ctx // (EXPERTS - 3))
                    for to, part in ctx_parts[each * (e - 3):each * (e - 2)]:
                        sp.dma_start(to, part).then_inc(ctx_stored.sem, 16)
            sp.wait_ge(*fs_high(0, EXPERTS))
            sp.wait_ge(*fs_low(0, EXPERTS))
            sp.dma_start(ffn_scr[EXPERTS - 1], fs_out[:, (EXPERTS - 1) % 2, :, :]
                         ).then_inc(fs_stored[(EXPERTS - 1) % 2].sem, 16)
            sp.wait_ge(*fs_stored[0](0, (EXPERTS + 1) // 2))
            sp.wait_ge(*fs_stored[1](0, EXPERTS // 2))
            load_tail(0, None)
            place_queries(0)
            sp.sem_inc(out_stored.sem, 16)
            with sp.Fori(0, NBLK - 1) as i:
                attention(i + 1)
                for n in range(H):
                    move_low(n, i + 1)
                ffn(i, i + 1)
                store(i)
            ffn(NBLK - 1, None)
            store(NBLK - 1)
            sp.wait_ge(*xs_loaded(0, NBLK + 1))
            sp.wait_ge(*out_stored(0, NBLK + 1))

        @block.gpsimd
        def _(pool):
            pool.memset(ident[:, :], 0.0).then_inc(consts.sem, 1)
            pool.memset(causal[:, :], 1.0).then_inc(consts.sem, 1)
            pool.memset(before_e[:, :, :], 1.0).then_inc(consts.sem, 1)
            pool.memset(before_g[:, :, :], 1.0).then_inc(consts.sem, 1)
            pool.memset(own_half[:, :], 1.0).then_inc(consts.sem, 1)
            pool.wait_ge(consts.sem, 5)
            pool.affine_select(out=ident[:, :], in_=ident[:, :], compare_op=ALU.not_equal, fill=1.0, base=0,
                               pattern=[[-1, P]], channel_multiplier=1).then_inc(consts.sem, 1)
            pool.affine_select(out=causal[:, :], in_=causal[:, :], compare_op=ALU.is_ge, fill=0.0, base=0,
                               pattern=[[1, P]], channel_multiplier=-1).then_inc(consts.sem, 1)
            pool.affine_select(out=before_e[:, :, :], in_=before_e[:, :, :], compare_op=ALU.is_gt, fill=0.0, base=0,
                               pattern=[[1, NE], [-1, NE]], channel_multiplier=0).then_inc(consts.sem, 1)
            pool.affine_select(out=before_g[:, :, :], in_=before_g[:, :, :], compare_op=ALU.is_gt, fill=0.0, base=0,
                               pattern=[[1, NGROUP], [-1, NGROUP]], channel_multiplier=0).then_inc(consts.sem, 1)
            pool.affine_select(out=own_half[:, :], in_=own_half[:, :], compare_op=ALU.is_ge, fill=0.0, base=0,
                               pattern=[[-XD, P // XD]], channel_multiplier=1).then_inc(consts.sem, 1)
            pool.wait_ge(consts.sem, 10)
            pool.affine_select(out=own_half[:, :], in_=own_half[:, :], compare_op=ALU.is_ge, fill=0.0, base=XD - 1,
                               pattern=[[XD, P // XD]], channel_multiplier=-1).then_inc(consts.sem, 1)

            pool.memset(xk[:, :, :], 0.0).then_inc(xk_const.sem, 1)
            pool.wait_ge(*xk_const(0, 1))
            pool.affine_select(out=xk[:, :, 0:GN].rearrange("p g (j n) -> p g j n", j=GH),
                               in_=xk[:, :, 0:GN].rearrange("p g (j n) -> p g j n", j=GH),
                               compare_op=ALU.not_equal, fill=-MAX_SCALE, base=-96,
                               pattern=[[-GH, NG], [-1, GH], [0, CTX]], channel_multiplier=1).then_inc(xk_const.sem, 1)

            def project_job(n, ab):
                pool.wait_ge(*p_sqh(ab, n + 1))
                pool.tensor_tensor(low_parts[:, n % 2, 1, :], square[:, n % 2, :],
                                   qk[:, n % 2, n // 2 % 2, 0, 1, :], ALU.subtract).then_inc(p_sql.sem, 1)

            def shared(ab, cb):
                for kind, n in opening(ab is not None, cb is not None):
                    if kind == "project":
                        project_job(n, ab)
                for s in range(LAST):
                    for kind, n in steps(s, ab is not None, cb is not None):
                        if kind == "project":
                            project_job(n, ab)
                        elif kind == "probs" and (ab is not None or n % 2 == 0):
                            pool.wait_ge(*pr_exp(cb, n + 1))
                            pool.tensor_tensor(prob[:, n % RING, 1, :], prob_full[:, n % 2, :], prob[:, n % RING, 0, :],
                                               ALU.subtract).then_inc(pr_low[n % 2].sem, 1)
                        elif kind == "weigh" and n % 2 == 1:
                            g = n // 2
                            if g == 0:
                                pool.wait_ge(*resid_set(cb, 1))
                            pool.wait_ge(*xo_kept(cb, g + 1))
                            pool.tensor_tensor(xsum[:, g % 2, :, :], xterm[:, g % 2, :, 0, :],
                                               xterm[:, g % 2, :, 1, :], ALU.add).then_inc(xo_sum.sem, 1)
                            pool.wait_ge(*xo_sum(cb, g + 1))
                            cols = slice(32 * g, 32 * g + 32)
                            pool.tensor_tensor(resid[:, :, cols], resid[:, :, cols],
                                               xsum[:, g % 2, :, :].rearrange("p (c h) d -> p c (h d)", c=NT),
                                               ALU.add).then_inc(xo_added.sem, 1)

            def ffn(fb):
                for e in range(EXPERTS):
                    pool.wait_ge(*h_high(fb, e + 1))
                    pool.tensor_tensor(hT[:, e % 3, 1, :], hid[:, e % 2, :], hT[:, e % 3, 0, :],
                                       ALU.subtract).then_inc(h_low.sem, 1)

            shared(0, None)
            with pool.Fori(0, NBLK - 1) as i:
                shared(i + 1, i)
                ffn(i)
            shared(None, NBLK - 1)
            ffn(NBLK - 1)

        @block.scalar
        def _(act):
            def keep_values(n, ab):
                act.wait_ge(*v_done(ab, n + 1))
                act.activation(v1[:, n // 2, H // 2 * (n % 2):H // 2 * (n % 2 + 1), 0:HD],
                               ps_a[n % 2][:, :].rearrange("p (h d) -> p h d", d=HD), ACT.Copy,
                               scale=1 / W_SCALE).then_inc(v_kept.sem, 1)

            def split_piece(n):
                act.wait_ge(*w_loaded[n % 2](0, loads_before(n)))
                if n == FEAT_PIECE:
                    act.activation(w_feat_high[:, :], w_stage[:, n % 2, 0:NF], ACT.Copy).then_inc(w_high.sem, 1)
                else:
                    act.activation(pieces[n][1], piece_stage(n, pieces[n][1]), ACT.Copy,
                                   scale=W_SCALE).then_inc(w_high.sem, 1)

            for n in range(2):
                split_piece(n)
            for n in range(2, QKV_PIECES + 1):
                keep_values(n - 2, 0)
                split_piece(n)
            for n in range(QKV_PIECES - 1, 2 * NT):
                keep_values(n, 0)

            def turn_output_job(n, ab):
                act.wait_ge(*yt_done(ab, n + 1))
                act.activation(yT[:, 0, n, :], ps_turn[:, :], ACT.Copy).then_inc(yt_high.sem, 1)

            def project_job(n, ab, bank):
                act.wait_ge(*p_done(ab, n + 1))
                pair = qk[:, n % 2, n // 2 % 2, :, :, :]
                act.activation(pair[:, 0, 0, :], bank[:, :], ACT.Copy, scale=1 / W_SCALE)
                act.activation(pair[HD:P, 1, 0, :], bank[HD:P, :], ACT.Copy, scale=1 / W_SCALE)
                act.activation(pair[HD:P, 1, 1, :], bank[HD:P, :], ACT.Square, scale=1 / W_SCALE)
                if n >= 2:
                    act.wait_ge(*p_sql(ab, n - 1))
                act.activation(square[:, n % 2, :], bank[:, :], ACT.Square,
                               scale=1 / W_SCALE).then_inc(p_sq.sem, 1)

            def shared(ab, cb):
                for kind, n in opening(ab is not None, cb is not None):
                    if kind == "values" and cb is not None:
                        keep_values(n, ab)
                    if kind == "project":
                        project_job(n, ab, ps_a[n])
                ring = ring_banks(ab)
                a_jobs = 0
                for s in range(LAST):
                    for kind, n in steps(s, ab is not None, cb is not None):
                        if kind == "project":
                            project_job(n, ab, ring[a_jobs % len(ring)])
                        elif kind == "turn keys":
                            act.wait_ge(*turned_k(ab, n + 1))
                            act.activation(kt[:, n % 2, :, :].rearrange("p c f -> p (c f)"), ps_turn[:, :],
                                           ACT.Copy).then_inc(kt_kept.sem, 1)
                        elif kind == "q features":
                            act.wait_ge(*qf_done(ab, n + 1))
                            act.activation(qf[:, n % 4, :], ps_f[:, :], ACT.Exp).then_inc(qf_exp.sem, 1)
                        elif kind == "k features":
                            act.wait_ge(*kf_done(ab, n + 1))
                            act.activation(kf[:, n % 2, :], ps_f[:, :], ACT.Exp).then_inc(kf_exp.sem, 1)
                        elif kind == "turn maxima":
                            act.wait_ge(*out_stored(cb, 1))
                            act.activation(resid[:, :, :], nxt[:, :, :], ACT.Copy).then_inc(resid_set.sem, 1)
                        elif kind == "probs":
                            act.wait_ge(*pr_done(cb, n + 1))
                            if n >= RING:
                                act.wait_ge(*weighed(cb, 2 * (n // GC - 1)))
                            bank = ring[a_jobs % len(ring)]
                            act.activation(prob[:, n % RING, 0, :], bank[:, :], ACT.Exp,
                                           scale=float(XD) ** -0.5).then_inc(pr_high.sem, 1)
                            if n >= 2:
                                act.wait_ge(*pr_low[n % 2](cb, n // 2))
                            act.activation(prob_full[:, n % 2, :], bank[:, :], ACT.Exp,
                                           scale=float(XD) ** -0.5).then_inc(pr_exp.sem, 1)
                        elif kind == "turn output":
                            turn_output_job(n, ab)
                        elif kind == "turn cross":
                            act.wait_ge(*x2_turned(cb, n + 1))
                            act.activation(turned[:, 0, :, stream_cols(n)],
                                           ps_turn[:, :].rearrange("p (k t) -> p k t", k=KD),
                                           ACT.Copy).then_inc(x2_high.sem, 1)
                        if kind in ("project", "probs"):
                            a_jobs += 1
                    if cb is None:
                        if 1 <= s < 1 + LATE_PIECES:
                            split_piece(QKV_PIECES + s)
                        if s == 1 + LATE_PIECES:
                            act.wait_ge(*lam_step(0, 2))
                            act.activation(lam_exp[:, :], lam_sum[:, :], ACT.Exp).then_inc(lam_exped.sem, 1)
                        if 1 <= s <= EXPERTS:
                            e = s - 1
                            act.wait_ge(*fs_loaded[e % 2](0, e // 2 + 1))
                            if e >= 2:
                                act.wait_ge(*fs_stored[e % 2](0, e // 2))
                            act.activation(fs_out[:, e % 2, 0, :], fs_in[:, e % 2, :], ACT.Copy,
                                           scale=W_SCALE).then_inc(fs_high.sem, 1)

            def ffn(fb, ab):
                act.wait_ge(*gl_done(fb, 1))
                act.activation(ge[:, :], ps_turn[:, 0:NT * NE], ACT.Exp, scale=-1 / W_SCALE).then_inc(gl_exp.sem, 1)
                for e in range(EXPERTS + 1):
                    if e < EXPERTS:
                        act.wait_ge(*g_done(fb, e + 1))
                        if e >= 2:
                            act.wait_ge(*h_low(fb, e - 1))
                        act.activation(hid[:, e % 2, :], (ps_a[0], ps_f)[e % 2][:, :], ACT.Silu,
                                       scale=1 / W_SCALE).then_inc(silu.sem, 1)
                    if e >= 1:
                        act.wait_ge(*hid_ready(fb, e))
                        if e >= 4:
                            act.wait_ge(*down_done(fb, 2 * (e - 3)))
                        act.activation(hT[:, (e - 1) % 3, 0, :], hid[:, (e - 1) % 2, :],
                                       ACT.Copy).then_inc(h_high.sem, 1)
                    if ab is not None:
                        for kind, n in late_jobs(e) + tail_jobs(e):
                            tail_job(kind, n, ab, False)

            def tail_job(kind, n, ab, alone):
                if kind == "turn output":
                    turn_output_job(n, ab)
                elif kind == "turn stream":
                    act.wait_ge(*x1_turned(ab, n + 1))
                    act.activation(turned_next[:, 0, :, stream_cols(n)],
                                   tail_bank(kind, n, alone)[:, :].rearrange("p (k t) -> p k t", k=KD),
                                   ACT.Copy).then_inc(x1_high.sem, 1)
                elif kind == "queries":
                    act.wait_ge(*xq_done(ab, n + 1))
                    act.activation(xq_hl[:, 0, n, :], tail_bank(kind, n, alone)[:, :], ACT.Copy,
                                   scale=1 / W_SCALE).then_inc(xq_high.sem, 1)

            shared(0, None)
            for kind, n in tail_jobs(None):
                tail_job(kind, n, 0, True)
            with act.Fori(0, NBLK - 1) as i:
                shared(i + 1, i)
                ffn(i, i + 1)
            shared(None, NBLK - 1)
            ffn(NBLK - 1, None)

        @block.vector
        def _(dve):
            dve.memset(xv[:, :, :, :, :], 0.0).then_inc(zeros_v.sem, 1)
            dve.memset(w_feat_low[:, :, :], 0.0).then_inc(zeros_v.sem, 1)
            dve.memset(neg_half[:, :], -0.5).then_inc(v_ones.sem, 1)
            dve.memset(v1[:, :, :, HD:V1], 1.0).then_inc(v_ones.sem, 1)
            dve.memset(state[:, :, :], 0.0).then_inc(v_ones.sem, 1)
            dve.memset(keep[:, :], 0.0).then_inc(v_ones.sem, 1)
            dve.memset(coef[:, :, :], 1.0).then_inc(v_ones.sem, 1)

            def split_x(ab):
                dve.wait_ge(*xs_loaded(ab, 1))
                dve.tensor_copy(x_split[:, 0, :, :], x_stage[:, :, :]).then_inc(x_high.sem, 1)
                dve.wait_ge(*x_high(ab, 1))
                dve.tensor_tensor(x_split[:, 1, :, :], x_stage[:, :, :], x_split[:, 0, :, :],
                                  ALU.subtract).then_inc(x_low.sem, 1)

            def split_low(n):
                _, high, low = pieces[n]
                dve.wait_ge(*w_high(0, n + 1))
                dve.scalar_tensor_tensor(low, piece_stage(n, high), W_SCALE, high, ALU.mult,
                                         ALU.subtract).then_inc(w_low.sem, 1)

            def setup_step(s):
                if s == 0:
                    dve.memset(v_ext[0:CTX, 0, :, :, XV:XV + 1], 1.0).then_inc(v_copied.sem, 1)
                    dve.memset(v_ext[0:CTX, 1, :, :, XV:XV + 1], 0.0).then_inc(v_copied.sem, 1)
                    dve.wait_ge(*xkv_done(0, 1))
                    for b in range(B):
                        v_full = ps_st[0:CTX, D * b:D * b + D].rearrange("p (h d) -> p h d", d=XV)
                        dve.tensor_copy(v_ext[0:CTX, 0, b, :, 0:XV], v_full).then_inc(v_copied.sem, 1)
                        dve.wait_ge(*v_copied(0, 2 * b + 3))
                        dve.tensor_tensor(v_ext[0:CTX, 1, b, :, 0:XV], v_full, v_ext[0:CTX, 0, b, :, 0:XV],
                                          ALU.subtract).then_inc(v_copied.sem, 1)
                    dve.wait_ge(consts.sem, 11)
                    dve.tensor_reduce(own_row[:, :, 0], own_half[:, :].rearrange("p (q j) -> p j q", j=GH), AX.X,
                                      ALU.add).then_inc(own_ready.sem, 1)
                    dve.wait_ge(*own_ready(0, 1))
                if s in (1, 2):
                    for n in (2 * s - 2, 2 * s - 1):
                        if n:
                            dve.wait_ge(*kb_low(0, n))
                        dve.tensor_tensor(kb_full, ps_xo[:, CTX * n:CTX * n + CTX].unsqueeze(1).to_broadcast([P, GH, CTX]),
                                          own_row[:, :, :].to_broadcast([P, GH, CTX]), ALU.mult).then_inc(kb_masked.sem, 1)
                        dve.wait_ge(*kb_masked(0, n + 1))
                        flat_full = kb_full.rearrange("p j n -> p (j n)")
                        dve.tensor_copy(kb_hl[:, n, 0, :], flat_full).then_inc(kb_high.sem, 1)
                        dve.wait_ge(*kb_high(0, n + 1))
                        dve.tensor_tensor(kb_hl[:, n, 1, :], flat_full, kb_hl[:, n, 0, :],
                                          ALU.subtract).then_inc(kb_low.sem, 1)
                if 1 <= s < 1 + LATE_PIECES:
                    split_low(QKV_PIECES + s)
                if s == LATE_PIECES:
                    dve.wait_ge(*c_loaded(0, 5))
                    dve.tensor_tensor(lam_prod[:, :, :], lam_in[:, 0:4:2, :], lam_in[:, 1:4:2, :], ALU.mult
                                      ).then_inc(lam_step.sem, 1)
                    dve.wait_ge(*lam_step(0, 1))
                    dve.tensor_reduce(lam_sum[:, :], lam_prod[:, :, :], AX.X, ALU.add).then_inc(lam_step.sem, 1)
                if s == 2 + LATE_PIECES:
                    dve.wait_ge(*lam_exped(0, 1))
                    dve.tensor_tensor(lam_sum[:, 0:1], lam_exp[:, 1:2], lam_exp[:, 0:1], ALU.subtract
                                      ).then_inc(lam_step.sem, 1)
                    dve.wait_ge(*lam_step(0, 3))
                    dve.tensor_scalar(coef[:, 1:XV:2, 0], lam_sum[:, 0:1].to_broadcast([P, XV // 2]), -LAMBDA_INIT,
                                      None, ALU.add).then_inc(coef_ready.sem, 1)
                if 1 <= s <= EXPERTS:
                    e = s - 1
                    dve.wait_ge(*fs_high(0, e + 1))
                    dve.scalar_tensor_tensor(fs_out[:, e % 2, 1, :], fs_in[:, e % 2, :], W_SCALE,
                                             fs_out[:, e % 2, 0, :], ALU.mult, ALU.subtract).then_inc(fs_low.sem, 1)

            split_x(0)
            for n in range(QKV_PIECES):
                split_low(n)
            dve.wait_ge(*w_high(0, FEAT_PIECE + 1))
            dve.wait_ge(*zeros_v(0, 2))
            for head, rows in enumerate(high_rows):
                last = dve.tensor_tensor(w_feat_low[rows, head, :], w_stage[rows, FEAT_PIECE % 2, 0:NF],
                                         w_feat_high[rows, :], ALU.subtract)
            last.then_inc(w_low.sem, 1)

            def statistics(which, blk, c, stream):
                stats, mean_var = ln[which][:2]
                dve.bn_stats(st[:, c, :], stream[:, c, :]).then_inc(stats.sem, 1)
                dve.wait_ge(*stats(blk, c + 1))
                dve.sem_inc(held.sem, 1)
                dve.bn_aggr(mv[:, c, :], st[:, c, :]).then_inc(mean_var.sem, 1)

            def inverse_root(which, blk):
                step = ln[which][2]
                n = [0]

                def link(ins):
                    n[0] += 1
                    ins.then_inc(step.sem, 1)
                    dve.wait_ge(*step(blk, n[0]))

                v, a, r = root_v[:, :, 0], root_a[:, :, 0], rstd[:, :, 0]
                link(dve.tensor_scalar(v, mv[:, :, 1], LN_EPS, None, ALU.add))
                link(dve.tensor_scalar(a.bitcast(I32), v.bitcast(I32), 1, None, ALU.logical_shift_right))
                link(dve.tensor_scalar(r.bitcast(I32), a.bitcast(I32), -1.0, float(0x5F3759DF), ALU.mult, ALU.add))
                for _ in range(3):
                    link(dve.tensor_tensor(a, r, r, ALU.mult))
                    link(dve.scalar_tensor_tensor(a, a, -0.5, v, ALU.mult, ALU.mult))
                    link(dve.scalar_tensor_tensor(r, a, 1.5, r, ALU.add, ALU.mult))

            def norm(which, blk, stream, have_statistics=False):
                if not have_statistics:
                    for c in range(NT):
                        statistics(which, blk, c, stream)
                dve.wait_ge(*ln[which][1](blk, NT))
                inverse_root(which, blk)
                for c in range(NT):
                    dve.tensor_scalar(stream[:, c, :], stream[:, c, :], mv[:, c, 0:1], rstd[:, c, :], ALU.subtract,
                                      ALU.mult).then_inc(ln[which][3].sem, 1)

            def project_job(n, ab, bank):
                pair = qk[:, n % 2, n // 2 % 2, :, :, :]
                dve.wait_ge(*p_sq(ab, n + 1))
                if n >= 2:
                    dve.wait_ge(*low_moved[(n - 2) % 4](ab, 2 * ((n - 2) // 4 + 1)))
                dve.scalar_tensor_tensor(low_parts[:, n % 2, 0, :], bank[:, :], 1 / W_SCALE, pair[:, 0, 0, :],
                                         ALU.mult, ALU.subtract).then_inc(p_low.sem, 1)
                dve.tensor_copy(pair[:, 0, 1, :], square[:, n % 2, :]).then_inc(p_sqh.sem, 1)

            def shared(ab, cb):
                first = cb is None
                ring = ring_banks(ab)
                a_jobs = 0
                for kind, n in opening(ab is not None, cb is not None):
                    if kind == "scores":
                        maximum_job(n, cb)
                    if kind == "project":
                        project_job(n, ab, ps_a[n])
                for s in range(LAST):
                    for kind, n in steps(s, ab is not None, cb is not None):
                        if kind == "project":
                            project_job(n, ab, ring[a_jobs % len(ring)])
                        elif kind == "attend":
                            dve.wait_ge(*att_done(ab, n + 1))
                            dve.tensor_tensor(att[:, n % 3, :, :], ps_att[:, :].rearrange("p (c t) -> p c t", t=P),
                                              causal[:, :].unsqueeze(1).to_broadcast([P, NT, P]),
                                              ALU.mult).then_inc(att_kept.sem, 1)
                        elif kind == "state":
                            r = run[:, n % 2, :, :]
                            dve.wait_ge(*st_done(ab, n + 1))
                            dve.tensor_scalar(r[:, 0, :], state[:, n, :], keep[:, 0:1], None, ALU.mult
                                              ).then_inc(run_step.sem, 1)
                            for c in range(1, NT + 1):
                                dve.wait_ge(*run_step(ab, 4 * n + c))
                                dst = r[:, c, :] if c < NT else state[:, n, :]
                                dve.tensor_tensor(dst, r[:, c - 1, :], ps_st[:, V1 * (c - 1):V1 * c], ALU.add
                                                  ).then_inc((run_step if c < NT else run_ready).sem, 1)
                        elif kind == "output":
                            output_job(n, ab)
                        elif kind == "turn output":
                            turn_output_job(n, ab)
                        elif kind == "scores":
                            maximum_job(n, cb)
                        elif kind == "probs" and ab is None and n % 2 == 1:
                            dve.wait_ge(*pr_exp(cb, n + 1))
                            dve.tensor_tensor(prob[:, n % RING, 1, :], prob_full[:, n % 2, :], prob[:, n % RING, 0, :],
                                              ALU.subtract).then_inc(pr_low[1].sem, 1)
                        elif kind == "turn maxima":
                            dve.wait_ge(*mx_turned(cb, 1))
                            dve.tensor_scalar(xq[96:P, 0, :], ps_xo[0:XHALVES, :], 1 / MAX_SCALE, None, ALU.mult
                                              ).then_inc(mx_kept.sem, 1)
                            dve.wait_ge(*mx_kept(cb, 1))
                            dve.tensor_copy(xq[96:P, 1:NG, :], xq[96:P, 0:1, :].to_broadcast([P - 96, NG - 1, TB])
                                            ).then_inc(mx_spread.sem, 1)
                        elif kind == "weigh" and n % 2 == 1:
                            g = n // 2
                            o = weigh_bank(ab, g)[:, 0:NT * GV].rearrange("p (h v) -> p h v", v=XV + 1)
                            dve.wait_ge(*weighed(cb, 2 * g + 2))
                            dve.reciprocal(xrec[:, g % 2, :, :], o[:, :, XV:XV + 1]).then_inc(xo_rec.sem, 1)
                            dve.wait_ge(*xo_rec(cb, g + 1))
                            dve.tensor_tensor(xrec2[:, g % 2, :, :], xrec[:, g % 2, :, :], coef[:, :, :],
                                              ALU.mult).then_inc(xo_coef.sem, 1)
                            dve.wait_ge(*xo_coef(cb, g + 1))
                            if g >= 2:
                                dve.wait_ge(*xo_sum(cb, g - 1))
                            dve.tensor_tensor(xterm[:, g % 2, :, :, :].rearrange("p h i d -> p (h i) d"),
                                              o[:, :, 0:XV], xrec2[:, g % 2, :, :].to_broadcast([P, XV, XV]),
                                              ALU.mult).then_inc(xo_kept.sem, 1)
                        elif kind == "norm":
                            dve.wait_ge(*xo_added(cb, NG))
                            norm(1, cb, resid)
                        elif kind == "turn cross":
                            dve.wait_ge(*x2_high(cb, n + 1))
                            dve.tensor_tensor(turned[:, 1, :, stream_cols(n)],
                                              ps_turn[:, :].rearrange("p (k t) -> p k t", k=KD),
                                              turned[:, 0, :, stream_cols(n)], ALU.subtract).then_inc(x2_low.sem, 1)
                        if kind in ("project", "probs"):
                            a_jobs += 1
                    if first:
                        setup_step(s)

            def maximum_job(n, cb):
                c, g = n // NG, n % NG
                dve.wait_ge(*sc_done(cb, n + 1))
                dve.tensor_reduce(xmax[:, c, GH * g:GH * g + GH],
                                  score_banks[n % 4][:, 0:GN].rearrange("p (j n) -> p j n", j=GH),
                                  AX.X, ALU.max).then_inc(sc_max.sem, 1)

            def output_job(n, ab):
                o = output_bank(n)[:, 0:NT * V1].rearrange("p (c v) -> p c v", v=V1)
                dve.wait_ge(*o_done(ab, n + 1))
                dve.tensor_scalar(den[:, n % 2, :, :], o[:, :, HD:V1], EPS, None, ALU.add).then_inc(o_den.sem, 1)
                dve.wait_ge(*o_den(ab, n + 1))
                dve.reciprocal(rec[:, n % 2, :, :], den[:, n % 2, :, :]).then_inc(o_rec.sem, 1)
                dve.wait_ge(*o_rec(ab, n + 1))
                dve.tensor_tensor(y[:, n // 2 % 2, :, HD * (n % 2):HD * (n % 2) + HD], o[:, :, 0:HD],
                                  rec[:, n % 2, :, :].to_broadcast([P, NT, HD]), ALU.mult).then_inc(o_kept.sem, 1)

            def turn_output_job(n, ab):
                dve.wait_ge(*yt_high(ab, n + 1))
                dve.tensor_tensor(yT[:, 1, n, :], ps_turn[:, :], yT[:, 0, n, :], ALU.subtract).then_inc(yt_low.sem, 1)

            def toggle_keep():
                dve.tensor_scalar(keep[:, :], keep[:, :], -1.0, 1.0, ALU.mult, ALU.add).then_inc(keep_set.sem, 1)

            def ffn(fb, ab):
                done = [0]

                f = "p t e -> p (t e)"

                def link(ins):
                    done[0] += 1
                    ins.then_inc(route.sem, 1)
                    dve.wait_ge(*route(fb, done[0]))

                def routing_groups():
                    dve.wait_ge(*gl_exp(fb, 1))
                    link(dve.tensor_scalar(gd[:, :], ge[:, :], 1.0, None, ALU.add))
                    link(dve.reciprocal(score[:, :, :].rearrange(f), gd[:, :]))
                    link(dve.tensor_tensor(choice[:, :, :], score[:, :, :],
                                           bias[:, :].unsqueeze(1).to_broadcast([P, NT, NE]), ALU.add))
                    two = choice[:, :, :].rearrange("p t (g q i) -> p (t g) q i", g=NGROUP, i=2)
                    link(dve.tensor_tensor(g_max[:, :, :], two[:, :, :, 0], two[:, :, :, 1], ALU.max))
                    link(dve.tensor_tensor(g_min[:, :, :], two[:, :, :, 0], two[:, :, :, 1], ALU.min))
                    link(dve.tensor_tensor(g_a[:, :], g_max[:, :, 0], g_max[:, :, 1], ALU.max))
                    link(dve.tensor_tensor(g_b[:, :], g_max[:, :, 0], g_max[:, :, 1], ALU.min))
                    link(dve.tensor_tensor(g_c[:, :], g_min[:, :, 0], g_min[:, :, 1], ALU.max))
                    link(dve.tensor_tensor(g_d[:, :], g_b[:, :], g_c[:, :], ALU.max))
                    link(dve.tensor_tensor(g_sum[:, :, :].rearrange("p t g -> p (t g)"), g_a[:, :], g_d[:, :], ALU.add))

                def routing_ranks():
                    def ranks(v, gt, eq, before, n, rank):
                        other = v.unsqueeze(2).to_broadcast([P, NT, n, n])
                        own = v.unsqueeze(3).to_broadcast([P, NT, n, n])
                        link(dve.tensor_tensor(gt, other, own, ALU.is_gt))
                        link(dve.tensor_tensor(eq, other, own, ALU.is_equal))
                        link(dve.tensor_tensor(eq, eq, before.unsqueeze(1).to_broadcast([P, NT, n, n]), ALU.mult))
                        link(dve.tensor_tensor(gt, gt, eq, ALU.add))
                        link(dve.tensor_reduce(rank, gt.rearrange("p t i j -> p (t i) j"), AX.X, ALU.add))

                    ranks(g_sum[:, :, :], g_gt[:, :, :, :], g_eq[:, :, :, :], before_g[:, :, :], NGROUP, g_rank[:, :])
                    link(dve.tensor_scalar(g_in[:, :, 0], g_rank[:, :], TOPK_GROUP - 0.5, None, ALU.is_lt))
                    link(dve.tensor_tensor(masked[:, :, :].rearrange("p t (g i) -> p (t g) i", g=NGROUP),
                                           choice[:, :, :].rearrange("p t (g i) -> p (t g) i", g=NGROUP),
                                           g_in[:, :, :].to_broadcast([P, NT * NGROUP, PER_GROUP]), ALU.mult))
                    ranks(masked[:, :, :], e_gt[:, :, :].rearrange("p t (i j) -> p t i j", i=NE),
                          e_eq[:, :, :].rearrange("p t (i j) -> p t i j", i=NE), before_e[:, :, :], NE, e_rank[:, :])

                def routing_weights():
                    link(dve.scalar_tensor_tensor(chosen[:, :, :].rearrange(f), e_rank[:, :], TOPK - 0.5,
                                                  score[:, :, :].rearrange(f), ALU.is_lt, ALU.mult))
                    link(dve.tensor_reduce(w_sum[:, :], chosen[:, :, :], AX.X, ALU.add))
                    link(dve.tensor_scalar(w_sum[:, :], w_sum[:, :], 1e-20, None, ALU.add))
                    link(dve.reciprocal(w_rec[:, :], w_sum[:, :]))
                    link(dve.tensor_scalar(w_rec2[:, :, 0], w_rec[:, :], SCALING / W_SCALE, None, ALU.mult))
                    link(dve.tensor_tensor(weight[:, :, :], chosen[:, :, :],
                                           w_rec2[:, :, :].to_broadcast([P, NT, NE]), ALU.mult))
                    assert done[0] == ROUTE_STEPS

                routing_groups()
                for e in range(EXPERTS + 2):
                    if e < EXPERTS:
                        dve.wait_ge(*u_done(fb, e + 1))
                        dve.wait_ge(*silu(fb, e + 1))
                        dve.scalar_tensor_tensor(hid[:, e % 2, :], (ps_a[1], ps_o)[e % 2][:, :], 1 / W_SCALE,
                                                 hid[:, e % 2, :], ALU.mult, ALU.mult).then_inc(hid_ready.sem, 1)
                    if e >= 2:
                        d = e - 2
                        for half in range(2):
                            bank = down_banks[(2 * d + half) % 3]
                            dve.wait_ge(*down_done(fb, 2 * d + half + 1))
                            if d >= 1:
                                dve.wait_ge(*summed(fb, 2 * (d - 1) + half + 1))
                            for k in range(2):
                                c = 2 * half + k
                                by = 1 / W_SCALE if d == 0 else weight[:, c, d - 1:d]
                                last = dve.scalar_tensor_tensor(resid[:, c, :], bank[:, D * k:D * k + D], by,
                                                                resid[:, c, :], ALU.mult, ALU.add)
                            last.then_inc(summed.sem, 1)
                    if ab is not None:
                        for kind, n in late_jobs(e) + tail_jobs(e):
                            tail_job(kind, n, ab, False)
                    if e == 0:
                        routing_ranks()
                    if e == 1:
                        routing_weights()
                dve.wait_ge(*summed(fb, 2 * EXPERTS))
                toggle_keep()
                norm(2, fb, resid)

            def tail_job(kind, n, ab, alone):
                if kind == "output":
                    output_job(n, ab)
                elif kind == "turn output":
                    turn_output_job(n, ab)
                elif kind == "project out":
                    if n == 0:
                        dve.wait_ge(*xin_loaded(ab, 1))
                    dve.wait_ge(*wo_done(ab, n + 1))
                    dve.scalar_tensor_tensor(nxt[:, n, :], tail_bank(kind, n, alone)[:, 0:D], 1 / W_SCALE,
                                             nxt[:, n, :], ALU.mult, ALU.add).then_inc(x1_added.sem, 1)
                    dve.wait_ge(*x1_added(ab, n + 1))
                    statistics(0, ab, n, nxt)
                elif kind == "norm":
                    norm(0, ab, nxt, have_statistics=True)
                elif kind == "turn stream":
                    dve.wait_ge(*x1_high(ab, n + 1))
                    dve.tensor_tensor(turned_next[:, 1, :, stream_cols(n)],
                                      tail_bank(kind, n, alone)[:, :].rearrange("p (k t) -> p k t", k=KD),
                                      turned_next[:, 0, :, stream_cols(n)], ALU.subtract).then_inc(x1_low.sem, 1)
                elif kind == "queries":
                    dve.wait_ge(*xq_high(ab, n + 1))
                    dve.scalar_tensor_tensor(xq_hl[:, 1, n, :], tail_bank(kind, n, alone)[:, :], 1 / W_SCALE,
                                             xq_hl[:, 0, n, :], ALU.mult, ALU.subtract).then_inc(xq_low.sem, 1)
                elif kind == "split":
                    split_x(ab + 1)

            held = signal("held")
            shared(0, None)
            for kind, n in tail_jobs(None):
                tail_job(kind, n, 0, True)
            toggle_keep()
            with dve.Fori(0, NBLK - 1) as i:
                shared(i + 1, i)
                ffn(i, i + 1)
            shared(None, NBLK - 1)
            ffn(NBLK - 1, None)

        @block.tensor
        def _(pe):
            def three_pass(dst, lhs, rhs, first=True, last=True):
                for n, (i, j) in enumerate(((0, 0), (0, 1), (1, 0))):
                    ins = pe.matmul(dst, lhs(i), rhs(j), start=first and n == 0, stop=last and n == 2)
                return ins

            def cross_keys_values():
                pe.wait_ge(*ctx_loaded(0, 3))
                for b in range(B):
                    for m in range(KD):
                        n = KD * b + m
                        for k in range(KD):
                            pe.matmul(ps_xo[:, CTX * n:CTX * n + CTX], xwk_sb[:, k, P * m:P * m + P],
                                      ctx_sb[:, k, CTX * b:CTX * b + CTX], start=(k == 0), stop=(k == KD - 1))
                for b in range(B):
                    for k in range(KD):
                        last = pe.matmul(ps_st[0:CTX, D * b:D * b + D], ctx_sb[:, k, CTX * b:CTX * b + CTX],
                                         xwv_sb[:, k, :], start=(k == 0), stop=(k == KD - 1))
                last.then_inc(xkv_done.sem, 1)

            def output_job(n, ab):
                pe.wait_ge(*att_kept(ab, n + 1))
                pe.wait_ge(*run_ready(ab, n + 1))
                if n:
                    pe.wait_ge(*o_kept(ab, n))
                for c in range(NT):
                    o = output_bank(n)[:, V1 * c:V1 * c + V1]
                    pe.matmul(o, att[:, n % 3, c, :], v1[:, c, n, :], start=True, stop=False)
                    last = pe.matmul(o, qf[:, n % 4, P * c:P * c + P], run[:, n % 2, c, :], start=False, stop=True)
                last.then_inc(o_done.sem, 1)

            def turn_output_job(n, ab):
                pe.wait_ge(*o_kept(ab, 2 * n + 2))
                for c in range(NT):
                    last = pe.transpose(ps_turn[:, P * c:P * c + P], y[:, n % 2, c, :], ident[:, :])
                last.then_inc(yt_done.sem, 1)

            def score_job(n, cb):
                if n == 0:
                    pe.wait_ge(*keep_set(cb, 1))
                    pe.wait_ge(*xq_placed(cb, 12))
                    pe.wait_ge(*xkv_placed(cb, 2))
                if n >= 4:
                    pe.wait_ge(*sc_max(cb, n - 3))
                c, g = n // NG, n % NG
                pe.matmul(score_banks[n % 4][:, 0:GN], xq[0:96, g, P * c:P * c + P], xk[0:96, g, 0:GN],
                          start=True, stop=True).then_inc(sc_done.sem, 1)

            def project_job(n, ab, cb, bank):
                w = (w_q, w_k)[n % 2]
                if cb is None and n < 2:
                    pe.wait_ge(*w_low(0, 4 + 2 * n))
                for k in range(KD):
                    last = three_pass(bank[:, :], lambda i: w[:, i, k, P * (n // 2):P * (n // 2) + P],
                                      lambda j: x_split[:, j, k, :], k == 0, k == KD - 1)
                last.then_inc(p_done.sem, 1)

            def open_block(ab, cb):
                kept = {}
                if ab is not None:
                    pe.wait_ge(*x_high(ab, 1))
                    pe.wait_ge(*x_low(ab, 1))
                for kind, n in opening(ab is not None, cb is not None):
                    if kind == "values":
                        c, half = n // 2, n % 2
                        for free in kept.get(half, []):
                            pe.wait_ge(*free)
                        kept[half] = [v_kept(ab, n + 1)]
                        if cb is None and n == 0:
                            pe.wait_ge(*w_low(0, 2))
                        for k in range(KD):
                            last = three_pass(ps_a[half][:, :], lambda i: x_split[:, i, k, P * c:P * c + P],
                                              lambda j: w_v[:, j, k, 512 * half:512 * half + 512], k == 0, k == KD - 1)
                        last.then_inc(v_done.sem, 1)
                    elif kind == "project":
                        for free in kept[n]:
                            pe.wait_ge(*free)
                        kept[n] = [p_sq(ab, n + 1), p_low(ab, n + 1)]
                        project_job(n, ab, cb, ps_a[n])
                    else:
                        score_job(n, cb)
                return kept

            def shared(ab, cb):
                kept = open_block(ab, cb)
                if cb is None:
                    cross_keys_values()
                ring = ring_banks(ab)
                a_jobs = 0
                a_free = [[] for _ in ring]
                turn_free = []
                if ab is not None:
                    a_free = [kept[0], kept[1]]
                for s in range(LAST):
                    for kind, n in steps(s, ab is not None, cb is not None):
                        if kind in ("project", "probs"):
                            bank = ring[a_jobs % len(ring)]
                            for free in a_free[a_jobs % len(ring)]:
                                pe.wait_ge(*free)
                        if kind in ("turn keys", "turn output", "turn cross"):
                            for free in turn_free:
                                pe.wait_ge(*free)
                        if kind == "project":
                            project_job(n, ab, cb, bank)
                            a_free[a_jobs % len(ring)] = [p_sq(ab, n + 1), p_low(ab, n + 1)]
                        elif kind == "turn keys":
                            if n == 0 and cb is None:
                                pe.wait_ge(consts.sem, 11)
                            pe.wait_ge(*kf_exp(ab, n + 1))
                            for c in range(NT):
                                last = pe.transpose(ps_turn[:, P * c:P * c + P], kf[:, n % 2, P * c:P * c + P], ident[:, :])
                            last.then_inc(turned_k.sem, 1)
                            turn_free = [kt_kept(ab, n + 1)]
                        elif kind in ("q features", "k features"):
                            w, to = int(kind == "k features"), ps_f
                            source = qk[:, w, n // 2 % 2, n % 2, :, :]
                            job = 2 * (n // 2) + w
                            if n == 0 and w == 0 and cb is None:
                                pe.wait_ge(*w_low(0, FEAT_PIECE + 1))
                                pe.wait_ge(*v_ones(0, 5))
                            pe.wait_ge(*low_moved[job % 4](ab, 2 * (job // 4 + 1)))
                            if w == 1:
                                pe.wait_ge(*qf_exp(ab, n + 1))
                            elif n:
                                pe.wait_ge(*kf_exp(ab, n))
                            pe.matmul(to[:, :], w_feat_high[:, :], source[:, 0, :], start=True, stop=False)
                            pe.matmul(to[:, :], w_feat_low[:, n % 2, :], source[:, 0, :], start=False, stop=False)
                            pe.matmul(to[:, :], neg_half[:, :], source[:, 1, :], start=False, stop=True
                                      ).then_inc((qf_done, kf_done)[w].sem, 1)
                        elif kind == "attend":
                            pe.wait_ge(*qf_exp(ab, n + 1))
                            if n:
                                pe.wait_ge(*att_kept(ab, n))
                            for c in range(NT):
                                t = slice(P * c, P * c + P)
                                last = pe.matmul(ps_att[:, t], kf[:, n % 2, t], qf[:, n % 4, t], start=True, stop=True)
                            last.then_inc(att_done.sem, 1)
                        elif kind == "state":
                            pe.wait_ge(*kt_kept(ab, n + 1))
                            if n == 0:
                                pe.wait_ge(*v_kept(ab, 2 * NT))
                                if cb is None:
                                    pe.wait_ge(*v_copied(0, 2 * B + 2))
                            else:
                                pe.wait_ge(*run_ready(ab, n))
                            for c in range(NT):
                                last = pe.matmul(ps_st[:, V1 * c:V1 * c + V1], kt[:, n % 2, c, :], v1[:, c, n, :],
                                                 start=True, stop=True)
                            last.then_inc(st_done.sem, 1)
                        elif kind == "scores":
                            score_job(n, cb)
                        elif kind == "output":
                            output_job(n, ab)
                        elif kind == "turn output":
                            turn_output_job(n, ab)
                            turn_free = [yt_high(ab, n + 1), yt_low(ab, n + 1)]
                        elif kind == "turn maxima":
                            pe.wait_ge(*sc_max(cb, NT * NG))
                            for c in range(NT):
                                last = pe.transpose(ps_xo[0:XHALVES, P * c:P * c + P], xmax[:, c, :], ident[:, :])
                            last.then_inc(mx_turned.sem, 1)
                        elif kind == "probs":
                            if n == 0:
                                pe.wait_ge(*mx_spread(cb, 1))
                            g, chunk = n // GC, n % GC
                            pe.matmul(bank[:, :], xk[:, g, P * chunk:P * chunk + P], xq[:, g, :], start=True,
                                      stop=True).then_inc(pr_done.sem, 1)
                            a_free[a_jobs % len(ring)] = [pr_exp(cb, n + 1)]
                        elif kind == "weigh":
                            g, half = n // 2, n % 2
                            banks = 1 if ab is not None else 2
                            if half == 0:
                                pe.wait_ge(*pr_low[0](cb, (GC * (g + 1) + 1) // 2))
                                pe.wait_ge(*pr_low[1](cb, GC * (g + 1) // 2))
                                if g >= banks:
                                    pe.wait_ge(*xo_kept(cb, g - banks + 1))
                            for c in (2 * half, 2 * half + 1):
                                for chunk in range(GC):
                                    last = three_pass(
                                        weigh_bank(ab, g)[:, GV * c:GV * c + GV],
                                        lambda i: prob[:, (GC * g + chunk) % RING, i, P * c:P * c + P],
                                        lambda j: xv[:, g, chunk, j, :], chunk == 0, chunk == GC - 1)
                            last.then_inc(weighed.sem, 1)
                        elif kind == "turn cross":
                            pe.wait_ge(*ln[1][3](cb, 2 * n + 2))
                            for k in range(KD):
                                for c in range(2):
                                    last = pe.transpose(ps_turn[:, P * (2 * k + c):P * (2 * k + c) + P],
                                                        resid[:, 2 * n + c, P * k:P * k + P], ident[:, :])
                            last.then_inc(x2_turned.sem, 1)
                            turn_free = [x2_high(cb, n + 1), x2_low(cb, n + 1)]
                        if kind in ("project", "probs"):
                            a_jobs += 1

            def ffn(fb, ab):
                pe.wait_ge(*x2_high(fb, 2))
                pe.wait_ge(*x2_low(fb, 2))
                for c in range(NT):
                    for k in range(KD):
                        last = three_pass(ps_turn[:, NE * c:NE * c + NE], lambda i: turned[:, i, k, P * c:P * c + P],
                                          lambda j: w_gate[:, j, k, :], k == 0, k == KD - 1)
                last.then_inc(gl_done.sem, 1)
                for e in range(EXPERTS + 2):
                    if e < EXPERTS:
                        pe.wait_ge(*gw_loaded[e % 2](fb, e // 2 + 1))
                        for half, (banks, free, done) in enumerate((((ps_a[0], ps_f), silu, g_done),
                                                                    ((ps_a[1], ps_o), hid_ready, u_done))):
                            if e >= 2:
                                pe.wait_ge(*free(fb, e - 1))
                            for k in range(KD):
                                cols = slice(D * half + P * k, D * half + P * k + P)
                                last = three_pass(banks[e % 2][:, :], lambda i: gu_w[:, e % 2, i, cols],
                                                  lambda j: turned[:, j, k, :], k == 0, k == KD - 1)
                            last.then_inc(done.sem, 1)
                        if ab is not None:
                            for kind, n in late_jobs(e) + tail_jobs(e):
                                tail_job(kind, n, ab, fb)
                    if e >= 2:
                        d = e - 2
                        pe.wait_ge(*dw_loaded[d % 4](fb, d // 4 + 1))
                        pe.wait_ge(*h_high(fb, d + 1))
                        pe.wait_ge(*h_low(fb, d + 1))
                        for half in range(2):
                            u = 2 * d + half
                            bank = down_banks[u % 3]
                            if u >= 3:
                                pe.wait_ge(*summed(fb, u - 2))
                            elif u == 2 and ab is None:
                                pe.wait_ge(*gl_exp(fb, 1))
                            elif ab is not None:
                                pe.wait_ge(*(att_kept(ab, H), o_kept(ab, H), yt_low(ab, PAIRS))[u])
                            for t in range(2):
                                c = 2 * half + t
                                last = three_pass(bank[:, D * t:D * t + D], lambda i: hT[:, d % 3, i, P * c:P * c + P],
                                                  lambda j: down_w[:, d % 4, j, :])
                            last.then_inc(down_done.sem, 1)

            def tail_job(kind, n, ab, fb):
                alone = fb is None
                if kind == "norm" or kind == "split":
                    return
                if kind == "output":
                    output_job(n, ab)
                    return
                if kind == "turn output":
                    pe.wait_ge(*(yt_low(ab, n) if alone else gl_exp(fb, 1)))
                    turn_output_job(n, ab)
                    return
                bank = tail_bank(kind, n, alone)
                if kind == "project out":
                    if n == 0:
                        pe.wait_ge(*yt_high(ab, PAIRS))
                        pe.wait_ge(*yt_low(ab, PAIRS))
                        if alone:
                            pe.wait_ge(*w_low(0, len(pieces) - 1))
                        else:
                            pe.wait_ge(*xo_kept(fb, NG))
                    elif not alone:
                        pe.wait_ge(*x1_added(ab, n))
                    for p in range(PAIRS):
                        last = three_pass(bank[:, 0:D], lambda i: yT[:, i, p, P * n:P * n + P],
                                          lambda j: w_o[:, j, p, :], p == 0, p == PAIRS - 1)
                    last.then_inc(wo_done.sem, 1)
                elif kind == "turn stream":
                    pe.wait_ge(*ln[0][3](ab, 2 * n + 2))
                    if n and not alone:
                        pe.wait_ge(*x1_low(ab, n))
                    for k in range(KD):
                        for c in range(2):
                            last = pe.transpose(bank[:, P * (2 * k + c):P * (2 * k + c) + P],
                                                nxt[:, 2 * n + c, P * k:P * k + P], ident[:, :])
                    last.then_inc(x1_turned.sem, 1)
                elif kind == "queries":
                    if n == 0:
                        pe.wait_ge(*x1_high(ab, 2))
                        pe.wait_ge(*x1_low(ab, 2))
                    elif not alone:
                        pe.wait_ge(*xq_low(ab, n))
                    for k in range(KD):
                        last = three_pass(bank[:, :], lambda i: w_xq[:, i, k, P * n:P * n + P],
                                          lambda j: turned_next[:, j, k, :], k == 0, k == KD - 1)
                    last.then_inc(xq_done.sem, 1)

            shared(0, None)
            for kind, n in tail_jobs(None):
                tail_job(kind, n, 0, None)
            pe.wait_ge(*xq_high(0, KD))
            pe.wait_ge(*xq_low(0, KD))
            with pe.Fori(0, NBLK - 1) as i:
                shared(i + 1, i)
                ffn(i, i + 1)
            shared(None, NBLK - 1)
            ffn(NBLK - 1, None)


def kernel(x, ctx_1024, L0_attn_Wq, L0_attn_Wk, L0_attn_Wv, L0_attn_Wo, L0_attn_W_feat, L0_xattn_Wq, L0_xattn_Wk,
           L0_xattn_Wv, L0_xattn_lambda_q1, L0_xattn_lambda_q2, L0_xattn_lambda_k1, L0_xattn_lambda_k2,
           L0_ffn_gate_w, L0_ffn_e_bias, L0_ffn_gate_proj, L0_ffn_up_proj, L0_ffn_down_proj,
           L0_ffn_shared_gate_w, L0_ffn_shared_up_w, L0_ffn_shared_down_w):
    import concourse.bacc as bacc
    from concourse.bass_utils import run_bass_kernel_spmd

    def by_rows(w):
        w = np.swapaxes(np.asarray(w), -1, -2)
        w = w.reshape(*w.shape[:-2], KD, P, w.shape[-1])
        return np.swapaxes(w, -3, -2).reshape(*w.shape[:-3], P, -1)

    def with_shared(shared, experts):
        return np.concatenate([np.asarray(shared)[None], np.asarray(experts)], 0)

    gate = by_rows(with_shared(L0_ffn_shared_gate_w, L0_ffn_gate_proj))
    up = by_rows(with_shared(L0_ffn_shared_up_w, L0_ffn_up_proj))
    down = np.swapaxes(with_shared(L0_ffn_shared_down_w, L0_ffn_down_proj), 1, 2)
    tokens = np.asarray(x).reshape(B * S, D)
    arrays = {
        "x": tokens.reshape(NBLK, NT, P, D).transpose(2, 0, 1, 3),
        "xT": tokens.T.reshape(KD, P, B * S).transpose(1, 0, 2),
        "ctxT": np.asarray(ctx_1024).reshape(B * CTX, D).T,
        "wq": L0_attn_Wq, "wk": L0_attn_Wk, "wv": L0_attn_Wv, "wo": L0_attn_Wo, "wfeat": L0_attn_W_feat,
        "xwqT": np.asarray(L0_xattn_Wq).T, "xwkT": np.asarray(L0_xattn_Wk).T, "xwvT": np.asarray(L0_xattn_Wv).T,
        "lam_q1": L0_xattn_lambda_q1, "lam_q2": L0_xattn_lambda_q2,
        "lam_k1": L0_xattn_lambda_k1, "lam_k2": L0_xattn_lambda_k2,
        "gate_wT": np.asarray(L0_ffn_gate_w).T, "e_bias": L0_ffn_e_bias,
        "ffn_w": np.concatenate([gate, up, down], -1),
    }
    arrays = {name: np.ascontiguousarray(a) for name, a in arrays.items()}
    nc = bacc.Bacc("TRN2", target_bir_lowering=False, num_devices=1)
    args = {name: nc.dram_tensor(name, a.shape, mybir.dt.from_np(a.dtype), kind="ExternalInput").ap()
            for name, a in arrays.items()}
    args["out"] = nc.dram_tensor("out", (P, NBLK, NT, D), F32, kind="ExternalOutput").ap()
    decoder_layer(nc, **args)
    got = run_bass_kernel_spmd(nc, [arrays], core_ids=[0]).results[0]["out"]
    return np.asarray(got).transpose(1, 2, 0, 3).reshape(B, S, D)
```
